# Optimizing a Trainium2 kernel written in Bass

```python
import numpy as np
import jax
import jax.numpy as jnp

def _softmax(x, axis=-1):
    return jax.nn.softmax(x, axis=axis)

def _gelu(x):
    return jax.nn.gelu(x, approximate=True)

def _silu(x):
    return jax.nn.silu(x)

def _sigmoid(x):
    return jax.nn.sigmoid(x)

def _layernorm(x, axis=-1, eps=1e-05):
    m = jnp.mean(x, axis=axis, keepdims=True)
    v = jnp.var(x, axis=axis, keepdims=True)
    return (x - m) / jnp.sqrt(v + eps)

def _scatter_add(tgt, idx, src, axis=0):
    return tgt.at[idx].add(src)

def _segment_sum(src, seg, n):
    return jax.ops.segment_sum(src, seg, n)
kernel_name = 'mk_flamingo_gated_d4_seqx_r4_6383fc'

def setup_inputs(seed: int=0):
    np.random.seed(seed)
    _w = jnp.asarray

    def _rec_inputs():
        import jax
        import jax.numpy as jnp
        _rk = jax.random.key(seed)
        x = -0.000929 + 1 * jax.random.normal(jax.random.fold_in(_rk, 1), (2, 1024, 256), jnp.float32)
        _lenS = 1024 - jax.random.randint(jax.random.fold_in(_rk, 7), (2,), 0, max(1, 1024 // 4) + 1, jnp.int32)
        _lenS2 = 154 - jax.random.randint(jax.random.fold_in(_rk, 8), (2,), 0, max(1, 154 // 4) + 1, jnp.int32)
        _ctx_1024P = jax.random.normal(jax.random.fold_in(_rk, 11), (2, 16, 256), jnp.float32)
        _ctx_1024c = jax.random.dirichlet(jax.random.fold_in(_rk, 511), 0.3 * jnp.ones((16,), jnp.float32), (2, 154))
        _ctx_1024t = jnp.einsum('bsk,bkd->bsd', _ctx_1024c, _ctx_1024P)
        _ctx_1024t = _ctx_1024t * jax.lax.rsqrt(jnp.mean(jnp.square(_ctx_1024t)) + 1e-12) * 0.953939
        ctx_1024 = -1.52775e-05 + 0.999936 * (_ctx_1024t + 0.3 * jax.random.normal(jax.random.fold_in(_rk, 611), (2, 154, 256), jnp.float32))
        _validS = jnp.arange(1024)[None, :] < _lenS[:, None]
        _validS2 = jnp.arange(154)[None, :] < _lenS2[:, None]
        _causal = jnp.tril(jnp.ones((1024, 1024), dtype=bool))
        mask_BxS2_bf1 = jnp.ones((2, 154), dtype=bool)
        mask_Bx1xSxS2_bk1 = jnp.broadcast_to(_validS2[:, None, None, :], (2, 1, 1024, 154))
        _g = jax.random.normal(jax.random.fold_in(_rk, 9001), (2, 4), jnp.float32)
        _g = jnp.sign(_g) * jnp.maximum(jnp.abs(_g), 1.0) + (_g == 0) * 1.0
        g_xattn = _g[0]
        g_ffn = _g[1]
        return (x, ctx_1024, mask_BxS2_bf1, mask_Bx1xSxS2_bk1, g_xattn, g_ffn)
    x, ctx_1024, mask_BxS2_bf1, mask_Bx1xSxS2_bk1, g_xattn, g_ffn = _rec_inputs()

    def _L0_xattn_setup():
        import jax, jax.numpy as jnp
        import numpy as np
        B, N, L, D, H = (8, 128, 1024, 256, 16)
        key = jax.random.key(seed)
        ks = jax.random.split(key, 7)
        s = 1.0 / np.sqrt(D)
        return {'q': jax.random.normal(ks[0], (B, N, D), dtype=jnp.float32), 'k': jax.random.normal(ks[1], (B, L, D), dtype=jnp.float32), 'v': jax.random.normal(ks[2], (B, L, D), dtype=jnp.float32), 'Wq': jax.random.normal(ks[3], (D, D), dtype=jnp.float32) * s, 'Wk': jax.random.normal(ks[4], (D, D), dtype=jnp.float32) * s, 'Wv': jax.random.normal(ks[5], (D, D), dtype=jnp.float32) * s, 'Wo': jax.random.normal(ks[6], (D, D), dtype=jnp.float32) * s}
    _L0_xattn_all = _L0_xattn_setup()
    _L0_xattn_in = {k: v for k, v in _L0_xattn_all.items() if k in ('Wq', 'Wk', 'Wv', 'Wo')}
    del _L0_xattn_all

    def _L0_ffn_setup():
        import jax, jax.numpy as jnp
        import numpy as np
        HID, FFN, E, K = (256, 1024, 8, 2)
        CAP_FACTOR = 1.25
        key = jax.random.key(seed)
        k1, k2, k3, k4 = jax.random.split(key, 4)
        B, T = (4, 512)
        x = jax.random.normal(k1, (B, T, HID), dtype=jnp.float32)
        router_w = jax.random.normal(k2, (E, HID), dtype=jnp.float32) * 0.02
        w1 = jax.random.normal(k3, (E, HID, FFN), dtype=jnp.float32) * 0.02
        w2 = jax.random.normal(k4, (E, FFN, HID), dtype=jnp.float32) * 0.02
        return {'x': x, 'router_w': router_w, 'w1': w1, 'w2': w2}
    _L0_ffn_all = _L0_ffn_setup()
    _L0_ffn_in = {k: v for k, v in _L0_ffn_all.items() if k in ('router_w', 'w1', 'w2')}
    del _L0_ffn_all

    def _L1_xattn_setup():
        import jax, jax.numpy as jnp
        import numpy as np
        GAMMA = 10.0
        BASE = 10000.0
        SCALE = 64 ** (-0.5)
        NUM_HEADS = 16

        def _larope(t, seq_len):
            B, H, L, D = t.shape
            inv_freq = 1.0 / BASE ** (jnp.arange(0, D, 2, dtype=jnp.float32) / D)
            pos = GAMMA * (jnp.arange(L, dtype=jnp.float32) / float(seq_len))
            ang = pos[:, None] * inv_freq
            cos = jnp.cos(ang)
            sin = jnp.sin(ang)
            te, to = (t[..., 0::2], t[..., 1::2])
            re = te * cos - to * sin
            ro = te * sin + to * cos
            return jnp.stack([re, ro], axis=-1).reshape(t.shape)
        key = jax.random.key(seed)
        ks = jax.random.split(key, 8)
        B, Lq, Lk, D = (8, 512, 128, 256)
        s = D ** (-0.5)
        return {'x': jax.random.normal(ks[0], (B, Lq, D), jnp.float32), 'context': jax.random.normal(ks[1], (B, Lk, D), jnp.float32), 'context_mask': jnp.ones((B, Lk), dtype=bool), 'Wq': jax.random.normal(ks[2], (D, D), jnp.float32) * s, 'bq': jnp.zeros((D,), jnp.float32), 'Wkv': jax.random.normal(ks[3], (D, 2 * D), jnp.float32) * s, 'bkv': jnp.zeros((2 * D,), jnp.float32), 'Wo': jax.random.normal(ks[4], (D, D), jnp.float32) * s, 'bo': jnp.zeros((D,), jnp.float32)}
    _L1_xattn_all = _L1_xattn_setup()
    _L1_xattn_in = {k: v for k, v in _L1_xattn_all.items() if k in ('Wq', 'bq', 'Wkv', 'bkv', 'Wo', 'bo')}
    del _L1_xattn_all

    def _L1_ffn_setup():
        import jax, jax.numpy as jnp
        import numpy as np
        import math
        B, S, D = (2, 512, 256)
        H = 16
        HD = D // H
        FFN = 512
        E = 8
        TOP_K = 2
        CAP_FACTOR = 1.25
        EPS = 1e-06
        BASE = 10000.0
        CAP = max(math.ceil(B * S * TOP_K * CAP_FACTOR / E), 1)

        def _rmsnorm(x, w):
            rms = jax.lax.rsqrt(jnp.mean(x * x, axis=-1, keepdims=True) + EPS)
            return w * x * rms

        def _rope(x, cos, sin):
            xr = x[..., 0::2]
            xi = x[..., 1::2]
            c = cos[None, None]
            s_ = sin[None, None]
            out_r = xr * c - xi * s_
            out_i = xr * s_ + xi * c
            return jnp.stack([out_r, out_i], axis=-1).reshape(x.shape)

        def _mha(x, w_qkv, w_o):
            b, s, d = x.shape
            qkv = x @ w_qkv
            q, k, v = jnp.split(qkv, 3, axis=-1)
            to_heads = lambda z: z.reshape(b, s, H, HD).transpose(0, 2, 1, 3)
            q, k, v = (to_heads(q), to_heads(k), to_heads(v))
            theta = BASE ** (-2.0 * (jnp.arange(HD // 2, dtype=jnp.float32) / HD))
            freqs = jnp.arange(s, dtype=jnp.float32)[:, None] * theta[None, :]
            cos, sin = (jnp.cos(freqs), jnp.sin(freqs))
            q = _rope(q, cos, sin)
            k = _rope(k, cos, sin)
            scores = jnp.einsum('bhqd,bhkd->bhqk', q, k) / jnp.sqrt(jnp.float32(HD))
            causal = jnp.tril(jnp.ones((s, s), dtype=bool))
            scores = jnp.where(causal, scores, -jnp.inf)
            attn = jax.nn.softmax(scores, axis=-1)
            y = jnp.einsum('bhqk,bhkd->bhqd', attn, v)
            y = y.transpose(0, 2, 1, 3).reshape(b, s, d)
            return y @ w_o

        def _moe(x, w_router, w1, w2):
            b, s, d = x.shape
            t = b * s
            xf = x.reshape(t, d)
            logits = xf.astype(jnp.float32) @ w_router.astype(jnp.float32)
            probs = jax.nn.softmax(logits, axis=-1)
            g, eidx = jax.lax.top_k(probs, TOP_K)
            fg = g.reshape(t * TOP_K)
            fe = eidx.reshape(t * TOP_K)
            tok_of = jnp.arange(t * TOP_K) // TOP_K
            masked = jnp.where(fe[None, :] == jnp.arange(E)[:, None], fg[None, :], -jnp.inf)
            vals, idx = jax.lax.top_k(masked, CAP)
            valid = jnp.isfinite(vals)
            gates = jnp.where(valid, vals, 0.0)
            tok = tok_of[idx]
            xe = xf[tok]
            h = jax.nn.relu(jnp.einsum('ecd,edf->ecf', xe, w1))
            ye = jnp.einsum('ecf,efd->ecd', h, w2) * gates[..., None]
            y = jnp.zeros_like(xf).at[tok.reshape(-1)].add(ye.reshape(-1, d))
            return y.reshape(b, s, d)
        key = jax.random.key(seed)
        ks = jax.random.split(key, 6)
        sd = 0.02
        return {'x': jax.random.normal(ks[0], (B, S, D), jnp.float32), 'g1': jnp.ones((D,), jnp.float32), 'w_qkv': jax.random.normal(ks[1], (D, 3 * D), jnp.float32) * sd, 'w_o': jax.random.normal(ks[2], (D, D), jnp.float32) * sd, 'g2': jnp.ones((D,), jnp.float32), 'w_router': jax.random.normal(ks[3], (D, E), jnp.float32) * sd, 'w1': jax.random.normal(ks[4], (E, D, FFN), jnp.float32) * sd, 'w2': jax.random.normal(ks[5], (E, FFN, D), jnp.float32) * sd}
    _L1_ffn_all = _L1_ffn_setup()
    _L1_ffn_in = {k: v for k, v in _L1_ffn_all.items() if k in ('g1', 'w_qkv', 'w_o', 'g2', 'w_router', 'w1', 'w2')}
    del _L1_ffn_all

    def _L2_xattn_setup():
        import jax, jax.numpy as jnp
        import numpy as np
        from jax import lax
        BIG = jnp.float32(1e+30)

        def _pairwise_euclidean(a, b):
            aa = jnp.sum(a * a, axis=-1)[:, None]
            bb = jnp.sum(b * b, axis=-1)[None, :]
            ab = a @ b.T
            return jnp.sqrt(jnp.maximum(aa + bb - 2.0 * ab, 0.0))

        def _dtw_cost(D):
            row0 = jnp.cumsum(D[0])

            def row_step(prev_row, d_row):
                first = d_row[0] + prev_row[0]

                def col_step(left, inp):
                    d_ij, up, diag = inp
                    r = d_ij + jnp.minimum(jnp.minimum(up, left), diag)
                    return (r, r)
                _, rest = lax.scan(col_step, first, (d_row[1:], prev_row[1:], prev_row[:-1]))
                row = jnp.concatenate([first[None], rest])
                return (row, row)
            _, rows = lax.scan(row_step, row0, D[1:])
            return jnp.concatenate([row0[None], rows], axis=0)

        def _backtrack(R, T1, T2):
            L = T1 + T2 - 1

            def step(carry, _):
                i, j, done = carry
                valid = jnp.logical_not(done)
                cd = jnp.where((i > 0) & (j > 0), R[jnp.maximum(i - 1, 0), jnp.maximum(j - 1, 0)], BIG)
                cu = jnp.where(i > 0, R[jnp.maximum(i - 1, 0), j], BIG)
                cl = jnp.where(j > 0, R[i, jnp.maximum(j - 1, 0)], BIG)
                choice = jnp.argmin(jnp.stack([cd, cu, cl]))
                ni = jnp.where(choice <= 1, i - 1, i)
                nj = jnp.where((choice == 0) | (choice == 2), j - 1, j)
                at_origin = (i == 0) & (j == 0)
                ni = jnp.where(at_origin, 0, ni)
                nj = jnp.where(at_origin, 0, nj)
                return ((ni, nj, done | at_origin), (i, j, valid))
            init = (jnp.int32(T1 - 1), jnp.int32(T2 - 1), jnp.bool_(False))
            _, (i_idx, j_idx, valid) = lax.scan(step, init, None, length=L)
            return (i_idx, j_idx, valid)

        def _align_one(small, large):
            T_small, d = small.shape
            T_large = large.shape[0]
            D = _pairwise_euclidean(small, large)
            R = _dtw_cost(D)
            i_idx, j_idx, valid = _backtrack(R, T_small, T_large)
            contrib = small[i_idx] * valid[:, None].astype(small.dtype)
            expanded = jnp.zeros((T_large, d), dtype=small.dtype).at[j_idx].add(contrib)
            return expanded
        key = jax.random.key(seed)
        k1, k2 = jax.random.split(key)
        teacher = jax.random.normal(k1, (16, 100, 256), dtype=jnp.float32)
        student = jax.random.normal(k2, (16, 150, 256), dtype=jnp.float32)
        return {'teacher_features': teacher, 'student_features': student}
    _L2_xattn_all = _L2_xattn_setup()
    _L2_xattn_in = {k: v for k, v in _L2_xattn_all.items() if k in ()}
    del _L2_xattn_all

    def _L2_ffn_setup():
        import jax, jax.numpy as jnp
        import numpy as np
        B, S, D, H, E = (2, 512, 256, 1024, 8)
        key = jax.random.key(seed)
        k0, k1, k2, k3 = jax.random.split(key, 4)
        x = jax.random.normal(k0, (B, S, D), dtype=jnp.float32)
        router_w = jax.random.normal(k1, (E, D), dtype=jnp.float32) * 0.02
        w1 = jax.random.normal(k2, (E, D, H), dtype=jnp.float32) * 0.02
        w2 = jax.random.normal(k3, (E, H, D), dtype=jnp.float32) * 0.02
        return {'x': x, 'router_w': router_w, 'w1': w1, 'w2': w2}
    _L2_ffn_all = _L2_ffn_setup()
    _L2_ffn_in = {k: v for k, v in _L2_ffn_all.items() if k in ('router_w', 'w1', 'w2')}
    del _L2_ffn_all

    def _L3_xattn_setup():
        import jax, jax.numpy as jnp
        import numpy as np
        B, S, D, H = (4, 512, 256, 16)
        HD = D // H
        key = jax.random.key(seed)
        ks = jax.random.split(key, 12)
        scale = 1.0 / np.sqrt(D)
        inp = {'queries': jax.random.normal(ks[0], (B, S, D), jnp.float32), 'keys': jax.random.normal(ks[1], (B, S, D), jnp.float32), 'values': jax.random.normal(ks[2], (B, S, D), jnp.float32), 'mask': jax.random.randint(ks[3], (B, 1, S, S), 0, 2).astype(bool), 'Wq': jax.random.normal(ks[4], (D, D), jnp.float32) * scale, 'bq': jnp.zeros((D,), jnp.float32), 'Wk': jax.random.normal(ks[5], (D, D), jnp.float32) * scale, 'bk': jnp.zeros((D,), jnp.float32), 'Wv': jax.random.normal(ks[6], (D, D), jnp.float32) * scale, 'bv': jnp.zeros((D,), jnp.float32), 'Wo': jax.random.normal(ks[7], (D, D), jnp.float32) * scale, 'bo': jnp.zeros((D,), jnp.float32)}
        return inp
    _L3_xattn_all = _L3_xattn_setup()
    _L3_xattn_in = {k: v for k, v in _L3_xattn_all.items() if k in ('Wq', 'bq', 'Wk', 'bk', 'Wv', 'bv', 'Wo', 'bo')}
    del _L3_xattn_all

    def _L3_ffn_setup():
        import jax, jax.numpy as jnp
        import numpy as np
        D_MODEL = 256
        D_FF = 1024
        N_EXPERTS = 4
        key = jax.random.key(seed)
        ks = jax.random.split(key, 8)
        s_in = 1.0 / np.sqrt(D_MODEL)
        s_ff = 1.0 / np.sqrt(D_FF)
        x = jax.random.normal(ks[0], (4, 512, D_MODEL), dtype=jnp.float32)
        W1 = jax.random.uniform(ks[1], (N_EXPERTS, D_MODEL, D_FF), jnp.float32, -s_in, s_in)
        b1 = jax.random.uniform(ks[2], (N_EXPERTS, D_FF), jnp.float32, -s_in, s_in)
        W2 = jax.random.uniform(ks[3], (N_EXPERTS, D_FF, D_MODEL), jnp.float32, -s_ff, s_ff)
        b2 = jax.random.uniform(ks[4], (N_EXPERTS, D_MODEL), jnp.float32, -s_ff, s_ff)
        Wg = jax.random.uniform(ks[5], (D_MODEL, N_EXPERTS), jnp.float32, -s_in, s_in)
        bg = jax.random.uniform(ks[6], (N_EXPERTS,), jnp.float32, -s_in, s_in)
        return {'x': x, 'W1': W1, 'b1': b1, 'W2': W2, 'b2': b2, 'Wg': Wg, 'bg': bg}
    _L3_ffn_all = _L3_ffn_setup()
    _L3_ffn_in = {k: v for k, v in _L3_ffn_all.items() if k in ('W1', 'b1', 'W2', 'b2', 'Wg', 'bg')}
    del _L3_ffn_all
    return {'x': x, 'ctx_1024': ctx_1024, 'mask_BxS2_bf1': mask_BxS2_bf1, 'mask_Bx1xSxS2_bk1': mask_Bx1xSxS2_bk1, 'g_xattn': g_xattn, 'g_ffn': g_ffn, 'L0_xattn_Wq': _L0_xattn_in['Wq'], 'L0_xattn_Wk': _L0_xattn_in['Wk'], 'L0_xattn_Wv': _L0_xattn_in['Wv'], 'L0_xattn_Wo': _L0_xattn_in['Wo'], 'L0_ffn_router_w': _L0_ffn_in['router_w'], 'L0_ffn_w1': _L0_ffn_in['w1'], 'L0_ffn_w2': _L0_ffn_in['w2'], 'L1_xattn_Wq': _L1_xattn_in['Wq'], 'L1_xattn_bq': _L1_xattn_in['bq'], 'L1_xattn_Wkv': _L1_xattn_in['Wkv'], 'L1_xattn_bkv': _L1_xattn_in['bkv'], 'L1_xattn_Wo': _L1_xattn_in['Wo'], 'L1_xattn_bo': _L1_xattn_in['bo'], 'L1_ffn_g1': _L1_ffn_in['g1'], 'L1_ffn_w_qkv': _L1_ffn_in['w_qkv'], 'L1_ffn_w_o': _L1_ffn_in['w_o'], 'L1_ffn_g2': _L1_ffn_in['g2'], 'L1_ffn_w_router': _L1_ffn_in['w_router'], 'L1_ffn_w1': _L1_ffn_in['w1'], 'L1_ffn_w2': _L1_ffn_in['w2'], 'L2_ffn_router_w': _L2_ffn_in['router_w'], 'L2_ffn_w1': _L2_ffn_in['w1'], 'L2_ffn_w2': _L2_ffn_in['w2'], 'L3_xattn_Wq': _L3_xattn_in['Wq'], 'L3_xattn_bq': _L3_xattn_in['bq'], 'L3_xattn_Wk': _L3_xattn_in['Wk'], 'L3_xattn_bk': _L3_xattn_in['bk'], 'L3_xattn_Wv': _L3_xattn_in['Wv'], 'L3_xattn_bv': _L3_xattn_in['bv'], 'L3_xattn_Wo': _L3_xattn_in['Wo'], 'L3_xattn_bo': _L3_xattn_in['bo'], 'L3_ffn_W1': _L3_ffn_in['W1'], 'L3_ffn_b1': _L3_ffn_in['b1'], 'L3_ffn_W2': _L3_ffn_in['W2'], 'L3_ffn_b2': _L3_ffn_in['b2'], 'L3_ffn_Wg': _L3_ffn_in['Wg'], 'L3_ffn_bg': _L3_ffn_in['bg']}

def reference(x, ctx_1024, mask_BxS2_bf1, mask_Bx1xSxS2_bk1, g_xattn, g_ffn, L0_xattn_Wq, L0_xattn_Wk, L0_xattn_Wv, L0_xattn_Wo, L0_ffn_router_w, L0_ffn_w1, L0_ffn_w2, L1_xattn_Wq, L1_xattn_bq, L1_xattn_Wkv, L1_xattn_bkv, L1_xattn_Wo, L1_xattn_bo, L1_ffn_g1, L1_ffn_w_qkv, L1_ffn_w_o, L1_ffn_g2, L1_ffn_w_router, L1_ffn_w1, L1_ffn_w2, L2_ffn_router_w, L2_ffn_w1, L2_ffn_w2, L3_xattn_Wq, L3_xattn_bq, L3_xattn_Wk, L3_xattn_bk, L3_xattn_Wv, L3_xattn_bv, L3_xattn_Wo, L3_xattn_bo, L3_ffn_W1, L3_ffn_b1, L3_ffn_W2, L3_ffn_b2, L3_ffn_Wg, L3_ffn_bg):
    import jax
    import jax.numpy as jnp

    def _L0_xattn_ref(q, k, v, Wq, Wk, Wv, Wo):
        import jax, jax.numpy as jnp
        import numpy as np
        B, N, L, D, H = (8, 128, 1024, 256, 16)
        Bq, Nq, Dm = q.shape
        Lk = k.shape[1]
        Hh = H
        Dh = Dm // Hh
        scale = Dm ** (-0.5)
        qh = (q @ Wq.T).reshape(Bq, Nq, Hh, Dh).transpose(0, 2, 1, 3)
        kh = (k @ Wk.T).reshape(Bq, Lk, Hh, Dh).transpose(0, 2, 1, 3)
        vh = (v @ Wv.T).reshape(Bq, Lk, Hh, Dh).transpose(0, 2, 1, 3)
        attn = jnp.einsum('bhnc,bhlc->bhnl', qh * scale, kh)
        attn = jax.nn.softmax(attn, axis=2)
        attn = attn / jnp.sum(attn, axis=-1, keepdims=True)
        out = jnp.einsum('bhnl,bhlc->bhnc', attn, vh)
        out = out.transpose(0, 2, 1, 3).reshape(Bq, Nq, Dm)
        return out @ Wo.T

    def _L0_ffn_ref(x, router_w, w1, w2):
        import jax, jax.numpy as jnp
        import numpy as np
        HID, FFN, E, K = (256, 1024, 8, 2)
        CAP_FACTOR = 1.25
        B, T, H = x.shape
        N = B * T
        x_flat = x.reshape(N, H)
        C = max(1, int(CAP_FACTOR * N / E * K))
        logits = x_flat @ router_w.T
        probs = jax.nn.softmax(logits, axis=-1)
        top_v, top_i = jax.lax.top_k(probs, K)
        top_v = top_v / jnp.sum(top_v, axis=-1, keepdims=True)
        out = jnp.zeros_like(x_flat)
        for k in range(K):
            eid = top_i[:, k]
            gate = top_v[:, k]
            onehot = jax.nn.one_hot(eid, E, dtype=jnp.int32)
            pos = jnp.take_along_axis(jnp.cumsum(onehot, axis=0), eid[:, None], axis=1)[:, 0] - 1
            keep = pos < C
            slot = jnp.where(keep, eid * C + pos, E * C)
            buf = jnp.zeros((E * C + 1, H), dtype=x.dtype).at[slot].add(x_flat * keep[:, None].astype(x.dtype))
            expert_in = buf[:E * C].reshape(E, C, H)
            h = jax.nn.gelu(jnp.einsum('ech,ehf->ecf', expert_in, w1), approximate=False)
            y = jnp.einsum('ecf,efh->ech', h, w2)
            tok = y.reshape(E * C, H)[jnp.minimum(slot, E * C - 1)]
            out = out + tok * (gate * keep.astype(x.dtype))[:, None]
        return out.reshape(B, T, H)

    def _L1_xattn_ref(x, context, context_mask, Wq, bq, Wkv, bkv, Wo, bo):
        import jax, jax.numpy as jnp
        import numpy as np
        GAMMA = 10.0
        BASE = 10000.0
        SCALE = 64 ** (-0.5)
        NUM_HEADS = 16

        def _larope(t, seq_len):
            B, H, L, D = t.shape
            inv_freq = 1.0 / BASE ** (jnp.arange(0, D, 2, dtype=jnp.float32) / D)
            pos = GAMMA * (jnp.arange(L, dtype=jnp.float32) / float(seq_len))
            ang = pos[:, None] * inv_freq
            cos = jnp.cos(ang)
            sin = jnp.sin(ang)
            te, to = (t[..., 0::2], t[..., 1::2])
            re = te * cos - to * sin
            ro = te * sin + to * cos
            return jnp.stack([re, ro], axis=-1).reshape(t.shape)
        B, Lq, D = x.shape
        Lk = context.shape[1]
        H = NUM_HEADS
        hd = D // H
        q = x @ Wq + bq
        kv = context @ Wkv + bkv
        k, v = jnp.split(kv, 2, axis=-1)
        q = q.reshape(B, Lq, H, hd).transpose(0, 2, 1, 3)
        k = k.reshape(B, Lk, H, hd).transpose(0, 2, 1, 3)
        v = v.reshape(B, Lk, H, hd).transpose(0, 2, 1, 3)
        q = _larope(q, Lq)
        k = _larope(k, Lk)
        scores = jnp.einsum('bhqd,bhkd->bhqk', q, k) * SCALE
        scores = jnp.where(context_mask[:, None, None, :], scores, -jnp.inf)
        attn = jax.nn.softmax(scores, axis=-1)
        out = jnp.einsum('bhqk,bhkd->bhqd', attn, v)
        out = out.transpose(0, 2, 1, 3).reshape(B, Lq, H * hd)
        return out @ Wo + bo

    def _L1_ffn_ref(x, g1, w_qkv, w_o, g2, w_router, w1, w2):
        import jax, jax.numpy as jnp
        import numpy as np
        import math
        B, S, D = (2, 512, 256)
        H = 16
        HD = D // H
        FFN = 512
        E = 8
        TOP_K = 2
        CAP_FACTOR = 1.25
        EPS = 1e-06
        BASE = 10000.0
        CAP = max(math.ceil(B * S * TOP_K * CAP_FACTOR / E), 1)

        def _rmsnorm(x, w):
            rms = jax.lax.rsqrt(jnp.mean(x * x, axis=-1, keepdims=True) + EPS)
            return w * x * rms

        def _rope(x, cos, sin):
            xr = x[..., 0::2]
            xi = x[..., 1::2]
            c = cos[None, None]
            s_ = sin[None, None]
            out_r = xr * c - xi * s_
            out_i = xr * s_ + xi * c
            return jnp.stack([out_r, out_i], axis=-1).reshape(x.shape)

        def _mha(x, w_qkv, w_o):
            b, s, d = x.shape
            qkv = x @ w_qkv
            q, k, v = jnp.split(qkv, 3, axis=-1)
            to_heads = lambda z: z.reshape(b, s, H, HD).transpose(0, 2, 1, 3)
            q, k, v = (to_heads(q), to_heads(k), to_heads(v))
            theta = BASE ** (-2.0 * (jnp.arange(HD // 2, dtype=jnp.float32) / HD))
            freqs = jnp.arange(s, dtype=jnp.float32)[:, None] * theta[None, :]
            cos, sin = (jnp.cos(freqs), jnp.sin(freqs))
            q = _rope(q, cos, sin)
            k = _rope(k, cos, sin)
            scores = jnp.einsum('bhqd,bhkd->bhqk', q, k) / jnp.sqrt(jnp.float32(HD))
            causal = jnp.tril(jnp.ones((s, s), dtype=bool))
            scores = jnp.where(causal, scores, -jnp.inf)
            attn = jax.nn.softmax(scores, axis=-1)
            y = jnp.einsum('bhqk,bhkd->bhqd', attn, v)
            y = y.transpose(0, 2, 1, 3).reshape(b, s, d)
            return y @ w_o

        def _moe(x, w_router, w1, w2):
            b, s, d = x.shape
            t = b * s
            xf = x.reshape(t, d)
            logits = xf.astype(jnp.float32) @ w_router.astype(jnp.float32)
            probs = jax.nn.softmax(logits, axis=-1)
            g, eidx = jax.lax.top_k(probs, TOP_K)
            fg = g.reshape(t * TOP_K)
            fe = eidx.reshape(t * TOP_K)
            tok_of = jnp.arange(t * TOP_K) // TOP_K
            masked = jnp.where(fe[None, :] == jnp.arange(E)[:, None], fg[None, :], -jnp.inf)
            vals, idx = jax.lax.top_k(masked, CAP)
            valid = jnp.isfinite(vals)
            gates = jnp.where(valid, vals, 0.0)
            tok = tok_of[idx]
            xe = xf[tok]
            h = jax.nn.relu(jnp.einsum('ecd,edf->ecf', xe, w1))
            ye = jnp.einsum('ecf,efd->ecd', h, w2) * gates[..., None]
            y = jnp.zeros_like(xf).at[tok.reshape(-1)].add(ye.reshape(-1, d))
            return y.reshape(b, s, d)
        x = x + _mha(_rmsnorm(x, g1), w_qkv, w_o)
        x = x + _moe(_rmsnorm(x, g2), w_router, w1, w2)
        return x

    def _L2_xattn_ref(teacher_features, student_features):
        import jax, jax.numpy as jnp
        import numpy as np
        from jax import lax
        BIG = jnp.float32(1e+30)

        def _pairwise_euclidean(a, b):
            aa = jnp.sum(a * a, axis=-1)[:, None]
            bb = jnp.sum(b * b, axis=-1)[None, :]
            ab = a @ b.T
            return jnp.sqrt(jnp.maximum(aa + bb - 2.0 * ab, 0.0))

        def _dtw_cost(D):
            row0 = jnp.cumsum(D[0])

            def row_step(prev_row, d_row):
                first = d_row[0] + prev_row[0]

                def col_step(left, inp):
                    d_ij, up, diag = inp
                    r = d_ij + jnp.minimum(jnp.minimum(up, left), diag)
                    return (r, r)
                _, rest = lax.scan(col_step, first, (d_row[1:], prev_row[1:], prev_row[:-1]))
                row = jnp.concatenate([first[None], rest])
                return (row, row)
            _, rows = lax.scan(row_step, row0, D[1:])
            return jnp.concatenate([row0[None], rows], axis=0)

        def _backtrack(R, T1, T2):
            L = T1 + T2 - 1

            def step(carry, _):
                i, j, done = carry
                valid = jnp.logical_not(done)
                cd = jnp.where((i > 0) & (j > 0), R[jnp.maximum(i - 1, 0), jnp.maximum(j - 1, 0)], BIG)
                cu = jnp.where(i > 0, R[jnp.maximum(i - 1, 0), j], BIG)
                cl = jnp.where(j > 0, R[i, jnp.maximum(j - 1, 0)], BIG)
                choice = jnp.argmin(jnp.stack([cd, cu, cl]))
                ni = jnp.where(choice <= 1, i - 1, i)
                nj = jnp.where((choice == 0) | (choice == 2), j - 1, j)
                at_origin = (i == 0) & (j == 0)
                ni = jnp.where(at_origin, 0, ni)
                nj = jnp.where(at_origin, 0, nj)
                return ((ni, nj, done | at_origin), (i, j, valid))
            init = (jnp.int32(T1 - 1), jnp.int32(T2 - 1), jnp.bool_(False))
            _, (i_idx, j_idx, valid) = lax.scan(step, init, None, length=L)
            return (i_idx, j_idx, valid)

        def _align_one(small, large):
            T_small, d = small.shape
            T_large = large.shape[0]
            D = _pairwise_euclidean(small, large)
            R = _dtw_cost(D)
            i_idx, j_idx, valid = _backtrack(R, T_small, T_large)
            contrib = small[i_idx] * valid[:, None].astype(small.dtype)
            expanded = jnp.zeros((T_large, d), dtype=small.dtype).at[j_idx].add(contrib)
            return expanded
        return jax.vmap(_align_one)(teacher_features, student_features)

    def _L2_ffn_ref(x, router_w, w1, w2):
        import jax, jax.numpy as jnp
        import numpy as np
        B, S, D, H, E = (2, 512, 256, 1024, 8)
        b, s, d = x.shape
        e = router_w.shape[0]
        xf = x.reshape(-1, d)
        probs = jax.nn.softmax(xf @ router_w.T, axis=-1)
        topv, topi = jax.lax.top_k(probs, 2)
        topv = topv / (topv.sum(axis=-1, keepdims=True) + 1e-09)
        cw = (jax.nn.one_hot(topi, e, dtype=xf.dtype) * topv[..., None]).sum(axis=1)
        h = jax.nn.gelu(jnp.einsum('td,edh->teh', xf, w1), approximate=False)
        y = jnp.einsum('teh,ehd->ted', h, w2)
        out = jnp.einsum('te,ted->td', cw, y)
        return out.reshape(b, s, d)

    def _L3_xattn_ref(queries, keys, values, mask, Wq, bq, Wk, bk, Wv, bv, Wo, bo):
        import jax, jax.numpy as jnp
        import numpy as np
        B, S, D, H = (4, 512, 256, 16)
        HD = D // H
        b, sq, d = queries.shape

        def split_heads(x):
            return x.reshape(b, x.shape[1], H, HD).transpose(0, 2, 1, 3)
        q = split_heads(queries @ Wq + bq)
        k = split_heads(keys @ Wk + bk)
        v = split_heads(values @ Wv + bv)
        scores = jnp.einsum('bhqd,bhkd->bhqk', q, k) / jnp.sqrt(jnp.float32(HD))
        scores = jnp.where(mask, jnp.float32(-1000000000000000.0), scores)
        attn = jax.nn.softmax(scores, axis=-1)
        ctx = jnp.einsum('bhqk,bhkd->bhqd', attn, v)
        ctx = ctx.transpose(0, 2, 1, 3).reshape(b, sq, d)
        return ctx @ Wo + bo

    def _L3_ffn_ref(x, W1, b1, W2, b2, Wg, bg):
        import jax, jax.numpy as jnp
        import numpy as np
        D_MODEL = 256
        D_FF = 1024
        N_EXPERTS = 4
        gate_logits = jnp.einsum('bld,de->ble', x, Wg) + bg
        idx = jnp.argmax(jax.nn.softmax(gate_logits, axis=-1), axis=-1)
        h = jnp.einsum('bld,edf->belf', x, W1) + b1[None, :, None, :]
        h = jax.nn.gelu(h, approximate=False)
        y = jnp.einsum('belf,efd->beld', h, W2) + b2[None, :, None, :]
        onehot = jax.nn.one_hot(idx, N_EXPERTS, dtype=x.dtype)
        out = jnp.einsum('beld,ble->bld', y, onehot)
        return out
    x = x + jnp.tanh(g_xattn[0]) * _L0_xattn_ref(_layernorm(x, axis=-1), ctx_1024, ctx_1024, L0_xattn_Wq, L0_xattn_Wk, L0_xattn_Wv, L0_xattn_Wo)
    x = x + jnp.tanh(g_ffn[0]) * _L0_ffn_ref(_layernorm(x, axis=-1), L0_ffn_router_w, L0_ffn_w1, L0_ffn_w2)
    x = x + jnp.tanh(g_xattn[1]) * _L1_xattn_ref(_layernorm(x, axis=-1), ctx_1024, mask_BxS2_bf1, L1_xattn_Wq, L1_xattn_bq, L1_xattn_Wkv, L1_xattn_bkv, L1_xattn_Wo, L1_xattn_bo)
    x = x + jnp.tanh(g_ffn[1]) * _L1_ffn_ref(_layernorm(x, axis=-1), L1_ffn_g1, L1_ffn_w_qkv, L1_ffn_w_o, L1_ffn_g2, L1_ffn_w_router, L1_ffn_w1, L1_ffn_w2)
    x = x + jnp.tanh(g_xattn[2]) * _L2_xattn_ref(ctx_1024, _layernorm(x, axis=-1))
    x = x + jnp.tanh(g_ffn[2]) * _L2_ffn_ref(_layernorm(x, axis=-1), L2_ffn_router_w, L2_ffn_w1, L2_ffn_w2)
    x = x + jnp.tanh(g_xattn[3]) * _L3_xattn_ref(_layernorm(x, axis=-1), ctx_1024, ctx_1024, mask_Bx1xSxS2_bk1, L3_xattn_Wq, L3_xattn_bq, L3_xattn_Wk, L3_xattn_bk, L3_xattn_Wv, L3_xattn_bv, L3_xattn_Wo, L3_xattn_bo)
    x = x + jnp.tanh(g_ffn[3]) * _L3_ffn_ref(_layernorm(x, axis=-1), L3_ffn_W1, L3_ffn_b1, L3_ffn_W2, L3_ffn_b2, L3_ffn_Wg, L3_ffn_bg)
    return x

_drawn_inputs = setup_inputs


def setup_inputs(seed=0):
    import zlib

    import numpy as np

    out = dict(_drawn_inputs(seed))
    spreads = {'L1_xattn_bq': (0.0, 0.463),
     'L1_xattn_bkv': (0.0, 0.1),
     'L1_xattn_bo': (0.0, 0.1),
     'L1_ffn_g1': (1.0, 0.6),
     'L1_ffn_g2': (1.0, 0.6),
     'L3_xattn_bq': (0.0, 0.597),
     'L3_xattn_bk': (0.0, 2.0),
     'L3_xattn_bv': (0.0, 0.1),
     'L3_xattn_bo': (0.0, 0.1)}
    factors = {'g_ffn': 25.576,
     'L1_ffn_w_router': 5.607,
     'L1_ffn_w2': 4.885,
     'L3_ffn_b1': 8.0,
     'L3_ffn_b2': 8.0,
     'L3_ffn_bg': 2.765}
    for name, (base, spread) in spreads.items():
        noise = np.random.default_rng([zlib.crc32(name.encode()), seed]).standard_normal(out[name].shape)
        drawn = base * np.exp(spread * noise) if base else spread * noise
        out[name] = jnp.asarray(drawn.astype(out[name].dtype))
    for name, factor in factors.items():
        out[name] = (out[name] * factor).astype(out[name].dtype)
    return out
```

```python
from contextlib import ExitStack

import numpy as np

import concourse.bass as bass
from concourse import mybir

ALU = mybir.AluOpType
ACT = mybir.ActivationFunctionType
F32 = mybir.dt.float32
I32 = mybir.dt.int32
U8 = mybir.dt.uint8
AX_X = mybir.AxisListType.X

P = 128
B = 2
S = 1024
L = 154
D = 256
H = 16
HD = D // H
KD = D // P
T = B * S
NT = T // P
TPB = S // P
TAIL = L - P
HG = 4
NG = H // HG
TR = HG * TAIL
VW = HD + 1
E8 = 8
BIG = 1e30


class Steps:

    def __init__(self):
        self.total, self.earlier = 0, 0

    def next(self):
        self.total += 1
        return self.total + self.earlier

    def turn(self, i, per):
        self.first, self.earlier, self.per = self.total, i * per, per

    def end(self, turns):
        assert self.total - self.first == self.per, (self.total - self.first, self.per)
        self.total, self.earlier = self.first + self.per * turns, 0


def shape_constants():
    f = np.float32
    row = np.arange(P)
    ec, cc = row // NT, row % NT
    out = {
        "ident": np.eye(P, dtype=f),
        "earlier": ((ec[:, None] == ec[None, :]) & (cc[:, None] < cc[None, :])).astype(f),
        "sameexp": (ec[:, None] == ec[None, :]).astype(f),
        "hm8": (row[:, None] // 16 == np.arange(8)[None, :]).astype(f),
        "hm4": (row[:, None] // 32 == np.arange(4)[None, :]).astype(f),
        "causal": np.where(row[None, :] > row[:, None], f(-BIG), f(0)).astype(f),
        "tailmask": np.broadcast_to((np.arange(TR)[:, None] % HG == np.arange(H)[None, :] % HG)[:, :, None], (TR, H, VW)).astype(f).reshape(TR, H * VW),
        "firstof": np.broadcast_to((E8 - np.arange(E8))[None, :, None], (P, E8, NT)).astype(f).reshape(P, E8 * NT).copy(),
    }

    start = np.full((B, 32, S // 16 + 1), f(BIG))
    start[:, 1, 0] = 0
    out["dtw_start"] = start.reshape(B * 32, -1)
    end = np.zeros((B, 32, S // 16), f)
    end[:, 16, -1] = 1
    out["dtw_end"] = end.reshape(B * 32, -1)[:, ::-1]

    def rope(freq, pos):
        ang = (pos[:, None] * freq[None, :]).astype(f)
        return np.cos(ang).astype(f), np.sin(ang).astype(f)

    pair = (row % HD) // 2
    isswap = (row % 32) >= HD
    f1 = (f(1) / np.power(f(10000), np.arange(0, HD, 2, dtype=f) / f(HD))).astype(f)
    f2 = np.power(f(10000), f(-2) * (np.arange(HD // 2, dtype=f) / f(HD))).astype(f)
    for name, freq, pos in (
        ("1q", f1, f(10) * (np.arange(S, dtype=f) / f(S))),
        ("1k", f1, f(10) * (np.arange(L, dtype=f) / f(L))),
        ("2", f2, np.arange(S, dtype=f)),
    ):
        c, s = rope(freq, pos)
        c, s = c[:, pair].T, s[:, pair].T
        out["stack" + name] = np.where(isswap[:, None], s, c).astype(f)
        out["cos" + name], out["sin" + name] = np.ascontiguousarray(c), np.ascontiguousarray(s)
    del out["stack1k"], out["cos1q"], out["sin1q"]
    return {k: np.ascontiguousarray(v) for k, v in out.items()}


def build(nc, a, out):
    ctx = ExitStack()

    def sb(name, shape, dt=F32):
        return ctx.enter_context(nc.sbuf_tensor(name, shape, dt))

    begun = {}

    def semaphore(name):
        handle = ctx.enter_context(nc.semaphore(name))
        begun[handle] = 0
        return handle

    def at(sem, n):
        return begun[sem] + n

    def advance(*grown):
        for sem, n in grown:
            begun[sem] += n

    dve_step = semaphore("dve_step")
    ao_ready = semaphore("ao_ready")
    ao_turned = semaphore("ao_turned")
    aot_ready = semaphore("aot_ready")
    att = semaphore("att")
    chosen = semaphore("chosen")
    cleared = semaphore("cleared")
    counted = semaphore("counted")
    cst = semaphore("cst")
    dist = semaphore("dist")
    dist2 = semaphore("dist2")
    dist_stored = semaphore("dist_stored")
    evac = semaphore("evac")
    exps_made = semaphore("exps_made")
    hT_free = semaphore("hT_free")
    h_free = semaphore("h_free")
    h_out = semaphore("h_out")
    h_ready = semaphore("h_ready")
    kept_made = semaphore("kept_made")
    loaded = semaphore("loaded")
    logits = semaphore("logits")
    max_ready = semaphore("max_ready")
    norms = semaphore("norms")
    path_stored = semaphore("path_stored")
    pe_out = semaphore("pe_out")
    probs = semaphore("probs")
    pt_ready = semaphore("pt_ready")
    ptt_ready = semaphore("ptt_ready")
    pv = semaphore("pv")
    q_out = semaphore("q_out")
    q_ready = semaphore("q_ready")
    row_made = semaphore("row_made")
    row_free = semaphore("row_free")
    row_ready = semaphore("row_ready")
    s_free = semaphore("s_free")
    scores_made = semaphore("scores_made")
    skewed = semaphore("skewed")
    squares = semaphore("squares")
    std_ready = semaphore("std_ready")
    stored = semaphore("stored")
    tails_turned = semaphore("tails_turned")
    turned = semaphore("turned")
    v_out = semaphore("v_out")
    v_ready = semaphore("v_ready")
    v_scaled = semaphore("v_scaled")
    var_ready = semaphore("var_ready")
    w_free = semaphore("w_free")
    x_loaded = semaphore("x_loaded")
    x_used = semaphore("x_used")
    y_free = semaphore("y_free")
    y_out = semaphore("y_out")
    w_loaded = [semaphore(f"w_loaded{i}") for i in range(2)]
    named = {}

    def sbuf(name, shape, dt=F32):
        named[name] = named.get(name, 0) + 1
        return nc.sbuf_tensor(name + (str(named[name]) if named[name] > 1 else ""), shape, dt)

    with ctx:
        ps = ctx.enter_context(nc.psum_tensor("banks", [P, 8, 512], F32))
        X = sb("X", [P, NT, D])
        XT = sb("XT", [P, KD, T])
        XN = sb("XN", [P, NT, D])
        ident = sb("ident", [P, P])
        ones = sb("ones", [P, 512])
        CR = sb("CR", [P, B, D])
        CRT = sb("CRT", [TAIL, B, D])
        CT = sb("CT", [P, KD, B, L])
        CTT = sb("CTT", [P, KD, B, TAIL, HG])
        tg = sb("tg", [P, 8])
        hm8 = sb("hm8", [P, 8])
        hm4 = sb("hm4", [P, 4])
        tailmask = sb("tailmask", [TR, H, VW])
        stats = sb("stats", [P, NT, 6])
        mv = sb("mv", [P, NT, 2])
        nrm = sb("nrm", [P, 4, NT])

        def prepare():
            with ExitStack() as own:
                def tmp(name, shape, dt=F32):
                    return own.enter_context(sbuf(name, shape, dt))
                grow = tmp("grow", [1, 8])
                with nc.Block() as block:
                    @block.sync
                    def _(sp):
                        sp.dma_start(CR[:, :, :], a["ctx"].rearrange("(b l) d -> l b d", b=B)[0:P]).then_inc(loaded, 16)
                        sp.dma_start(CRT[:, :, :], a["ctx"].rearrange("(b l) d -> l b d", b=B)[P:L]).then_inc(loaded, 16)
                        sp.dma_start(ident[:, :], a["ident"]).then_inc(loaded, 16)
                        sp.dma_start(hm8[:, :], a["hm8"]).then_inc(loaded, 16)
                        sp.dma_start(hm4[:, :], a["hm4"]).then_inc(loaded, 16)
                        sp.dma_start(tailmask[:, :, :], a["tailmask"].rearrange("p (h w) -> p h w", h=H)).then_inc(loaded, 16)
                        sp.dma_start(grow[:, 0:4], a["g_xattn"]).then_inc(loaded, 16)
                        sp.dma_start(grow[:, 4:8], a["g_ffn"]).then_inc(loaded, 16)
                        sp.dma_start(X[:, :, :], a["x"].rearrange("(t p) d -> p t d", p=P)).then_inc(x_loaded, 16)
                        sp.wait_ge(x_loaded, at(x_loaded, 16))

                    @block.tensor
                    def _(pe):
                        pe.wait_ge(loaded, at(loaded, 16 * 8))
                        pe.wait_ge(cst, at(cst, 1))
                        for b in range(B):
                            for k in range(KD):
                                nc.tensor.transpose(ps[:, b, k * L:k * L + P], CR[:, b, k * P:(k + 1) * P], ident[:, :])
                                ins = nc.tensor.transpose(ps[:, b, k * L + P:(k + 1) * L], CRT[:, b, k * P:(k + 1) * P],
                                                          ident[0:TAIL, 0:TAIL])
                            ins.then_inc(pe_out, 1)
                        nc.tensor.matmul(ps[:, 2, 0:8], ones[0:1, 0:P], grow[:, :], start=True, stop=True).then_inc(pe_out, 1)

                    @block.vector
                    def _(dve):
                        nc.vector.memset(ones[:, :], 1.0).then_inc(cst, 1)

                    @block.scalar
                    def _(act):
                        for b in range(B):
                            act.wait_ge(pe_out, at(pe_out, b + 1))
                            src = ps[:, b, 0:KD * L].rearrange("p (k l) -> p k l", k=KD)
                            nc.scalar.copy(CT[:, :, b, :], src)
                            for k in range(KD):
                                nc.scalar.copy(CTT[:, k, b, :, :],
                                               src[:, k, P:L].unsqueeze(2).broadcast_to([P, TAIL, HG]))
                        act.wait_ge(pe_out, at(pe_out, 3))
                        nc.scalar.activation(tg[:, :], ps[:, 2, 0:8], ACT.Tanh)
            advance((loaded, 16 * 8), (x_loaded, 16), (pe_out, 3), (cst, 1))

        def normalise(src, dst, mean, eps, gcol=None, also=None):
            with nc.Block() as block:
                @block.vector
                def _(dve):
                    step = Steps()
                    for c in range(NT):
                        ins = nc.vector.bn_stats(stats[:, c, :], src[:, c, :])
                    ins.then_inc(dve_step, 1)
                    dve.wait_ge(dve_step, at(dve_step, step.next()))
                    for c in range(NT):
                        ins = nc.vector.bn_aggr(mv[:, c, :], stats[:, c, :])
                    ins.then_inc(dve_step, 1)
                    dve.wait_ge(dve_step, at(dve_step, step.next()))
                    if mean:
                        nc.vector.tensor_scalar(nrm[:, 0, :], mv[:, :, 1], eps, None, ALU.add).then_inc(dve_step, 1)
                        dve.wait_ge(dve_step, at(dve_step, step.next()))
                    else:
                        nc.vector.tensor_tensor(nrm[:, 1, :], mv[:, :, 0], mv[:, :, 0], ALU.mult).then_inc(dve_step, 1)
                        dve.wait_ge(dve_step, at(dve_step, step.next()))
                        nc.vector.scalar_tensor_tensor(nrm[:, 0, :], mv[:, :, 1], eps, nrm[:, 1, :], ALU.add, ALU.add).then_inc(dve_step, 1)
                        dve.wait_ge(dve_step, at(dve_step, step.next()))
                    nc.vector.engine_nop().then_inc(var_ready, 1)
                    dve.wait_ge(std_ready, at(std_ready, 1))
                    nc.vector.reciprocal(nrm[:, 3, :], nrm[:, 2, :]).then_inc(dve_step, 1)
                    dve.wait_ge(dve_step, at(dve_step, step.next()))
                    for c in range(NT):
                        if mean:
                            ins = nc.vector.tensor_scalar(dst[:, c, :], src[:, c, :], mv[:, c, 0:1], nrm[:, 3, c:c + 1],
                                                          ALU.subtract, ALU.mult)
                        else:
                            ins = nc.vector.tensor_scalar(dst[:, c, :], src[:, c, :], nrm[:, 3, c:c + 1], None, ALU.mult)
                        ins.then_inc(row_ready, 1)
                    advance((dve_step, step.total))

                @block.scalar
                def _(act):
                    act.wait_ge(var_ready, at(var_ready, 1))
                    nc.scalar.activation(nrm[:, 2, :], nrm[:, 0, :], ACT.Sqrt).then_inc(std_ready, 1)
                    for c2 in range(NT // 2):
                        act.wait_ge(pe_out, at(pe_out, c2 + 1))
                        for k in range(KD):
                            src_ = ps[:, c2 % 4, k * D:(k + 1) * D]
                            d_ = XT[:, k, c2 * D:(c2 + 1) * D]
                            if gcol is None:
                                ins = nc.scalar.copy(d_, src_)
                            else:
                                ins = nc.scalar.activation(d_, src_, ACT.Copy, scale=gcol[:, k:k + 1])
                        ins.then_inc(evac, 1)

                @block.tensor
                def _(pe):
                    for c2 in range(NT // 2):
                        pe.wait_ge(row_ready, at(row_ready, 2 * c2 + 2))
                        if c2 >= 4:
                            pe.wait_ge(evac, at(evac, c2 - 3))
                        for k in range(KD):
                            for j in range(2):
                                ins = nc.tensor.transpose(ps[:, c2 % 4, k * D + j * P:k * D + (j + 1) * P],
                                                          dst[:, 2 * c2 + j, k * P:(k + 1) * P], ident[:, :])
                        ins.then_inc(pe_out, 1)
            advance((var_ready, 1), (std_ready, 1), (row_ready, NT), (pe_out, NT // 2), (evac, NT // 2))

        def load_weights(pairs):
            with nc.Block() as block:
                @block.sync
                def _(sp):
                    for dst, src in pairs:
                        sp.dma_start(dst, src).then_inc(loaded, 16)
                    sp.wait_ge(loaded, at(loaded, 16 * len(pairs)))
            advance((loaded, 16 * len(pairs)))

        def transpose_weights(pairs):
            with nc.Block() as block:
                @block.tensor
                def _(pe):
                    for n, (dst, src) in enumerate(pairs):
                        if n >= 4:
                            pe.wait_ge(evac, at(evac, 2 * (n - 3)))
                        for ki in range(KD):
                            for ko in range(KD):
                                ins = nc.tensor.transpose(ps[:, (n % 4) * 2 + ki, ko * P:(ko + 1) * P],
                                                          src[:, ko, ki * P:(ki + 1) * P], ident[:, :])
                            ins.then_inc(pe_out, 1)

                @block.scalar
                def _(act):
                    for n, (dst, src) in enumerate(pairs):
                        for ki in range(KD):
                            act.wait_ge(pe_out, at(pe_out, 2 * n + ki + 1))
                            nc.scalar.copy(dst[:, ki, :], ps[:, (n % 4) * 2 + ki, 0:D]).then_inc(evac, 1)
            advance((pe_out, 2 * len(pairs)), (evac, 2 * len(pairs)))

        def keys_values(KB, VM, VT, heads, mask, scale, wkA, wv, wkB=None, bkA=None, bkB=None, bv=None, cosk=None, sink=None, kr=None):
            ch_n = H // heads
            n_ps = B * 2
            with nc.Block() as block:
                @block.tensor
                def _(pe):
                    flat = CT[:, :, :, :].rearrange("p k b l -> p k (b l)")
                    for ch in range(ch_n):
                        if ch >= 2:
                            pe.wait_ge(evac, at(evac, ch - 1))
                        for bank, w, bias in ((ch % 2, wkA, bkA), (2 + ch % 2, wkB, bkB)):
                            if w is None:
                                continue
                            for k in range(KD):
                                ins = nc.tensor.matmul(ps[:, bank, 0:B * L], w[:, k, ch * P:(ch + 1) * P], flat[:, k, :],
                                                       start=(k == 0), stop=(k == KD - 1 and bias is None))
                            if bias is not None:
                                ins = nc.tensor.matmul(ps[:, bank, 0:B * L], bias[0:1, ch * P:(ch + 1) * P], ones[0:1, 0:B * L],
                                                       start=False, stop=True)
                        ins.then_inc(pe_out, 1)
                    for b in range(B):
                        for k in range(KD):
                            ins = nc.tensor.matmul(ps[:, 4 + b, 0:D], CT[:, k, b, 0:P], wv[:, k, :],
                                                   start=(k == 0), stop=(k == KD - 1 and bv is None))
                        if bv is not None:
                            ins = nc.tensor.matmul(ps[:, 4 + b, 0:D], ones[0:1, 0:P], bv[0:1, :], start=False, stop=True)
                        ins.then_inc(v_out, 1)
                        for k in range(KD):
                            ins = nc.tensor.matmul(ps[0:TR, 6 + b, 0:D], CTT[:, k, b, :, :].rearrange("p l g -> p (l g)"), wv[:, k, :],
                                                   start=(k == 0), stop=(k == KD - 1 and bv is None))
                        if bv is not None:
                            ins = nc.tensor.matmul(ps[0:TR, 6 + b, 0:D], ones[0:1, 0:TR], bv[0:1, :], start=False, stop=True)
                        ins.then_inc(v_out, 1)

                @block.vector
                def _(dve):
                    step = Steps()
                    for ch in range(ch_n):
                        dve.wait_ge(pe_out, at(pe_out, ch + 1))
                        src = ps[:, ch % 2, 0:B * L].rearrange("p (b l) -> p b l", b=B)
                        if cosk is not None:
                            cb = cosk[:, :].unsqueeze(1).broadcast_to([P, B, L])
                            sb_ = sink[:, :].unsqueeze(1).broadcast_to([P, B, L])
                            nc.vector.tensor_tensor(kr[:, 0], src, cb, ALU.mult)
                            nc.vector.tensor_tensor(kr[:, 1], ps[:, 2 + ch % 2, 0:B * L].rearrange("p (b l) -> p b l", b=B),
                                                         sb_, ALU.mult).then_inc(dve_step, 1)
                            dve.wait_ge(dve_step, at(dve_step, step.next()))
                            nc.vector.tensor_tensor(kr[:, 0], kr[:, 0], kr[:, 1], ALU.add).then_inc(dve_step, 1)
                            dve.wait_ge(dve_step, at(dve_step, step.next()))
                            src = kr[:, 0]
                        for hh in range(heads):
                            ins = nc.vector.tensor_scalar(KB[:, (ch * heads + hh) // HG, :, :, hh % HG], src, mask[:, hh:hh + 1], scale, ALU.mult, ALU.mult)
                        ins.then_inc(evac, 1)
                        dve.wait_ge(evac, at(evac, ch + 1))
                    nc.vector.memset(VM[:, :, :, HD:VW], 1.0)
                    for b in range(B):
                        dve.wait_ge(v_out, at(v_out, 2 * b + 1))
                        nc.vector.tensor_copy(VM[:, b, :, 0:HD], ps[:, 4 + b, 0:D].rearrange("p (h w) -> p h w", h=H))
                        dve.wait_ge(v_out, at(v_out, 2 * b + 2))
                        nc.vector.tensor_tensor(VT[:, b, :, 0:HD], ps[0:TR, 6 + b, 0:D].rearrange("p (h w) -> p h w", h=H),
                                                tailmask[:, :, 0:HD], ALU.mult)
                        nc.vector.tensor_copy(VT[:, b, :, HD:VW], tailmask[:, :, HD:VW])
                    advance((dve_step, step.total))
            advance((pe_out, ch_n), (evac, ch_n), (v_out, 2 * B))

        def attention0():
            with ExitStack() as own:
                def tmp(name, shape, dt=F32):
                    return own.enter_context(sbuf(name, shape, dt))
                W = [tmp(f"a0w{i}", [P, KD, D]) for i in range(4)]
                KB = tmp("a0KB", [P, NG, B, L, HG])
                VM = tmp("a0VM", [P, B, H, VW])
                VT = tmp("a0VT", [TR, B, H, VW])
                with ExitStack() as own2:
                    R = [own2.enter_context(sbuf(f"a0r{i}", [P, KD, D], F32)) for i in range(4)]
                    load_weights([(R[i][:, :, :], a[f"L0_xattn_W{c}"].rearrange("(k p) d -> p k d", p=P))
                                  for i, c in enumerate("qkvo")])
                    transpose_weights([(W[i], R[i]) for i in range(4)])
                wq, wk, wv, wo = W
                keys_values(KB, VM, VT, 8, hm8, float(D) ** -0.5, wk, wv)
                normalise(X, XN, True, 1e-5)
                AT = XN[:, :, :].rearrange("p c d -> p (c d)").rearrange("p (k t) -> p k t", k=KD)
                QT = tmp("a0QT", [P, KD, T])
                with nc.Block() as block:
                    @block.tensor
                    def _(pe):
                        for m in range(KD):
                            for n in range(4):
                                i = 4 * m + n
                                for k in range(KD):
                                    ins = nc.tensor.matmul(ps[:, i, :], wq[:, k, m * P:(m + 1) * P], XT[:, k, n * 512:(n + 1) * 512],
                                                           start=(k == 0), stop=(k == KD - 1))
                                ins.then_inc(pe_out, 1)

                    @block.scalar
                    def _(act):
                        for i in range(8):
                            act.wait_ge(pe_out, at(pe_out, i + 1))
                            nc.scalar.copy(QT[:, i // 4, (i % 4) * 512:(i % 4 + 1) * 512], ps[:, i, :])
                advance((pe_out, 8))

                EX = tmp("a0E", [P, H + NG, S])
                nm = tmp("a0nm", [P, H + NG])
                sm = tmp("a0sm", [P, H + NG])
                rc = tmp("a0rc", [P, H + NG])
                VB = XT[:, :, :].rearrange("p k t -> p (k t)")[:, 0:(H + NG) * P].rearrange("p (u c) -> p u c", c=P)
                NB = tmp("a0NB", [P, H + NG, P])
                dn = tmp("a0dn", [P, 2, 512])
                with nc.Block() as block:
                    @block.vector
                    def _(dve):
                        nc.vector.memset(VB[:, :, :], 0.0)
                        nc.vector.memset(NB[:, :, :], 0.0)
                units = [(u, P, u // 8, u % 8) for u in range(H)] + [(H + g, TR, g // 2, g) for g in range(NG)]
                for b in range(B):
                    with nc.Block() as block:
                        @block.tensor
                        def _(pe):
                            for u, rows, m, hh in units:
                                if u >= 2:
                                    pe.wait_ge(probs, at(probs, u - 1))
                                lhs = (KB[:, u // HG, b, 0:P, u % HG] if u < H else
                                       KB[:, hh, b, P:L, :].rearrange("p l h -> p (l h)"))
                                for n in range(2):
                                    ins = nc.tensor.matmul(ps[0:rows, 2 * (u % 2) + n, :], lhs,
                                                           QT[:, m, b * S + n * 512:b * S + (n + 1) * 512], start=True, stop=True)
                                ins.then_inc(scores_made, 1)
                            pe.wait_ge(v_scaled, at(v_scaled, 1))
                            for i in range(4):
                                m, n = i // 2, i % 2
                                if i >= 2:
                                    pe.wait_ge(att, at(att, i - 1))
                                us = [8 * m + j for j in range(8)] + [H + 2 * m, H + 2 * m + 1]
                                for bank, lhs in ((4 + i % 2, VB), (6 + i % 2, NB)):
                                    for j, u in enumerate(us):
                                        rows = P if u < H else TR
                                        ins = nc.tensor.matmul(ps[:, bank, :], lhs[0:rows, u, :],
                                                               EX[0:rows, u, n * 512:(n + 1) * 512], start=(j == 0), stop=(j == 9))
                                ins.then_inc(pv, 1)

                        @block.vector
                        def _(dve):
                            step = Steps()
                            for u, rows, m, hh in units:
                                dve.wait_ge(scores_made, at(scores_made, u + 1))
                                nc.vector.tensor_reduce(nm[0:rows, u:u + 1], ps[0:rows, 2 * (u % 2):2 * (u % 2) + 2, :],
                                                            mybir.AxisListType.XY, ALU.max, negate=True).then_inc(max_ready, 1)
                            dve.wait_ge(probs, at(probs, H + NG))
                            nc.vector.reciprocal(rc[:, 0:H], sm[:, 0:H])
                            nc.vector.reciprocal(rc[0:TR, H:], sm[0:TR, H:]).then_inc(dve_step, 1)
                            dve.wait_ge(dve_step, at(dve_step, step.next()))
                            for h in range(H):
                                col = (h % 8) * HD
                                nc.vector.tensor_scalar(VB[:, h, col:col + HD], VM[:, b, h, 0:HD], rc[:, h:h + 1], None, ALU.mult)
                                nc.vector.tensor_scalar(NB[:, h, col:col + HD], ones[:, 0:HD], rc[:, h:h + 1], None, ALU.mult)
                            for g in range(NG):
                                col = (g % 2) * HG * HD
                                v = VB[0:TR, H + g, col:col + HG * HD].rearrange("p (h w) -> p h w", h=HG)
                                w = NB[0:TR, H + g, col:col + HG * HD].rearrange("p (h w) -> p h w", h=HG)
                                nc.vector.tensor_scalar(v, VT[:, b, g * HG:(g + 1) * HG, 0:HD], rc[0:TR, H + g:H + g + 1], None, ALU.mult)
                                ins = nc.vector.tensor_scalar(w, tailmask[:, g * HG:(g + 1) * HG, 0:HD], rc[0:TR, H + g:H + g + 1], None, ALU.mult)
                            ins.then_inc(v_scaled, 1)
                            for i in range(4):
                                m, n = i // 2, i % 2
                                dve.wait_ge(pv, at(pv, i + 1))
                                nc.vector.reciprocal(dn[:, i % 2, :], ps[:, 6 + i % 2, :]).then_inc(dve_step, 1)
                                dve.wait_ge(dve_step, at(dve_step, step.next()))
                                nc.vector.tensor_tensor(AT[:, m, b * S + n * 512:b * S + (n + 1) * 512], ps[:, 4 + i % 2, :],
                                                            dn[:, i % 2, :], ALU.mult).then_inc(att, 1)
                            advance((dve_step, step.total))

                        @block.scalar
                        def _(act):
                            for u, rows, m, hh in units:
                                act.wait_ge(max_ready, at(max_ready, u + 1))
                                nc.scalar.activation(EX[0:rows, u, :].rearrange("p (n q) -> p n q", n=2), ps[0:rows, 2 * (u % 2):2 * (u % 2) + 2, :],
                                                         ACT.Exp, bias=nm[0:rows, u:u + 1], accum_out=sm[0:rows, u:u + 1]).then_inc(probs, 1)
                    advance((scores_made, H + NG), (max_ready, H + NG), (probs, H + NG), (v_scaled, 1), (pv, 4), (att, 4))
                with nc.Block() as block:
                    @block.tensor
                    def _(pe):
                        for c in range(NT):
                            if c >= 4:
                                pe.wait_ge(x_used, at(x_used, c - 3))
                            for k in range(KD):
                                ins = nc.tensor.matmul(ps[:, c % 4, 0:D], AT[:, k, c * P:(c + 1) * P], wo[:, k, :],
                                                       start=(k == 0), stop=(k == KD - 1))
                            ins.then_inc(pe_out, 1)

                    @block.vector
                    def _(dve):
                        for c in range(NT):
                            dve.wait_ge(pe_out, at(pe_out, c + 1))
                            nc.vector.scalar_tensor_tensor(X[:, c, :], ps[:, c % 4, 0:D], tg[:, 0:1], X[:, c, :],
                                                               ALU.mult, ALU.add).then_inc(x_used, 1)
                advance((pe_out, NT), (x_used, NT))

        def route(mode, n_exp, wr, gate, G, bias=None, capacity=None):
            with ExitStack() as own:
                def tmp(name, shape, dt=F32):
                    return own.enter_context(sbuf("r_" + name, shape, dt))
                firstof = tmp("firstof", [P, E8, NT])
                earlier = tmp("earlier", [P, P])
                sameexp = tmp("sameexp", [P, P])
                pr = tmp("pr", [P, n_exp, NT])
                w = tmp("w", [P, n_exp, NT])
                oh = [tmp(f"oh{i}", [P, n_exp, NT]) for i in range(2)]
                m = tmp("m", [P, 8, NT])
                ohT = [tmp(f"ohT{i}", [P, P]) for i in range(2)]
                cs = [tmp(f"cs{i}", [P, P]) for i in range(2)]
                keep = [tmp(f"keep{i}", [P, P]) for i in range(2)]
                col = tmp("col", [P, 8])
                thr = tmp("thr", [P, 4], I32)

                def bc(v):
                    return v.unsqueeze(1).broadcast_to([P, n_exp, NT])

                def by_tile(v):
                    return v.rearrange("p e c -> p c e")

                with nc.Block() as block:
                    @block.sync
                    def _(sp):
                        sp.dma_start(firstof[:, :, :], a["firstof"].rearrange("p (e c) -> p e c", e=E8)).then_inc(loaded, 16)
                        sp.dma_start(earlier[:, :], a["earlier"]).then_inc(loaded, 16)
                        sp.dma_start(sameexp[:, :], a["sameexp"]).then_inc(loaded, 16)

                    @block.tensor
                    def _(pe):
                        for c in range(NT):
                            for k in range(KD):
                                ins = nc.tensor.matmul(ps[:, 0, c * n_exp:(c + 1) * n_exp], XT[:, k, c * P:(c + 1) * P], wr[:, k, :],
                                                       start=(k == 0), stop=(k == KD - 1 and bias is None))
                            if bias is not None:
                                ins = nc.tensor.matmul(ps[:, 0, c * n_exp:(c + 1) * n_exp], ones[0:1, 0:P], bias[0:1, :],
                                                       start=False, stop=True)
                        ins.then_inc(pe_out, 1)
                        if mode == "first":
                            pe.wait_ge(loaded, at(loaded, 48))
                            for i in range(2):
                                pe.wait_ge(chosen, at(chosen, i + 1))
                                nc.tensor.transpose(ps[:, 1 + i, 0:P], oh[i][:, :, :].rearrange("p e c -> p (e c)"), ident[:, :]).then_inc(pe_out, 1)
                            for i in range(2):
                                pe.wait_ge(counted, at(counted, i + 1))
                                nc.tensor.matmul(ps[:, 3 + i, 0:1], earlier[:, :], cs[i][:, P - 1:P], start=True, stop=True).then_inc(pe_out, 1)
                            for i in range(2):
                                pe.wait_ge(kept_made, at(kept_made, i + 1))
                                nc.tensor.transpose(ps[:, 5 + i, 0:P], keep[i][:, :], ident[:, :]).then_inc(pe_out, 1)
                        if mode == "best":
                            pe.wait_ge(loaded, at(loaded, 48))
                            pe.wait_ge(chosen, at(chosen, 1))
                            nc.tensor.transpose(ps[:, 1, 0:P], w[:, :, :].rearrange("p e c -> p (e c)"), ident[:, :]).then_inc(pe_out, 1)
                            for i in range(31):
                                pe.wait_ge(counted, at(counted, i + 1))
                                nc.tensor.matmul(ps[:, 2 + i % 2, 0:1], sameexp[:, :], col[:, 0:1], start=True, stop=True).then_inc(pe_out, 1)
                            pe.wait_ge(counted, at(counted, 32))
                            nc.tensor.matmul(ps[:, 4, 0:1], earlier[:, :], cs[0][:, P - 1:P], start=True, stop=True).then_inc(pe_out, 1)
                            pe.wait_ge(kept_made, at(kept_made, 1))
                            nc.tensor.transpose(ps[:, 5, 0:P], keep[0][:, :], ident[:, :]).then_inc(pe_out, 1)

                    @block.scalar
                    def _(act):
                        act.wait_ge(logits, at(logits, 1))
                        nc.scalar.activation(pr[:, :, :], pr[:, :, :], ACT.Exp).then_inc(exps_made, 1)

                    @block.vector
                    def _(dve):
                        step = Steps()
                        dve.wait_ge(pe_out, at(pe_out, 1))
                        nc.vector.tensor_copy(pr[:, :, :], ps[:, 0, 0:NT * n_exp].rearrange("p (c e) -> p e c", c=NT)).then_inc(dve_step, 1)
                        dve.wait_ge(dve_step, at(dve_step, step.next()))
                        nc.vector.tensor_reduce(m[:, 0, :], by_tile(pr[:, :, :]), AX_X, ALU.max).then_inc(dve_step, 1)
                        dve.wait_ge(dve_step, at(dve_step, step.next()))
                        nc.vector.tensor_tensor(pr[:, :, :], pr[:, :, :], bc(m[:, 0, :]), ALU.subtract).then_inc(logits, 1)
                        dve.wait_ge(exps_made, at(exps_made, 1))
                        nc.vector.tensor_reduce(m[:, 0, :], by_tile(pr[:, :, :]), AX_X, ALU.add).then_inc(dve_step, 1)
                        dve.wait_ge(dve_step, at(dve_step, step.next()))
                        nc.vector.reciprocal(m[:, 1, :], m[:, 0, :]).then_inc(dve_step, 1)
                        dve.wait_ge(dve_step, at(dve_step, step.next()))
                        nc.vector.tensor_tensor(pr[:, :, :], pr[:, :, :], bc(m[:, 1, :]), ALU.mult).then_inc(dve_step, 1)
                        dve.wait_ge(dve_step, at(dve_step, step.next()))
                        dve.wait_ge(loaded, at(loaded, 48))
                        ks = 1 if mode == "top1" else 2
                        for i in range(ks):
                            nc.vector.tensor_reduce(m[:, 2 + i, :], by_tile(pr[:, :, :]), AX_X, ALU.max).then_inc(dve_step, 1)
                            dve.wait_ge(dve_step, at(dve_step, step.next()))
                            nc.vector.tensor_tensor(w[:, :, :], pr[:, :, :], bc(m[:, 2 + i, :]), ALU.is_equal).then_inc(dve_step, 1)
                            dve.wait_ge(dve_step, at(dve_step, step.next()))
                            nc.vector.tensor_tensor(w[:, :, :], w[:, :, :], firstof[:, 0:n_exp, :], ALU.mult).then_inc(dve_step, 1)
                            dve.wait_ge(dve_step, at(dve_step, step.next()))
                            nc.vector.tensor_reduce(m[:, 4, :], by_tile(w[:, :, :]), AX_X, ALU.max).then_inc(dve_step, 1)
                            dve.wait_ge(dve_step, at(dve_step, step.next()))
                            ins = nc.vector.tensor_tensor(oh[i][:, :, :], w[:, :, :], bc(m[:, 4, :]), ALU.is_equal)
                            ins.then_inc(dve_step, 1)
                            dve.wait_ge(dve_step, at(dve_step, step.next()))
                            if i == 0 and ks == 2:
                                nc.vector.scalar_tensor_tensor(pr[:, :, :], oh[0][:, :, :], -2.0, pr[:, :, :], ALU.mult, ALU.add).then_inc(dve_step, 1)
                                dve.wait_ge(dve_step, at(dve_step, step.next()))
                        if mode == "top1":
                            nc.vector.tensor_scalar(G[:, :, :], oh[0][:, :, :], gate, None, ALU.mult).then_inc(dve_step, 1)
                            dve.wait_ge(dve_step, at(dve_step, step.next()))
                        if mode in ("first", "top2"):
                            eps = 1e-9 if mode == "top2" else 0.0
                            nc.vector.scalar_tensor_tensor(m[:, 5, :], m[:, 2, :], eps, m[:, 3, :], ALU.add, ALU.add).then_inc(dve_step, 1)
                            dve.wait_ge(dve_step, at(dve_step, step.next()))
                            nc.vector.reciprocal(m[:, 6, :], m[:, 5, :]).then_inc(dve_step, 1)
                            dve.wait_ge(dve_step, at(dve_step, step.next()))
                            for i in range(2):
                                nc.vector.scalar_tensor_tensor(m[:, 2 + i, :], m[:, 2 + i, :], gate, m[:, 6, :], ALU.mult, ALU.mult).then_inc(dve_step, 1)
                                dve.wait_ge(dve_step, at(dve_step, step.next()))
                        kept = [oh[0][:, :, :], oh[1][:, :, :]]
                        if mode == "first":
                            nc.vector.engine_nop().then_inc(chosen, 2)
                            for i in range(2):
                                dve.wait_ge(pe_out, at(pe_out, 2 + i))
                                nc.vector.tensor_copy(ohT[i][:, :], ps[:, 1 + i, 0:P]).then_inc(dve_step, 1)
                                dve.wait_ge(dve_step, at(dve_step, step.next()))
                                nc.vector.tensor_tensor_scan(cs[i][:, :], ones[:, 0:P], ohT[i][:, :], 0.0, ALU.mult, ALU.add).then_inc(counted, 1)
                            for i in range(2):
                                dve.wait_ge(counted, at(counted, i + 1))
                                dve.wait_ge(pe_out, at(pe_out, 4 + i))
                                nc.vector.tensor_scalar(cs[i][:, :], cs[i][:, :], ps[:, 3 + i, 0:1], float(capacity), ALU.add, ALU.is_le).then_inc(dve_step, 1)
                                dve.wait_ge(dve_step, at(dve_step, step.next()))
                                nc.vector.tensor_tensor(keep[i][:, :], cs[i][:, :], ohT[i][:, :], ALU.mult).then_inc(kept_made, 1)
                            for i in range(2):
                                dve.wait_ge(pe_out, at(pe_out, 6 + i))
                                kept[i] = ps[:, 5 + i, 0:P].rearrange("p (e c) -> p e c", e=n_exp)
                        if mode in ("first", "top2", "best"):
                            dst = w if mode == "best" else G
                            nc.vector.tensor_tensor(oh[0][:, :, :], kept[0], bc(m[:, 2, :]), ALU.mult).then_inc(dve_step, 1)
                            dve.wait_ge(dve_step, at(dve_step, step.next()))
                            nc.vector.tensor_tensor(oh[1][:, :, :], kept[1], bc(m[:, 3, :]), ALU.mult).then_inc(dve_step, 1)
                            dve.wait_ge(dve_step, at(dve_step, step.next()))
                            nc.vector.tensor_tensor(dst[:, :, :], oh[0][:, :, :], oh[1][:, :, :], ALU.add).then_inc(dve_step, 1)
                            dve.wait_ge(dve_step, at(dve_step, step.next()))
                        if mode == "best":
                            nc.vector.engine_nop().then_inc(chosen, 1)
                            gT = ohT[0]
                            dve.wait_ge(pe_out, at(pe_out, 2))
                            nc.vector.memset(thr[:, 0:1], 0)
                            nc.vector.tensor_copy(gT[:, :], ps[:, 1, 0:P]).then_inc(dve_step, 1)
                            dve.wait_ge(dve_step, at(dve_step, step.next()))
                            for i in range(30):
                                bit = 1 << (29 - i)
                                nc.vector.tensor_scalar(thr[:, 1:2], thr[:, 0:1], bit, None, ALU.bitwise_or).then_inc(dve_step, 1)
                                dve.wait_ge(dve_step, at(dve_step, step.next()))
                                nc.vector.tensor_scalar(cs[1][:, :], gT[:, :], thr[:, 1:2].bitcast(F32), None, ALU.is_ge, ALU.add,
                                                            accum_out=col[:, 0:1]).then_inc(counted, 1)
                                dve.wait_ge(pe_out, at(pe_out, 3 + i))
                                nc.vector.tensor_scalar(thr[:, 2:3], ps[:, 2 + i % 2, 0:1], float(capacity), float(bit), ALU.is_ge, ALU.mult).then_inc(dve_step, 1)
                                dve.wait_ge(dve_step, at(dve_step, step.next()))
                                nc.vector.tensor_tensor(thr[:, 0:1], thr[:, 0:1], thr[:, 2:3], ALU.bitwise_or).then_inc(dve_step, 1)
                                dve.wait_ge(dve_step, at(dve_step, step.next()))
                            t32 = thr[:, 0:1].bitcast(F32)
                            nc.vector.tensor_scalar(keep[1][:, :], gT[:, :], t32, None, ALU.is_gt, ALU.add, accum_out=col[:, 0:1]).then_inc(counted, 1)
                            nc.vector.tensor_scalar(ohT[1][:, :], gT[:, :], t32, None, ALU.is_equal).then_inc(dve_step, 1)
                            dve.wait_ge(dve_step, at(dve_step, step.next()))
                            nc.vector.tensor_tensor_scan(cs[0][:, :], ones[:, 0:P], ohT[1][:, :], 0.0, ALU.mult, ALU.add).then_inc(counted, 1)
                            dve.wait_ge(pe_out, at(pe_out, 33))
                            nc.vector.tensor_scalar(col[:, 1:2], ps[:, 2, 0:1], -1.0, float(capacity), ALU.mult, ALU.add).then_inc(dve_step, 1)
                            dve.wait_ge(dve_step, at(dve_step, step.next()))
                            dve.wait_ge(pe_out, at(pe_out, 34))
                            nc.vector.tensor_scalar(cs[1][:, :], cs[0][:, :], ps[:, 4, 0:1], col[:, 1:2], ALU.add, ALU.is_le).then_inc(dve_step, 1)
                            dve.wait_ge(dve_step, at(dve_step, step.next()))
                            nc.vector.tensor_tensor(cs[1][:, :], cs[1][:, :], ohT[1][:, :], ALU.mult).then_inc(dve_step, 1)
                            dve.wait_ge(dve_step, at(dve_step, step.next()))
                            nc.vector.tensor_tensor(cs[1][:, :], cs[1][:, :], keep[1][:, :], ALU.add).then_inc(dve_step, 1)
                            dve.wait_ge(dve_step, at(dve_step, step.next()))
                            nc.vector.tensor_tensor(keep[0][:, :], cs[1][:, :], gT[:, :], ALU.mult).then_inc(kept_made, 1)
                            dve.wait_ge(pe_out, at(pe_out, 35))
                            nc.vector.tensor_scalar(G[:, :, :], ps[:, 5, 0:P].rearrange("p (e c) -> p e c", e=n_exp), gate, None, ALU.mult).then_inc(dve_step, 1)
                            dve.wait_ge(dve_step, at(dve_step, step.next()))
                        advance((dve_step, step.total))
            advance((loaded, 48), (logits, 1), (exps_made, 1), (pe_out, {"first": 7, "best": 35}.get(mode, 1)), (chosen, {"first": 2, "best": 1}.get(mode, 0)), (counted, {"first": 2, "best": 32}.get(mode, 0)), (kept_made, {"first": 2, "best": 1}.get(mode, 0)))

        def experts(n_exp, ff, w1d, w2d, func, G, b1=None, b2=None):
            fc = ff // P
            NB4 = 4
            GT = T // 512
            with ExitStack() as own:
                def tmp(name, shape, dt=F32):
                    return own.enter_context(sbuf("e_" + name, shape, dt))
                w1 = [tmp(f"w1{i}", [P, KD, ff]) for i in range(2)]
                w2 = [tmp(f"w2{i}", [P, fc, D]) for i in range(2)]
                hT = [tmp(f"hT{i}", [P, fc, 512]) for i in range(2)]
                w1v = w1d.rearrange("e (k p) f -> e p k f", p=P)
                w2v = w2d.rearrange("e (f p) d -> e p f d", p=P)
                with nc.Block() as block:
                    @block.sync
                    def _(sp):
                        with sp.Fori(0, n_exp // 2) as ep:
                            for par in range(2):
                                sp.wait_ge(w_free, at(w_free, 2 * ep + par + 1))
                                sp.dma_start(w1[par][:, :, :], w1v[2 * ep + par]).then_inc(w_loaded[par], 16)
                                sp.dma_start(w2[par][:, :, :], w2v[2 * ep + par]).then_inc(w_loaded[par], 16)

                    @block.tensor
                    def _(pe):
                        pe.sem_inc(w_free, 2)
                        with pe.Fori(0, n_exp // 2) as ep:
                            for par in range(2):
                                with pe.Fori(0, GT // 2) as gp:
                                    for gg in range(2):
                                        if gg == 0:
                                            pe.wait_ge(w_loaded[par], at(w_loaded[par], 32 * ep + 32))
                                        n = ep * (2 * GT) + par * GT + gp * 2 + gg
                                        for f in range(fc):
                                            pe.wait_ge(h_free, at(h_free, n * fc + f + 1))
                                            for k in range(KD):
                                                ins = nc.tensor.matmul(ps[:, f % NB4, :], w1[par][:, k, f * P:(f + 1) * P],
                                                                       XT[:, k, bass.ds(gp * 1024 + gg * 512, 512)],
                                                                       start=(k == 0), stop=(k == KD - 1))
                                            ins.then_inc(h_out, 1)
                                        for tt in range(4):
                                            pe.wait_ge(y_free, at(y_free, n * 4 + tt + 1))
                                            for f in range(fc):
                                                if tt == 0:
                                                    pe.wait_ge(h_ready, at(h_ready, n * fc + f + 1))
                                                ins = nc.tensor.matmul(ps[:, NB4 + tt, 0:D], hT[gg][:, f, tt * P:(tt + 1) * P],
                                                                       w2[par][:, f, :], start=(f == 0), stop=(f == fc - 1 and b2 is None))
                                            if b2 is not None:
                                                ins = nc.tensor.matmul(ps[:, NB4 + tt, 0:D], ones[0:1, 0:P], b2[0:1, bass.ds(ep * (2 * D) + par * D, D)],
                                                                       start=False, stop=True)
                                            ins.then_inc(y_out, 1)
                                pe.wait_ge(y_out, at(y_out, ep * (8 * GT) + (par + 1) * 4 * GT))
                                pe.sem_inc(w_free, 1)

                    @block.scalar
                    def _(act):
                        def hidden(ep):
                            for par in range(2):
                                with act.Fori(0, GT // 2) as gp:
                                    for gg in range(2):
                                        n = ep * (2 * GT) + par * GT + gp * 2 + gg
                                        act.wait_ge(hT_free, at(hT_free, n + 1))
                                        for f in range(fc):
                                            act.wait_ge(h_out, at(h_out, n * fc + f + 1))
                                            col = 0 if b1 is None else (2 * ep + par) * fc + f
                                            bias = 0.0 if b1 is None else b1[:, col:col + 1]
                                            ins = nc.scalar.activation(hT[gg][:, f, :], ps[:, f % NB4, :], func, bias=bias)
                                            ins.then_inc(h_ready, 1)
                                            act.wait_ge(h_ready, at(h_ready, n * fc + f + 1))
                                            act.sem_inc(h_free, 1)

                        act.sem_inc(h_free, NB4)
                        if b1 is None:
                            with act.Fori(0, n_exp // 2) as ep:
                                hidden(ep)
                        else:
                            for ep in range(n_exp // 2):
                                hidden(ep)

                    @block.vector
                    def _(dve):
                        dve.sem_inc(y_free, 4)
                        dve.sem_inc(hT_free, 2)
                        with dve.Fori(0, n_exp // 2) as ep:
                            for par in range(2):
                                with dve.Fori(0, GT // 2) as gp:
                                    for gg in range(2):
                                        n = ep * (2 * GT) + par * GT + gp * 2 + gg
                                        for tt in range(4):
                                            dve.wait_ge(y_out, at(y_out, n * 4 + tt + 1))
                                            c = gp * 8 + gg * 4 + tt
                                            x = X[:, bass.ds(c, 1), :].rearrange("p c d -> p (c d)")
                                            g = G[:, :, :].rearrange("p e c -> p (e c)")[:, bass.ds(ep * (2 * NT) + par * NT + c, 1)]
                                            nc.vector.scalar_tensor_tensor(x, ps[:, NB4 + tt, 0:D], g, x, ALU.mult, ALU.add).then_inc(y_free, 1)
                                        dve.sem_inc(hT_free, 1)
                n = n_exp * GT
                advance((w_free, 2 + n_exp), (w_loaded[0], 16 * n_exp), (w_loaded[1], 16 * n_exp), (h_free, NB4 + n * fc), (h_out, n * fc), (h_ready, n * fc), (y_free, 4 + 4 * n), (y_out, 4 * n), (hT_free, 2 + n))

        def experts_layer0():
            with ExitStack() as own:
                def tmp(name, shape, dt=F32):
                    return own.enter_context(sbuf(name, shape, dt))
                G = tmp("G0", [P, E8, NT])
                wr = tmp("wr0", [P, KD, E8])
                routers(wr, a["L0_ffn_router_w"])
                normalise(X, XN, True, 1e-5)
                route("first", E8, wr, tg[:, 4:5], G, capacity=max(1, int(1.25 * T / E8 * 2)))
                experts(E8, 1024, a["L0_ffn_w1"], a["L0_ffn_w2"], ACT.Gelu, G)

        def routers(wr, src):
            with ExitStack() as own:
                rows = own.enter_context(sbuf("rrows", [E8, D], F32))
                with nc.Block() as block:
                    @block.sync
                    def _(sp):
                        sp.dma_start(rows[:, :], src).then_inc(loaded, 16)

                    @block.tensor
                    def _(pe):
                        pe.wait_ge(loaded, at(loaded, 16))
                        for k in range(KD):
                            ins = nc.tensor.transpose(ps[:, 0, k * E8:(k + 1) * E8], rows[:, k * P:(k + 1) * P], ident[0:E8, 0:E8])
                        ins.then_inc(pe_out, 1)

                    @block.scalar
                    def _(act):
                        act.wait_ge(pe_out, at(pe_out, 1))
                        nc.scalar.copy(wr[:, :, :], ps[:, 0, 0:KD * E8].rearrange("p (k e) -> p k e", k=KD))
                advance((loaded, 16), (pe_out, 1))

        def rope_forms(eng, dst, src, kind):
            def swap(out_):
                eng.tensor_scalar(out_.rearrange("p n h (i two) -> p n h i two", two=2)[:, :, :, :, 0],
                                  src.rearrange("p n h (i two) -> p n h i two", two=2)[:, :, :, :, 1], -1.0, None, ALU.mult)
                return eng.tensor_copy(out_.rearrange("p n h (i two) -> p n h i two", two=2)[:, :, :, :, 1],
                                       src.rearrange("p n h (i two) -> p n h i two", two=2)[:, :, :, :, 0])
            lo, hi = dst[:, :, :, 0:HD], dst[:, :, :, HD:2 * HD]
            if kind == "stack":
                eng.tensor_copy(lo, src)
                return swap(hi)
            if kind == "same":
                eng.tensor_copy(lo, src)
                return eng.tensor_copy(hi, src)
            swap(lo)
            return swap(hi)

        def context_attention(name, gate, wq, bq, wo, bo, KB, VM, VT, mask, rows, table=None):
            ch_n = H * rows // P
            gpc = P // rows // HG
            with ExitStack() as own:
                def tmp(nm_, shape, dt=F32):
                    return own.enter_context(sbuf(name + nm_, shape, dt))
                Q = tmp("Q", [P, ch_n, P])
                PR = tmp("PR", [P, NG, L, HG])
                nm = tmp("nm", [P, NG, HG])
                PT = tmp("PT", [P, H, P])
                PTT = tmp("PTT", [TR, NG, P])
                rs = tmp("rs", [P, H])
                AO = tmp("AO", [P, H, HD])
                AOT = tmp("AOT", [P, KD, P])
                with nc.Block() as block:
                    @block.tensor
                    def _(pe):
                        def scores(i, b, g):
                            pe.wait_ge(s_free, at(s_free, i * NG + g + 1))
                            for half in range(2):
                                lo = half * L // 2
                                ins = nc.tensor.matmul(ps[:, 2 * (g % 2) + half, 0:L // 2 * HG], Q[:, g // gpc, :],
                                                       KB[:, g, bass.ds(b, 1), lo:lo + L // 2, :].rearrange("p b l h -> p (b l h)"),
                                                       start=True, stop=True)
                            ins.then_inc(scores_made, 1)

                        def turn(g, i):
                            pe.wait_ge(probs, at(probs, i * NG + g + 1))
                            pe.wait_ge(pt_ready, at(pt_ready, i * NG + g))
                            for hh in range(HG):
                                ins = nc.tensor.transpose(ps[:, 4, hh * P:(hh + 1) * P], PR[:, g, 0:P, hh], ident[:, :])
                            ins.then_inc(turned, 1)
                            if g == 0:
                                pe.wait_ge(ptt_ready, at(ptt_ready, i))
                            ins = nc.tensor.transpose(ps[0:TR, 5, g * P:(g + 1) * P], PR[:, g, P:L, :].rearrange("p l h -> p (l h)"), ident[:, :])
                            ins.then_inc(tails_turned, 1)

                        with pe.Fori(0, NT) as i:
                            b = i // TPB
                            pe.wait_ge(x_used, at(x_used, i))
                            for ch in range(ch_n):
                                for k in range(KD):
                                    ins = nc.tensor.matmul(ps[:, 7, ch * P:(ch + 1) * P], wq[:, k, ch * P:(ch + 1) * P],
                                                           XT[:, k, bass.ds(i * P, P)], start=(k == 0), stop=(k == KD - 1 and bq is None))
                                if bq is not None:
                                    ins = nc.tensor.matmul(ps[:, 7, ch * P:(ch + 1) * P], bq[0:1, ch * P:(ch + 1) * P], ones[0:1, 0:P],
                                                           start=False, stop=True)
                            ins.then_inc(q_out, 1)
                            pe.wait_ge(q_ready, at(q_ready, i + 1))
                            scores(i, b, 0)
                            scores(i, b, 1)
                            for g in range(NG):
                                turn(g, i)
                                if g + 2 < NG:
                                    scores(i, b, g + 2)
                            pe.wait_ge(pt_ready, at(pt_ready, i * NG + NG))
                            pe.wait_ge(ptt_ready, at(ptt_ready, i + 1))
                            for g in range(NG):
                                nc.tensor.matmul(ps[:, 6, g * HG * VW:(g + 1) * HG * VW], PTT[:, g, :],
                                                 VT[:, bass.ds(b, 1), g * HG:(g + 1) * HG, :].rearrange("p b h w -> p (b h w)"),
                                                 start=(g == 0), stop=False, skip_group_check=True)
                            for h in range(H):
                                ins = nc.tensor.matmul(ps[:, 6, h * VW:(h + 1) * VW], PT[:, h, :],
                                                       VM[:, bass.ds(b, 1), h, :].rearrange("p b w -> p (b w)"),
                                                       start=False, stop=True, skip_group_check=True)
                            ins.then_inc(pv, 1)
                            pe.wait_ge(ao_ready, at(ao_ready, i + 1))
                            for k in range(KD):
                                ins = nc.tensor.transpose(ps[:, 7, k * P:(k + 1) * P],
                                                          AO[:, :, :].rearrange("p h w -> p (h w)")[:, k * P:(k + 1) * P], ident[:, :])
                            ins.then_inc(ao_turned, 1)
                            pe.wait_ge(aot_ready, at(aot_ready, i + 1))
                            for k in range(KD):
                                ins = nc.tensor.matmul(ps[:, 7, D:2 * D], AOT[:, k, :], wo[:, k, :], start=(k == 0), stop=(k == KD - 1 and bo is None))
                            if bo is not None:
                                ins = nc.tensor.matmul(ps[:, 7, D:2 * D], ones[0:1, 0:P], bo[0:1, :], start=False, stop=True)
                            ins.then_inc(y_out, 1)

                    @block.vector
                    def _(dve):
                        dve.sem_inc(s_free, 2)
                        step = Steps()
                        with dve.Fori(0, NT) as i:
                            step.turn(i, 1)
                            dve.wait_ge(q_out, at(q_out, i + 1))
                            src = ps[:, 7, 0:ch_n * P].rearrange("p (c q) -> p c q", c=ch_n)
                            if table is None:
                                ins = nc.vector.tensor_copy(Q[:, :, :], src)
                            else:
                                tb = table[:, bass.ds((i % TPB) * P, P)].unsqueeze(1).broadcast_to([P, ch_n, P])
                                ins = nc.vector.tensor_tensor(Q[:, :, :], src, tb, ALU.mult)
                            ins.then_inc(q_ready, 1)
                            for g in range(NG):
                                dve.wait_ge(scores_made, at(scores_made, i * NG + g + 1))
                                mrow = mask(i)
                                for half in range(2):
                                    lo = half * L // 2
                                    ins = nc.vector.tensor_tensor(PR[:, g, lo:lo + L // 2, :],
                                                                  ps[:, 2 * (g % 2) + half, 0:L // 2 * HG].rearrange("p (l h) -> p l h", h=HG),
                                                                  mrow[:, lo:lo + L // 2].unsqueeze(2).broadcast_to([P, L // 2, HG]), ALU.add)
                                ins.then_inc(s_free, 1)
                                dve.wait_ge(s_free, at(s_free, i * NG + g + 1 + 2))
                                nc.vector.tensor_reduce(nm[:, g, :], PR[:, g, :, :].rearrange("p l h -> p h l"), AX_X, ALU.max, negate=True).then_inc(max_ready, 1)
                            dve.wait_ge(tails_turned, at(tails_turned, i * NG + NG))
                            nc.vector.tensor_copy(PTT[:, :, :], ps[0:TR, 5, :].rearrange("p (g q) -> p g q", g=NG)).then_inc(ptt_ready, 1)
                            dve.wait_ge(pv, at(pv, i + 1))
                            o = ps[:, 6, 0:H * VW].rearrange("p (h w) -> p h w", h=H)
                            nc.vector.reciprocal(rs[:, :], o[:, :, HD]).then_inc(dve_step, 1)
                            dve.wait_ge(dve_step, at(dve_step, step.next()))
                            nc.vector.tensor_tensor(AO[:, :, :], o[:, :, 0:HD], rs[:, :].unsqueeze(2).broadcast_to([P, H, HD]), ALU.mult).then_inc(ao_ready, 1)
                            dve.wait_ge(y_out, at(y_out, i + 1))
                            x = X[:, bass.ds(i, 1), :].rearrange("p c d -> p (c d)")
                            nc.vector.scalar_tensor_tensor(x, ps[:, 7, D:2 * D], gate, x, ALU.mult, ALU.add).then_inc(x_used, 1)
                        step.end(NT)
                        advance((dve_step, step.total))

                    @block.scalar
                    def _(act):
                        with act.Fori(0, NT) as i:
                            def exps(g):
                                act.wait_ge(max_ready, at(max_ready, i * NG + g + 1))
                                for hh in range(HG):
                                    ins = nc.scalar.activation(PR[:, g, :, hh], PR[:, g, :, hh], ACT.Exp, bias=nm[:, g, hh:hh + 1])
                                ins.then_inc(probs, 1)

                            def copied(g):
                                act.wait_ge(turned, at(turned, i * NG + g + 1))
                                if g == 0:
                                    act.wait_ge(pv, at(pv, i))
                                nc.scalar.copy(PT[:, g * HG:(g + 1) * HG, :], ps[:, 4, :].rearrange("p (h q) -> p h q", h=HG)).then_inc(pt_ready, 1)

                            exps(0)
                            exps(1)
                            copied(0)
                            exps(2)
                            copied(1)
                            exps(3)
                            copied(2)
                            copied(3)
                            act.wait_ge(ao_turned, at(ao_turned, i + 1))
                            nc.scalar.copy(AOT[:, :, :], ps[:, 7, 0:D].rearrange("p (k q) -> p k q", k=KD)).then_inc(aot_ready, 1)
                advance((s_free, 2 + NT * NG), (scores_made, NT * NG), (probs, NT * NG), (pt_ready, NT * NG), (turned, NT * NG), (tails_turned, NT * NG), (ptt_ready, NT), (x_used, NT), (q_out, NT), (q_ready, NT), (pv, NT), (ao_ready, NT), (ao_turned, NT), (aot_ready, NT), (y_out, NT), (max_ready, NT * NG))

        def attention1():
            with ExitStack() as own:
                def tmp(name, shape, dt=F32):
                    return own.enter_context(sbuf(name, shape, dt))
                wqs = tmp("a1wqs", [P, KD, 2 * D])
                wo = tmp("a1wo", [P, KD, D])
                rowb = tmp("a1rowb", [1, 3, 2 * D])
                bo = tmp("a1bo", [1, D])
                KB = tmp("a1KB", [P, NG, B, L, HG])
                VM = tmp("a1VM", [P, B, H, VW])
                VT = tmp("a1VT", [TR, B, H, VW])
                mb = tmp("a1mask", [P, B, L])
                tq = tmp("a1tq", [P, S])
                with ExitStack() as own2:
                    def tmp2(name, shape, dt=F32):
                        return own2.enter_context(sbuf(name, shape, dt))
                    wq = tmp2("a1wq", [P, KD, D])
                    wkv = tmp2("a1wkv", [P, KD, 2 * D])
                    wv = tmp2("a1wv", [P, KD, D])
                    wkA = tmp2("a1wkA", [P, KD, 2 * D])
                    wkB = tmp2("a1wkB", [P, KD, 2 * D])
                    bq = tmp2("a1bq", [1, D])
                    bkv = tmp2("a1bkv", [1, 2 * D])
                    bv = tmp2("a1bv", [1, D])
                    m8 = tmp2("a1m8", [1, B * L], U8)
                    mf = tmp2("a1mf", [1, B * L])
                    cosk = tmp2("a1cos", [P, L])
                    sink = tmp2("a1sin", [P, L])
                    kr = tmp2("a1kr", [P, 2, B, L])
                    load_weights([
                        (wq[:, :, :], a["L1_xattn_Wq"].rearrange("(k p) d -> p k d", p=P)),
                        (wkv[:, :, :], a["L1_xattn_Wkv"].rearrange("(k p) d -> p k d", p=P)),
                        (wo[:, :, :], a["L1_xattn_Wo"].rearrange("(k p) d -> p k d", p=P)),
                        (bq[:, :], a["L1_xattn_bq"]), (bkv[:, :], a["L1_xattn_bkv"]), (bo[:, :], a["L1_xattn_bo"]),
                        (m8[:, :], a["ctx_mask"]), (cosk[:, :], a["cos1k"]), (sink[:, :], a["sin1k"]), (tq[:, :], a["stack1q"])])
                    with nc.Block() as block:
                        @block.vector
                        def _(dve):
                            def h4(t, p=P):
                                return t.rearrange("p n (h w) -> p n h w", h=H)
                            q1 = bq[:, :].unsqueeze(1)
                            k1 = bkv[:, 0:D].unsqueeze(1)
                            rope_forms(nc.vector, h4(wqs[:, :, :]), h4(wq[:, :, :]), "stack")
                            rope_forms(nc.vector, h4(wkA[:, :, :]), h4(wkv[:, :, 0:D]), "same")
                            rope_forms(nc.vector, h4(wkB[:, :, :]), h4(wkv[:, :, 0:D]), "swap")
                            rope_forms(nc.vector, h4(rowb[:, 0:1, :]), h4(q1), "stack")
                            rope_forms(nc.vector, h4(rowb[:, 1:2, :]), h4(k1), "same")
                            rope_forms(nc.vector, h4(rowb[:, 2:3, :]), h4(k1), "swap")
                            nc.vector.tensor_copy(wv[:, :, :], wkv[:, :, D:2 * D])
                            nc.vector.tensor_copy(bv[:, :], bkv[:, D:2 * D])
                            nc.vector.tensor_copy(mf[:, :], m8[:, :]).then_inc(cst, 1)
                            dve.wait_ge(cst, at(cst, 1))
                            nc.vector.tensor_scalar(mf[:, :], mf[:, :], -1.0, None, ALU.add).then_inc(cst, 1)
                            dve.wait_ge(pe_out, at(pe_out, 1))
                            nc.vector.tensor_scalar(mb[:, :, :], ps[:, 0, 0:B * L].rearrange("p (b l) -> p b l", b=B), 3e38, 10.0, ALU.mult, ALU.mult)

                        @block.tensor
                        def _(pe):
                            pe.wait_ge(cst, at(cst, 2))
                            nc.tensor.matmul(ps[:, 0, 0:B * L], ones[0:1, 0:P], mf[:, :], start=True, stop=True).then_inc(pe_out, 1)
                    advance((cst, 2), (pe_out, 1))
                    keys_values(KB, VM, VT, HG, hm4, 64 ** -0.5, wkA, wv, wkB, rowb[:, 1, :], rowb[:, 2, :], bv, cosk, sink, kr)
                normalise(X, XN, True, 1e-5)
                context_attention("a1", tg[:, 1:2], wqs, rowb[:, 0, :], wo, bo, KB, VM, VT,
                                  lambda i: mb[:, bass.ds(i // TPB, 1), :].rearrange("p b l -> p (b l)"), 32, tq)

        def attention3():
            with ExitStack() as own:
                def tmp(name, shape, dt=F32):
                    return own.enter_context(sbuf(name, shape, dt))
                w = [tmp(f"a3w{i}", [P, KD, D]) for i in range(4)]
                bias = [tmp(f"a3b{i}", [1, D]) for i in range(4)]
                KB = tmp("a3KB", [P, NG, B, L, HG])
                VM = tmp("a3VM", [P, B, H, VW])
                VT = tmp("a3VT", [TR, B, H, VW])
                m8 = tmp("a3m8", [P, NT, L], U8)
                mb = tmp("a3mask", [P, NT, L])
                load_weights([(w[i][:, :, :], a[f"L3_xattn_W{c}"].rearrange("(k p) d -> p k d", p=P)) for i, c in enumerate("qkvo")]
                             + [(bias[i][:, :], a[f"L3_xattn_b{c}"]) for i, c in enumerate("qkvo")]
                             + [(m8[:, :, :], a["q_mask"].rearrange("(t p) l -> p t l", p=P))])
                with nc.Block() as block:
                    @block.vector
                    def _(dve):
                        nc.vector.tensor_scalar(mb[:, :, :], m8[:, :, :], -1e15, None, ALU.mult)
                keys_values(KB, VM, VT, 8, hm8, HD ** -0.5, w[1], w[2], bkA=bias[1], bv=bias[2])
                normalise(X, XN, True, 1e-5)
                context_attention("a3", tg[:, 3:4], w[0], bias[0], w[3], bias[3], KB, VM, VT,
                                  lambda i: mb[:, bass.ds(i, 1), :].rearrange("p b l -> p (b l)"), 16)

        def block1():
            with ExitStack() as own:
                def tmp(name, shape, dt=F32):
                    return own.enter_context(sbuf(name, shape, dt))
                Z = XN
                gc = tmp("f1gc", [P, 2, KD])
                G = tmp("G1", [P, E8, NT])
                wr = tmp("wr1", [P, KD, E8])
                with ExitStack() as own2:
                    def tmp2(name, shape, dt=F32):
                        return own2.enter_context(sbuf(name, shape, dt))
                    scratch = tmp2("f1n", [P, NT, D])
                    grows = tmp2("f1g", [1, 2, D])
                    load_weights([(grows[:, 0, :], a["L1_ffn_g1"]), (grows[:, 1, :], a["L1_ffn_g2"]),
                                  (wr[:, :, :], a["L1_ffn_w_router"].rearrange("(k p) e -> p k e", p=P))])
                    with nc.Block() as block:
                        @block.tensor
                        def _(pe):
                            for i in range(2):
                                for k in range(KD):
                                    ins = nc.tensor.matmul(ps[:, 0, 2 * i + k:2 * i + k + 1], grows[:, i, k * P:(k + 1) * P], ones[0:1, 0:1],
                                                           start=True, stop=True)
                            ins.then_inc(pe_out, 1)

                        @block.scalar
                        def _(act):
                            act.wait_ge(pe_out, at(pe_out, 1))
                            nc.scalar.copy(gc[:, :, :], ps[:, 0, 0:4].rearrange("p (i k) -> p i k", i=2))
                    advance((pe_out, 1))
                    normalise(X, Z, True, 1e-5)
                    normalise(Z, scratch, False, 1e-6, gcol=gc[:, 0, :])
                self_attention(Z)
                with ExitStack() as own2:
                    scratch = own2.enter_context(sbuf("f1n2", [P, NT, D], F32))
                    normalise(Z, scratch, False, 1e-6, gcol=gc[:, 1, :])
                route("best", E8, wr, tg[:, 5:6], G, capacity=-(-2 * 512 * 2 * 5 // (4 * E8)))
                with nc.Block() as block:
                    @block.vector
                    def _(dve):
                        for c in range(NT):
                            nc.vector.scalar_tensor_tensor(X[:, c, :], Z[:, c, :], tg[:, 5:6], X[:, c, :], ALU.mult, ALU.add)
                experts(E8, 512, a["L1_ffn_w1"], a["L1_ffn_w2"], ACT.Relu, G)

        def self_attention(Z):
            with ExitStack() as own:
                def tmp(name, shape, dt=F32):
                    return own.enter_context(sbuf("s_" + name, shape, dt))
                wqs = tmp("wqs", [P, KD, 2 * D])
                wo = tmp("wo", [P, KD, D])
                tq = tmp("tq", [P, S])
                causal = tmp("causal", [P, P])
                KT = tmp("KT", [P, 4, T])
                V = tmp("V", [P, NT, H, VW])
                with ExitStack() as own2:
                    def tmp2(name, shape, dt=F32):
                        return own2.enter_context(sbuf("s_" + name, shape, dt))
                    w = tmp2("w", [P, KD, 3 * D])
                    wkA = tmp2("wkA", [P, KD, 2 * D])
                    wkB = tmp2("wkB", [P, KD, 2 * D])
                    cosk = tmp2("cos", [P, S])
                    sink = tmp2("sin", [P, S])
                    kr = tmp2("kr", [P, 2, 512])
                    load_weights([(w[:, :, :], a["L1_ffn_w_qkv"].rearrange("(k p) d -> p k d", p=P)),
                                  (wo[:, :, :], a["L1_ffn_w_o"].rearrange("(k p) d -> p k d", p=P)),
                                  (tq[:, :], a["stack2"]), (cosk[:, :], a["cos2"]), (sink[:, :], a["sin2"]),
                                  (causal[:, :], a["causal"])])
                    with nc.Block() as block:
                        @block.vector
                        def _(dve):
                            def h4(t):
                                return t.rearrange("p n (h w) -> p n h w", h=H)
                            rope_forms(nc.vector, h4(wqs[:, :, :]), h4(w[:, :, 0:D]), "stack")
                            rope_forms(nc.vector, h4(wkA[:, :, :]), h4(w[:, :, D:2 * D]), "same")
                            rope_forms(nc.vector, h4(wkB[:, :, :]), h4(w[:, :, D:2 * D]), "swap").then_inc(cst, 1)
                            dve.wait_ge(cst, at(cst, 1))
                            nc.vector.tensor_scalar(wqs[:, :, :], wqs[:, :, :], HD ** -0.5, None, ALU.mult)
                            nc.vector.memset(V[:, :, :, HD:VW], 1.0)
                    advance((cst, 1))
                    with nc.Block() as block:
                        @block.tensor
                        def _(pe):
                            for n in range(16):
                                ch, t = n // 4, n % 4
                                if n >= 2:
                                    pe.wait_ge(evac, at(evac, n - 1))
                                for bank, wk in ((n % 2, wkA), (2 + n % 2, wkB)):
                                    for k in range(KD):
                                        ins = nc.tensor.matmul(ps[:, bank, :], wk[:, k, ch * P:(ch + 1) * P], XT[:, k, t * 512:(t + 1) * 512],
                                                               start=(k == 0), stop=(k == KD - 1))
                                ins.then_inc(pe_out, 1)
                            for c in range(NT):
                                if c >= 4:
                                    pe.wait_ge(v_ready, at(v_ready, c - 3))
                                for k in range(KD):
                                    ins = nc.tensor.matmul(ps[:, 4 + c % 4, 0:D], XT[:, k, c * P:(c + 1) * P], w[:, k, 2 * D:3 * D],
                                                           start=(k == 0), stop=(k == KD - 1))
                                ins.then_inc(v_out, 1)

                        @block.vector
                        def _(dve):
                            step = Steps()
                            for n in range(16):
                                ch, t = n // 4, n % 4
                                dve.wait_ge(pe_out, at(pe_out, n + 1))
                                pos = slice((t % 2) * 512, (t % 2) * 512 + 512)
                                nc.vector.tensor_tensor(kr[:, 0, :], ps[:, n % 2, :], cosk[:, pos], ALU.mult)
                                ins = nc.vector.tensor_tensor(kr[:, 1, :], ps[:, 2 + n % 2, :], sink[:, pos], ALU.mult)
                                ins.then_inc(evac, 1)
                                dve.wait_ge(evac, at(evac, n + 1))
                                nc.vector.tensor_tensor(KT[:, ch, t * 512:(t + 1) * 512], kr[:, 0, :], kr[:, 1, :], ALU.add).then_inc(dve_step, 1)
                                dve.wait_ge(dve_step, at(dve_step, step.next()))
                            advance((dve_step, step.total))

                        @block.scalar
                        def _(act):
                            for c in range(NT):
                                act.wait_ge(v_out, at(v_out, c + 1))
                                nc.scalar.copy(V[:, c, :, 0:HD], ps[:, 4 + c % 4, 0:D].rearrange("p (h w) -> p h w", h=H)).then_inc(v_ready, 1)
                    advance((pe_out, 16), (evac, 16), (v_out, NT), (v_ready, NT))

                Q = tmp("Q", [P, 4, 4, P])
                PR = tmp("PR", [P, 2, S])
                PT = tmp("PT", [P, 2, TPB, P])
                nm = tmp("nm", [P, 2])
                rs = tmp("rs", [P, H])
                AO = tmp("AO", [P, H, HD])
                AOT = tmp("AOT", [P, KD, P])
                for j in range(TPB):
                    nk = j + 1
                    n_piece = -(-nk // 4)
                    with nc.Block() as block:
                        @block.tensor
                        def _(pe):
                            def scores(i, h):
                                if h >= 2:
                                    pe.wait_ge(probs, at(probs, i * H + h - 1))
                                for half in range(0, nk * P, 512):
                                    n = min(512, nk * P - half)
                                    ins = nc.tensor.matmul(ps[:, 2 * (h % 2) + half // 512, 0:n], Q[:, h // 4, h % 4, :],
                                                           KT[:, h // 4, bass.ds(i * S + half, n)], start=True, stop=True)
                                ins.then_inc(scores_made, 1)

                            def turn(i, h):
                                pe.wait_ge(probs, at(probs, i * H + h + 1))
                                for q in range(n_piece):
                                    piece = h * n_piece + q
                                    if piece >= 2:
                                        pe.wait_ge(pt_ready, at(pt_ready, i * H * n_piece + piece - 1))
                                    for t in range(4 * q, min(4 * q + 4, nk)):
                                        ins = nc.tensor.transpose(ps[:, 4 + piece % 2, (t % 4) * P:(t % 4 + 1) * P],
                                                                  PR[:, h % 2, t * P:(t + 1) * P], ident[:, :])
                                    ins.then_inc(turned, 1)

                            def values(i, h):
                                pe.wait_ge(pt_ready, at(pt_ready, i * H * n_piece + (h + 1) * n_piece))
                                for t in range(nk):
                                    ins = nc.tensor.matmul(ps[:, 6, h * VW:(h + 1) * VW], PT[:, h % 2, t, :],
                                                           V[:, bass.ds(i * TPB + t, 1), h, :].rearrange("p b w -> p (b w)"),
                                                           start=(t == 0), stop=(t == nk - 1))
                                ins.then_inc(pv, 1)

                            with pe.Fori(0, B) as i:
                                pe.wait_ge(x_used, at(x_used, i))
                                for ch in range(4):
                                    for k in range(KD):
                                        ins = nc.tensor.matmul(ps[:, 7, ch * P:(ch + 1) * P], wqs[:, k, ch * P:(ch + 1) * P],
                                                               XT[:, k, bass.ds(i * S + j * P, P)], start=(k == 0), stop=(k == KD - 1))
                                ins.then_inc(q_out, 1)
                                pe.wait_ge(q_ready, at(q_ready, i + 1))
                                scores(i, 0)
                                for h in range(H):
                                    if h + 1 < H:
                                        scores(i, h + 1)
                                    turn(i, h)
                                    if h >= 1:
                                        values(i, h - 1)
                                values(i, H - 1)
                                pe.wait_ge(ao_ready, at(ao_ready, i + 1))
                                for k in range(KD):
                                    ins = nc.tensor.transpose(ps[:, 7, k * P:(k + 1) * P],
                                                              AO[:, :, :].rearrange("p h w -> p (h w)")[:, k * P:(k + 1) * P], ident[:, :])
                                ins.then_inc(ao_turned, 1)
                                pe.wait_ge(aot_ready, at(aot_ready, i + 1))
                                for k in range(KD):
                                    ins = nc.tensor.matmul(ps[:, 7, D:2 * D], AOT[:, k, :], wo[:, k, :], start=(k == 0), stop=(k == KD - 1))
                                ins.then_inc(y_out, 1)

                        @block.vector
                        def _(dve):
                            step = Steps()
                            with dve.Fori(0, B) as i:
                                step.turn(i, H + 1)
                                dve.wait_ge(q_out, at(q_out, i + 1))
                                tb = tq[:, j * P:(j + 1) * P].unsqueeze(1).broadcast_to([P, 4, P])
                                for hh in range(4):
                                    ins = nc.vector.scalar_tensor_tensor(Q[:, :, hh, :], ps[:, 7, :].rearrange("p (c q) -> p c q", c=4),
                                                                         hm4[:, hh:hh + 1], tb, ALU.mult, ALU.mult)
                                ins.then_inc(q_ready, 1)

                                def copied(h):
                                    for q in range(n_piece):
                                        piece = h * n_piece + q
                                        n = min(4, nk - 4 * q)
                                        dve.wait_ge(turned, at(turned, i * H * n_piece + piece + 1))
                                        if q == 0 and h >= 2:
                                            dve.wait_ge(pv, at(pv, i * H + h - 1))
                                        nc.vector.tensor_copy(PT[:, h % 2, 4 * q:4 * q + n, :],
                                                                  ps[:, 4 + piece % 2, 0:n * P].rearrange("p (t q) -> p t q", t=n)).then_inc(pt_ready, 1)

                                for h in range(H):
                                    dve.wait_ge(scores_made, at(scores_made, i * H + h + 1))
                                    last = ps[:, 2 * (h % 2) + j // 4, (j % 4) * P:(j % 4 + 1) * P]
                                    nc.vector.tensor_tensor(last, last, causal[:, :], ALU.add).then_inc(dve_step, 1)
                                    dve.wait_ge(dve_step, at(dve_step, step.next()))
                                    src = (ps[:, 2 * (h % 2):2 * (h % 2) + 2, :].rearrange("p n q -> p (n q)"))[:, 0:nk * P]
                                    nc.vector.tensor_reduce(nm[:, h % 2:h % 2 + 1], src, AX_X, ALU.max, negate=True).then_inc(max_ready, 1)
                                    if h >= 1:
                                        copied(h - 1)
                                copied(H - 1)
                                dve.wait_ge(pv, at(pv, i * H + H))
                                o = ps[:, 6, 0:H * VW].rearrange("p (h w) -> p h w", h=H)
                                nc.vector.reciprocal(rs[:, :], o[:, :, HD]).then_inc(dve_step, 1)
                                dve.wait_ge(dve_step, at(dve_step, step.next()))
                                nc.vector.tensor_tensor(AO[:, :, :], o[:, :, 0:HD], rs[:, :].unsqueeze(2).broadcast_to([P, H, HD]), ALU.mult).then_inc(ao_ready, 1)
                                dve.wait_ge(y_out, at(y_out, i + 1))
                                z = Z[:, bass.ds(i * TPB + j, 1), :].rearrange("p c d -> p (c d)")
                                nc.vector.tensor_tensor(z, ps[:, 7, D:2 * D], z, ALU.add).then_inc(x_used, 1)
                            step.end(B)
                            advance((dve_step, step.total))

                        @block.scalar
                        def _(act):
                            with act.Fori(0, B) as i:
                                for h in range(H):
                                    act.wait_ge(max_ready, at(max_ready, i * H + h + 1))
                                    if h >= 2:
                                        act.wait_ge(turned, at(turned, i * H * n_piece + (h - 1) * n_piece))
                                    src = (ps[:, 2 * (h % 2):2 * (h % 2) + 2, :].rearrange("p n q -> p (n q)"))[:, 0:nk * P]
                                    nc.scalar.activation(PR[:, h % 2, 0:nk * P], src, ACT.Exp, bias=nm[:, h % 2:h % 2 + 1]).then_inc(probs, 1)
                                act.wait_ge(ao_turned, at(ao_turned, i + 1))
                                nc.scalar.copy(AOT[:, :, :], ps[:, 7, 0:D].rearrange("p (k q) -> p k q", k=KD)).then_inc(aot_ready, 1)
                    advance((scores_made, B * H), (probs, B * H), (turned, B * H * n_piece), (pt_ready, B * H * n_piece), (pv, B * H), (x_used, B), (q_out, B), (q_ready, B), (ao_ready, B), (ao_turned, B), (aot_ready, B), (y_out, B), (max_ready, B * H))

        def experts_layer2():
            with ExitStack() as own:
                G = own.enter_context(sbuf("G2", [P, E8, NT], F32))
                wr = own.enter_context(sbuf("wr2", [P, KD, E8], F32))
                routers(wr, a["L2_ffn_router_w"])
                normalise(X, XN, True, 1e-5)
                route("top2", E8, wr, tg[:, 6:7], G)
                experts(E8, 1024, a["L2_ffn_w1"], a["L2_ffn_w2"], ACT.Gelu, G)

        def experts_layer3():
            E4, FF = 4, 1024
            with ExitStack() as own:
                def tmp(name, shape, dt=F32):
                    return own.enter_context(sbuf(name, shape, dt))
                G = tmp("G3", [P, E4, NT])
                wr = tmp("wr3", [P, KD, E4])
                bg = tmp("bg3", [1, E4])
                b1r = tmp("b1r3", [E4 * FF // P, P])
                b1 = tmp("b13", [P, E4 * FF // P])
                b2 = tmp("b23", [1, E4 * D])
                load_weights([(wr[:, :, :], a["L3_ffn_Wg"].rearrange("(k p) e -> p k e", p=P)), (bg[:, :], a["L3_ffn_bg"]),
                              (b1r[:, :], a["L3_ffn_b1"].rearrange("e (f p) -> (e f) p", p=P)),
                              (b2[:, :], a["L3_ffn_b2"].rearrange("(o e) d -> o (e d)", o=1))])
                with nc.Block() as block:
                    @block.tensor
                    def _(pe):
                        n = E4 * FF // P
                        nc.tensor.transpose(ps[:, 0, 0:n], b1r[:, :], ident[0:n, 0:n]).then_inc(pe_out, 1)

                    @block.scalar
                    def _(act):
                        act.wait_ge(pe_out, at(pe_out, 1))
                        nc.scalar.copy(b1[:, :], ps[:, 0, 0:E4 * FF // P])
                advance((pe_out, 1))
                normalise(X, XN, True, 1e-5)
                route("top1", E4, wr, tg[:, 7:8], G, bias=bg)
                experts(E4, FF, a["L3_ffn_W1"], a["L3_ffn_W2"], ACT.Gelu, G, b1, b2)

        def alignment():
            NC = 16
            W = S // NC
            NSTEP = L + NC - 1
            NF = -(-NSTEP // 4) * 4
            LN = 32 * B
            down = [max(l - 1, 0) for l in range(32)]
            up = [min(l + 1, 31) for l in range(32)]
            cost_d, path_d = a["dtw_cost"], a["dtw_path"]
            with ExitStack() as own:
                def tmp(name, shape, dt=F32):
                    return own.enter_context(sbuf("t_" + name, shape, dt))
                CD = tmp("CD", [LN, NF, W])
                NL = tmp("NL", [LN, NF, W + 1])
                CC = tmp("CC", [LN, NF, W])
                R = tmp("R", [LN, 4, W + 1])
                M = tmp("M", [LN, 4, W])
                PA = tmp("PA", [LN, NF, 2])
                V = tmp("V", [LN, 2, W + 2])
                seed = tmp("seed", [LN, W])
                hv = tmp("hv", [LN, 2])
                normalise(X, XN, True, 1e-5)
                SQ = XN[:, :, :].rearrange("p c d -> p (c d)").rearrange("p (k t) -> p k t", k=KD)
                with ExitStack() as own2:
                    def tmp2(name, shape, dt=F32):
                        return own2.enter_context(sbuf("t_" + name, shape, dt))
                    C2 = tmp2("C2", [P, KD, B, L])
                    DD = tmp2("DD", [P, 4, 512])
                    aa = tmp2("aa", [P, 2 * B])
                    with nc.Block() as block:
                        outs = [(b, r, n) for b in range(B) for r in range(2) for n in range(2)]

                        @block.scalar
                        def _(act):
                            for k in range(KD):
                                ins = nc.scalar.activation(SQ[:, k, :], XT[:, k, :], ACT.Square)
                            ins.then_inc(squares, 1)
                            for b in range(B):
                                nc.scalar.activation(DD[:, b, 0:D], CR[:, b, :], ACT.Square, accum_out=aa[:, b:b + 1])
                                ins = nc.scalar.activation(DD[0:TAIL, B + b, 0:D], CRT[:, b, :], ACT.Square, accum_out=aa[0:TAIL, B + b:B + b + 1])
                            ins.then_inc(norms, 1)
                            for m, (b, r, n) in enumerate(outs):
                                rows = TAIL if r else P
                                act.wait_ge(dist2, at(dist2, m + 1))
                                nc.scalar.activation(DD[0:rows, m % 4, :], DD[0:rows, m % 4, :], ACT.Sqrt).then_inc(dist, 1)

                        @block.tensor
                        def _(pe):
                            pe.wait_ge(squares, at(squares, 1))
                            pe.wait_ge(cst, at(cst, 1))
                            for m, (b, r, n) in enumerate(outs):
                                rows, lo, hi = (TAIL, P, L) if r else (P, 0, P)
                                for k in range(KD):
                                    cols = slice(b * S + n * 512, b * S + (n + 1) * 512)
                                    nc.tensor.matmul(ps[0:rows, m, :], C2[:, k, b, lo:hi], XT[:, k, cols], start=(k == 0), stop=False)
                                    ins = nc.tensor.matmul(ps[0:rows, m, :], ones[:, 0:rows], SQ[:, k, cols], start=False, stop=(k == KD - 1))
                                ins.then_inc(pe_out, 1)

                        @block.vector
                        def _(dve):
                            nc.vector.tensor_scalar(C2[:, :, :, :], CT[:, :, :, :], -2.0, None, ALU.mult).then_inc(cst, 1)
                            nc.vector.memset(CD[:, :, :], 0.0).then_inc(cleared, 1)
                            nc.vector.memset(NL[:, :, 0:1], 0.0)
                            dve.wait_ge(norms, at(norms, 1))
                            for m, (b, r, n) in enumerate(outs):
                                rows = TAIL if r else P
                                dve.wait_ge(pe_out, at(pe_out, m + 1))
                                if m >= 4:
                                    dve.wait_ge(dist_stored, at(dist_stored, 16 * (m - 3)))
                                nc.vector.tensor_scalar(DD[0:rows, m % 4, :], ps[0:rows, m, :], aa[0:rows, r * B + b:r * B + b + 1], 0.0,
                                                            ALU.add, ALU.max).then_inc(dist2, 1)

                        @block.sync
                        def _(sp):
                            for m, (b, r, n) in enumerate(outs):
                                rows, lo, hi = (TAIL, P, L) if r else (P, 0, P)
                                sp.wait_ge(dist, at(dist, m + 1))
                                sp.dma_start(cost_d[b * L + lo:b * L + hi, n * 512:(n + 1) * 512], DD[0:rows, m % 4, :]).then_inc(dist_stored, 16)
                                sp.wait_ge(dist_stored, at(dist_stored, 16 * (m + 1)))
                            sp.wait_ge(cleared, at(cleared, 1))
                            for b in range(B):
                                for k in range(NC):
                                    lane = 32 * b + 1 + k
                                    sp.dma_start(CD[lane:lane + 1, k:k + L, :],
                                                     cost_d[b * L:(b + 1) * L, k * W:(k + 1) * W].rearrange("(o i) w -> o i w", o=1)).then_inc(skewed, 16)
                            sp.dma_start(R[:, 3, :], a["dtw_start"]).then_inc(skewed, 16)
                            sp.dma_start(seed[:, :], a["dtw_end"]).then_inc(skewed, 16)
                            sp.wait_ge(skewed, at(skewed, 16 * (B * NC + 2)))
                    advance((squares, 1), (norms, 1), (dist2, 8), (dist, 8), (pe_out, 8), (cst, 1), (cleared, 1), (dist_stored, 16 * 8), (skewed, 16 * (B * NC + 2)))

                with nc.Block() as block:
                    @block.vector
                    def _(dve):
                        dve.sem_inc(row_free, 3)
                        step = Steps()
                        with dve.Fori(0, NF // 4) as t:
                            step.turn(t, 4)
                            for q in range(4):
                                prev = (q + 3) % 4
                                dve.wait_ge(row_free, at(row_free, t * 4 + q + 1))
                                nc.vector.tensor_tensor(M[:, q, :], R[:, prev, 0:W], R[:, prev, 1:W + 1], ALU.min)
                                nc.vector.stream_shuffle(R[:, q, 0:1], R[:, prev, W:W + 1], down).then_inc(dve_step, 1)
                                dve.wait_ge(dve_step, at(dve_step, step.next()))
                                nc.vector.tensor_tensor_scan(R[:, q, 1:W + 1], M[:, q, :],
                                                                 CD[:, bass.ds(t * 4 + q, 1), :].rearrange("p s w -> p (s w)"),
                                                                 R[:, q, 0:1], ALU.min, ALU.add).then_inc(row_made, 1)
                                dve.wait_ge(row_made, at(row_made, t * 4 + q + 1))
                        step.end(NF // 4)
                        dve.wait_ge(row_free, at(row_free, 3 + NF))
                        nc.vector.tensor_scalar(NL[:, :, 1:W + 1], NL[:, :, 1:W + 1], 0.0, None, ALU.is_ge)
                        nc.vector.tensor_scalar(CC[:, :, :], CC[:, :, :], 0.0, 2.0, ALU.is_gt, ALU.mult).then_inc(dve_step, 1)
                        dve.wait_ge(dve_step, at(dve_step, step.next()))
                        nc.vector.scalar_tensor_tensor(CC[:, :, :], CC[:, :, :], -1.0, NL[:, :, 1:W + 1], ALU.add, ALU.mult).then_inc(dve_step, 1)
                        dve.wait_ge(dve_step, at(dve_step, step.next()))
                        nc.vector.tensor_copy(PA[:, :, 1:2], CC[:, :, W - 1:W])
                        nc.vector.tensor_scalar(PA[:, :, 0:1], NL[:, :, W:W + 1], -1.0, 1.0, ALU.mult, ALU.add)
                        nc.vector.memset(V[:, :, :], 0.0).then_inc(dve_step, 1)
                        dve.wait_ge(dve_step, at(dve_step, step.next()))

                        def back(s, now):
                            p = CD[:, bass.ds(s, 1), :].rearrange("p s w -> p (s w)")
                            nl = NL[:, bass.ds(s, 1), :].rearrange("p s w -> p (s w)")
                            c = CC[:, bass.ds(s, 1), :].rearrange("p s w -> p (s w)")
                            pa = PA[:, bass.ds(s, 1), :].rearrange("p s w -> p (s w)")
                            nc.vector.tensor_tensor_scan(p, nl[:, 0:W], seed[:, :], V[:, now, 0:1],
                                                              ALU.is_lt, ALU.max).then_inc(dve_step, 1)
                            dve.wait_ge(dve_step, at(dve_step, step.next()))
                            nc.vector.tensor_scalar(hv[:, :], pa, p[:, W - 1:W], None, ALU.mult)
                            nc.vector.tensor_tensor(V[:, now, 2:W + 2], p, c, ALU.mult).then_inc(dve_step, 1)
                            dve.wait_ge(dve_step, at(dve_step, step.next()))
                            nc.vector.scalar_tensor_tensor(seed[:, :], V[:, now, 1:W + 1], -1.0, V[:, now, 2:W + 2], ALU.mult, ALU.max)
                            nc.vector.stream_shuffle(V[:, 1 - now, 0:2], hv[:, :], up).then_inc(dve_step, 1)
                            dve.wait_ge(dve_step, at(dve_step, step.next()))

                        back(NSTEP - 1, 1)
                        n = (NSTEP - 1) // 4
                        with dve.Fori(0, n) as t:
                            step.turn(t, 12)
                            for q in range(4):
                                back((n - 1 - t) * 4 + 3 - q, q % 2)
                        step.end(n)
                        advance((dve_step, step.total))

                    @block.gpsimd
                    def _(pool):
                        with pool.Fori(0, NF // 4) as t:
                            for q in range(4):
                                prev = (q + 3) % 4
                                pool.wait_ge(row_made, at(row_made, t * 4 + q + 1))
                                nc.gpsimd.tensor_tensor(NL[:, bass.ds(t * 4 + q, 1), 1:W + 1].rearrange("p s w -> p (s w)"),
                                                        R[:, q, 0:W][:, ::-1], M[:, q, :][:, ::-1], ALU.subtract)
                                nc.gpsimd.tensor_tensor(CC[:, bass.ds(t * 4 + q, 1), :].rearrange("p s w -> p (s w)"),
                                                            R[:, prev, 0:W][:, ::-1], R[:, prev, 1:W + 1][:, ::-1], ALU.subtract).then_inc(row_free, 1)
                advance((row_free, 3 + NF), (row_made, NF))

                RAWT = XN[0:TAIL, 0:8, :].rearrange("p c d -> p (c d)")
                TAILP = XN[0:TAIL, 8:16, :].rearrange("p c d -> p (c d)")
                with nc.Block() as block:
                    @block.sync
                    def _(sp):
                        for b in range(B):
                            for k in range(NC):
                                lane = 32 * b + 1 + k
                                sp.dma_start(path_d[b * L:(b + 1) * L, k * W:(k + 1) * W].rearrange("(o i) w -> o i w", o=1),
                                                 CD[lane:lane + 1, k:k + L, :]).then_inc(path_stored, 16)
                        sp.wait_ge(path_stored, at(path_stored, 16 * B * NC))
                        src = path_d.rearrange("(b i) t -> i b t", b=B)
                        sp.dma_start(XT[:, 0, :].rearrange("p (b t) -> p b t", b=B), src[0:P]).then_inc(loaded, 16)
                        sp.dma_start(RAWT.rearrange("p (b t) -> p b t", b=B), src[P:L]).then_inc(loaded, 16)

                    @block.tensor
                    def _(pe):
                        pe.wait_ge(turned, at(turned, 2))
                        for c in range(NT):
                            b = c // TPB
                            if c >= 8:
                                pe.wait_ge(x_used, at(x_used, c - 7))
                            nc.tensor.matmul(ps[:, c % 8, 0:D], XT[:, 1, c * P:(c + 1) * P], CR[:, b, :], start=True, stop=False)
                            nc.tensor.matmul(ps[:, c % 8, 0:D], TAILP[:, c * P:(c + 1) * P], CRT[:, b, :], start=False, stop=True).then_inc(pe_out, 1)

                    @block.vector
                    def _(dve):
                        dve.wait_ge(loaded, at(loaded, 32))
                        for to, raw in ((XT[:, 1, :], XT[:, 0, :]), (TAILP, RAWT)):
                            nc.vector.tensor_copy(to.rearrange("p (k w) -> p k w", w=W),
                                                      raw.rearrange("p (k w) -> p k w", w=W)[:, :, ::-1]).then_inc(turned, 1)
                        for c in range(NT):
                            dve.wait_ge(pe_out, at(pe_out, c + 1))
                            nc.vector.scalar_tensor_tensor(X[:, c, :], ps[:, c % 8, 0:D], tg[:, 2:3], X[:, c, :], ALU.mult, ALU.add).then_inc(x_used, 1)
                advance((path_stored, 16 * B * NC), (loaded, 32), (pe_out, NT), (x_used, NT), (turned, 2))

        def store():
            with nc.Block() as block:
                @block.sync
                def _(sp):
                    sp.dma_start(out.rearrange("(t p) d -> p t d", p=P), X[:, :, :]).then_inc(stored, 16)
                    sp.wait_ge(stored, at(stored, 16))

        prepare()
        for layer in (attention0, experts_layer0, attention1, block1, alignment, experts_layer2, attention3, experts_layer3):
            layer()
        store()


_INPUTS = ['g_xattn', 'g_ffn', 'L0_xattn_Wq', 'L0_xattn_Wk', 'L0_xattn_Wv', 'L0_xattn_Wo', 'L0_ffn_router_w', 'L0_ffn_w1', 'L0_ffn_w2', 'L1_xattn_Wq', 'L1_xattn_bq', 'L1_xattn_Wkv', 'L1_xattn_bkv', 'L1_xattn_Wo', 'L1_xattn_bo',
           'L3_xattn_Wq', 'L3_xattn_bq', 'L3_xattn_Wk', 'L3_xattn_bk', 'L3_xattn_Wv', 'L3_xattn_bv', 'L3_xattn_Wo', 'L3_xattn_bo',
           'L1_ffn_g1', 'L1_ffn_w_qkv', 'L1_ffn_w_o', 'L1_ffn_g2', 'L1_ffn_w_router', 'L1_ffn_w1', 'L1_ffn_w2', 'L2_ffn_router_w', 'L2_ffn_w1', 'L2_ffn_w2',
           'L3_ffn_W1', 'L3_ffn_b1', 'L3_ffn_W2', 'L3_ffn_b2', 'L3_ffn_Wg', 'L3_ffn_bg']


def kernel(**inputs):
    import concourse.bacc as _bacc
    from concourse.bass_utils import run_bass_kernel_spmd as _run

    nc = _bacc.Bacc("TRN2", target_bir_lowering=False, num_devices=1)
    arrays = {}
    arrays["x"] = np.ascontiguousarray(inputs["x"]).reshape(T, D)
    arrays["ctx"] = np.ascontiguousarray(inputs["ctx_1024"]).reshape(B * L, D)
    arrays["ctx_mask"] = np.ascontiguousarray(inputs["mask_BxS2_bf1"]).reshape(1, B * L)
    arrays["q_mask"] = np.ascontiguousarray(inputs["mask_Bx1xSxS2_bk1"]).reshape(T, L)
    for name in _INPUTS:
        v = np.ascontiguousarray(inputs[name])
        arrays[name] = v.reshape(1, -1) if v.ndim == 1 else v
    arrays.update(shape_constants())
    aps = {k: nc.dram_tensor(f"in_{k}_dram", v.shape, mybir.dt.uint8 if v.dtype == np.bool_ else mybir.dt.from_np(v.dtype), kind="ExternalInput").ap() for k, v in arrays.items()}
    for name in ("dtw_cost", "dtw_path"):
        aps[name] = nc.dram_tensor(name, (B * L, S), F32).ap()
    out = nc.dram_tensor("out_0_dram", (T, D), F32, kind="ExternalOutput").ap()
    build(nc, aps, out)
    r = _run(nc, [{f"in_{k}_dram": v for k, v in arrays.items()}], core_ids=[0])
    return np.asarray(r.results[0]["out_0_dram"]).reshape(B, S, D)
```

```python
from contextlib import ExitStack

import numpy as np

import concourse.bass as bass
from concourse import mybir

ALU = mybir.AluOpType
ACT = mybir.ActivationFunctionType
F32 = mybir.dt.float32
I32 = mybir.dt.int32
U8 = mybir.dt.uint8
AX_X = mybir.AxisListType.X

P = 128
B = 2
S = 1024
L = 154
D = 256
H = 16
HD = D // H
KD = D // P
T = B * S
NT = T // P
TPB = S // P
TAIL = L - P
HG = 4
NG = H // HG
TR = HG * TAIL
VW = HD + 1
E8 = 8
BIG = 1e30
CAPACITY1 = -(-2 * 512 * 2 * 5 // (4 * E8))
CAPACITY1_TILES = -(-CAPACITY1 // P)
SLOT_TILES = 2 * T // P + E8


class Plan:

    def __init__(self, tmp, n_exp, ks, n_tiles, stride):
        self.n_exp, self.ks, self.n_tiles, self.stride = n_exp, ks, n_tiles, stride
        self.to = tmp("to", [P, 2, NT], I32)
        self.back = tmp("back", [P, 2, NT], I32)
        self.weight = tmp("weight", [P, 2, NT])
        self.offset = tmp("offset", [1, n_tiles], I32)


class Steps:

    def __init__(self):
        self.total, self.earlier = 0, 0

    def next(self):
        self.total += 1
        return self.total + self.earlier

    def turn(self, i, per):
        self.first, self.earlier, self.per = self.total, i * per, per

    def end(self, turns):
        assert self.total - self.first == self.per, (self.total - self.first, self.per)
        self.total, self.earlier = self.first + self.per * turns, 0


def shape_constants():
    f = np.float32
    row = np.arange(P)
    ec, cc = row // NT, row % NT
    out = {
        "ident": np.eye(P, dtype=f),
        "earlier": ((ec[:, None] == ec[None, :]) & (cc[:, None] < cc[None, :])).astype(f),
        "sameexp": (ec[:, None] == ec[None, :]).astype(f),
        "experts_before": np.where((cc[:, None] == 0) & (ec[:, None] < ec[None, :]), f(P), f(0)).astype(f),
        "experts_through": np.where((cc[:, None] == 0) & (ec[:, None] <= ec[None, :]), f(P), f(0)).astype(f),
        "first_tile": (cc == 0).astype(f).reshape(P, 1),
        "tile_rows": np.broadcast_to(P * np.arange(SLOT_TILES, dtype=f), (P, SLOT_TILES)).copy(),
        "spare": (SLOT_TILES * P + row[:, None] + P * np.arange(2 * NT)[None, :] + 1).astype(f),
        "hm8": (row[:, None] // 16 == np.arange(8)[None, :]).astype(f),
        "hm4": (row[:, None] // 32 == np.arange(4)[None, :]).astype(f),
        "causal": np.where(row[None, :] > row[:, None], f(-BIG), f(0)).astype(f),
        "tailmask": np.broadcast_to((np.arange(TR)[:, None] % HG == np.arange(H)[None, :] % HG)[:, :, None], (TR, H, VW)).astype(f).reshape(TR, H * VW),
        "firstof": np.broadcast_to((E8 - np.arange(E8))[None, :, None], (P, E8, NT)).astype(f).reshape(P, E8 * NT).copy(),
    }

    start = np.full((B, 32, S // 16 + 1), f(BIG))
    start[:, 1, 0] = 0
    out["dtw_start"] = start.reshape(B * 32, -1)
    end = np.zeros((B, 32, S // 16), f)
    end[:, 16, -1] = 1
    out["dtw_end"] = end.reshape(B * 32, -1)[:, ::-1]

    def rope(freq, pos):
        ang = (pos[:, None] * freq[None, :]).astype(f)
        return np.cos(ang).astype(f), np.sin(ang).astype(f)

    pair = (row % HD) // 2
    isswap = (row % 32) >= HD
    f1 = (f(1) / np.power(f(10000), np.arange(0, HD, 2, dtype=f) / f(HD))).astype(f)
    f2 = np.power(f(10000), f(-2) * (np.arange(HD // 2, dtype=f) / f(HD))).astype(f)
    for name, freq, pos in (
        ("1q", f1, f(10) * (np.arange(S, dtype=f) / f(S))),
        ("1k", f1, f(10) * (np.arange(L, dtype=f) / f(L))),
        ("2", f2, np.arange(S, dtype=f)),
    ):
        c, s = rope(freq, pos)
        c, s = c[:, pair].T, s[:, pair].T
        out["stack" + name] = np.where(isswap[:, None], s, c).astype(f)
        out["cos" + name], out["sin" + name] = np.ascontiguousarray(c), np.ascontiguousarray(s)
    del out["stack1k"], out["cos1q"], out["sin1q"]
    return {k: np.ascontiguousarray(v) for k, v in out.items()}


def build(nc, a, out):
    ctx = ExitStack()

    def sb(name, shape, dt=F32):
        return ctx.enter_context(nc.sbuf_tensor(name, shape, dt))

    begun = {}

    def semaphore(name):
        handle = ctx.enter_context(nc.semaphore(name))
        begun[handle] = 0
        return handle

    def at(sem, n):
        return begun[sem] + n

    def advance(*grown):
        for sem, n in grown:
            begun[sem] += n

    dve_step = semaphore("dve_step")
    ao_ready = semaphore("ao_ready")
    ao_turned = semaphore("ao_turned")
    aot_ready = semaphore("aot_ready")
    att = semaphore("att")
    chosen = semaphore("chosen")
    cleared = semaphore("cleared")
    counted = semaphore("counted")
    cst = semaphore("cst")
    dist = semaphore("dist")
    dist2 = semaphore("dist2")
    dist_stored = semaphore("dist_stored")
    evac = semaphore("evac")
    exps_made = semaphore("exps_made")
    hT_free = semaphore("hT_free")
    h_out = semaphore("h_out")
    h_ready = semaphore("h_ready")
    kept_made = semaphore("kept_made")
    loaded = semaphore("loaded")
    logits = semaphore("logits")
    max_ready = semaphore("max_ready")
    norms = semaphore("norms")
    path_stored = semaphore("path_stored")
    pe_out = semaphore("pe_out")
    placed = semaphore("placed")
    place_out = semaphore("place_out")
    rows_put = semaphore("rows_put")
    filled = semaphore("filled")
    rows_in = semaphore("rows_in")
    x_in = [semaphore(f"x_in{i}") for i in range(4)]
    x_turned = semaphore("x_turned")
    xt_ready = semaphore("xt_ready")
    h_turned = semaphore("h_turned")
    y_ready = semaphore("y_ready")
    y_stored = [semaphore(f"y_stored{i}") for i in range(2)]
    tile_done = semaphore("tile_done")
    probs = semaphore("probs")
    pt_ready = semaphore("pt_ready")
    ptt_ready = semaphore("ptt_ready")
    pv = semaphore("pv")
    q_out = semaphore("q_out")
    q_ready = semaphore("q_ready")
    row_made = semaphore("row_made")
    row_free = semaphore("row_free")
    row_ready = semaphore("row_ready")
    s_free = semaphore("s_free")
    scores_made = semaphore("scores_made")
    skewed = semaphore("skewed")
    squares = semaphore("squares")
    std_ready = semaphore("std_ready")
    stored = semaphore("stored")
    tails_turned = semaphore("tails_turned")
    turned = semaphore("turned")
    v_out = semaphore("v_out")
    v_ready = semaphore("v_ready")
    v_scaled = semaphore("v_scaled")
    var_ready = semaphore("var_ready")
    x_loaded = semaphore("x_loaded")
    x_used = semaphore("x_used")
    y_out = semaphore("y_out")
    named = {}

    def sbuf(name, shape, dt=F32):
        named[name] = named.get(name, 0) + 1
        return nc.sbuf_tensor(name + (str(named[name]) if named[name] > 1 else ""), shape, dt)

    with ctx:
        ps = ctx.enter_context(nc.psum_tensor("banks", [P, 8, 512], F32))
        X = sb("X", [P, NT, D])
        XT = sb("XT", [P, KD, T])
        XN = sb("XN", [P, NT, D])
        ident = sb("ident", [P, P])
        ones = sb("ones", [P, 512])
        CR = sb("CR", [P, B, D])
        CRT = sb("CRT", [TAIL, B, D])
        CT = sb("CT", [P, KD, B, L])
        CTT = sb("CTT", [P, KD, B, TAIL, HG])
        tg = sb("tg", [P, 8])
        hm8 = sb("hm8", [P, 8])
        hm4 = sb("hm4", [P, 4])
        tailmask = sb("tailmask", [TR, H, VW])
        stats = sb("stats", [P, NT, 6])
        mv = sb("mv", [P, NT, 2])
        nrm = sb("nrm", [P, 4, NT])

        def prepare():
            with ExitStack() as own:
                def tmp(name, shape, dt=F32):
                    return own.enter_context(sbuf(name, shape, dt))
                grow = tmp("grow", [1, 8])
                with nc.Block() as block:
                    @block.sync
                    def _(sp):
                        sp.dma_start(CR[:, :, :], a["ctx"].rearrange("(b l) d -> l b d", b=B)[0:P]).then_inc(loaded, 16)
                        sp.dma_start(CRT[:, :, :], a["ctx"].rearrange("(b l) d -> l b d", b=B)[P:L]).then_inc(loaded, 16)
                        sp.dma_start(ident[:, :], a["ident"]).then_inc(loaded, 16)
                        sp.dma_start(hm8[:, :], a["hm8"]).then_inc(loaded, 16)
                        sp.dma_start(hm4[:, :], a["hm4"]).then_inc(loaded, 16)
                        sp.dma_start(tailmask[:, :, :], a["tailmask"].rearrange("p (h w) -> p h w", h=H)).then_inc(loaded, 16)
                        sp.dma_start(grow[:, 0:4], a["g_xattn"]).then_inc(loaded, 16)
                        sp.dma_start(grow[:, 4:8], a["g_ffn"]).then_inc(loaded, 16)
                        sp.dma_start(X[:, :, :], a["x"].rearrange("(t p) d -> p t d", p=P)).then_inc(x_loaded, 16)
                        sp.wait_ge(cleared, at(cleared, 1))
                        for lo in range(0, SLOT_TILES, NT):
                            n = min(NT, SLOT_TILES - lo)
                            sp.dma_start(a["expert_rows"][lo * P:(lo + n) * P, :].rearrange("(p c) d -> p c d", p=P), XN[:, 0:n, :]).then_inc(filled, 16)
                        sp.wait_ge(filled, at(filled, 16 * -(-SLOT_TILES // NT)))
                        sp.wait_ge(x_loaded, at(x_loaded, 16))

                    @block.gpsimd
                    def _(pool):
                        nc.gpsimd.memset(XN[:, :, :], 0.0).then_inc(cleared, 1)

                    @block.tensor
                    def _(pe):
                        pe.wait_ge(loaded, at(loaded, 16 * 8))
                        pe.wait_ge(cst, at(cst, 1))
                        for b in range(B):
                            for k in range(KD):
                                nc.tensor.transpose(ps[:, b, k * L:k * L + P], CR[:, b, k * P:(k + 1) * P], ident[:, :])
                                ins = nc.tensor.transpose(ps[:, b, k * L + P:(k + 1) * L], CRT[:, b, k * P:(k + 1) * P],
                                                          ident[0:TAIL, 0:TAIL])
                            ins.then_inc(pe_out, 1)
                        nc.tensor.matmul(ps[:, 2, 0:8], ones[0:1, 0:P], grow[:, :], start=True, stop=True).then_inc(pe_out, 1)

                    @block.vector
                    def _(dve):
                        nc.vector.memset(ones[:, :], 1.0).then_inc(cst, 1)

                    @block.scalar
                    def _(act):
                        for b in range(B):
                            act.wait_ge(pe_out, at(pe_out, b + 1))
                            src = ps[:, b, 0:KD * L].rearrange("p (k l) -> p k l", k=KD)
                            nc.scalar.copy(CT[:, :, b, :], src)
                            for k in range(KD):
                                nc.scalar.copy(CTT[:, k, b, :, :],
                                               src[:, k, P:L].unsqueeze(2).broadcast_to([P, TAIL, HG]))
                        act.wait_ge(pe_out, at(pe_out, 3))
                        nc.scalar.activation(tg[:, :], ps[:, 2, 0:8], ACT.Tanh)
            advance((loaded, 16 * 8), (x_loaded, 16), (pe_out, 3), (cst, 1), (cleared, 1), (filled, 16 * -(-SLOT_TILES // NT)))

        def normalise(src, dst, mean, eps, gcol=None, also=None):
            with nc.Block() as block:
                @block.vector
                def _(dve):
                    step = Steps()
                    for c in range(NT):
                        ins = nc.vector.bn_stats(stats[:, c, :], src[:, c, :])
                    ins.then_inc(dve_step, 1)
                    dve.wait_ge(dve_step, at(dve_step, step.next()))
                    for c in range(NT):
                        ins = nc.vector.bn_aggr(mv[:, c, :], stats[:, c, :])
                    ins.then_inc(dve_step, 1)
                    dve.wait_ge(dve_step, at(dve_step, step.next()))
                    if mean:
                        nc.vector.tensor_scalar(nrm[:, 0, :], mv[:, :, 1], eps, None, ALU.add).then_inc(dve_step, 1)
                        dve.wait_ge(dve_step, at(dve_step, step.next()))
                    else:
                        nc.vector.tensor_tensor(nrm[:, 1, :], mv[:, :, 0], mv[:, :, 0], ALU.mult).then_inc(dve_step, 1)
                        dve.wait_ge(dve_step, at(dve_step, step.next()))
                        nc.vector.scalar_tensor_tensor(nrm[:, 0, :], mv[:, :, 1], eps, nrm[:, 1, :], ALU.add, ALU.add).then_inc(dve_step, 1)
                        dve.wait_ge(dve_step, at(dve_step, step.next()))
                    nc.vector.engine_nop().then_inc(var_ready, 1)
                    dve.wait_ge(std_ready, at(std_ready, 1))
                    nc.vector.reciprocal(nrm[:, 3, :], nrm[:, 2, :]).then_inc(dve_step, 1)
                    dve.wait_ge(dve_step, at(dve_step, step.next()))
                    for c in range(NT):
                        if mean:
                            ins = nc.vector.tensor_scalar(dst[:, c, :], src[:, c, :], mv[:, c, 0:1], nrm[:, 3, c:c + 1],
                                                          ALU.subtract, ALU.mult)
                        else:
                            ins = nc.vector.tensor_scalar(dst[:, c, :], src[:, c, :], nrm[:, 3, c:c + 1], None, ALU.mult)
                        ins.then_inc(row_ready, 1)
                    advance((dve_step, step.total))

                @block.scalar
                def _(act):
                    act.wait_ge(var_ready, at(var_ready, 1))
                    nc.scalar.activation(nrm[:, 2, :], nrm[:, 0, :], ACT.Sqrt).then_inc(std_ready, 1)
                    for c2 in range(NT // 2):
                        act.wait_ge(pe_out, at(pe_out, c2 + 1))
                        for k in range(KD):
                            src_ = ps[:, c2 % 4, k * D:(k + 1) * D]
                            d_ = XT[:, k, c2 * D:(c2 + 1) * D]
                            if gcol is None:
                                ins = nc.scalar.copy(d_, src_)
                            else:
                                ins = nc.scalar.activation(d_, src_, ACT.Copy, scale=gcol[:, k:k + 1])
                        ins.then_inc(evac, 1)

                @block.tensor
                def _(pe):
                    for c2 in range(NT // 2):
                        pe.wait_ge(row_ready, at(row_ready, 2 * c2 + 2))
                        if c2 >= 4:
                            pe.wait_ge(evac, at(evac, c2 - 3))
                        for k in range(KD):
                            for j in range(2):
                                ins = nc.tensor.transpose(ps[:, c2 % 4, k * D + j * P:k * D + (j + 1) * P],
                                                          dst[:, 2 * c2 + j, k * P:(k + 1) * P], ident[:, :])
                        ins.then_inc(pe_out, 1)
            advance((var_ready, 1), (std_ready, 1), (row_ready, NT), (pe_out, NT // 2), (evac, NT // 2))

        def load_weights(pairs):
            with nc.Block() as block:
                @block.sync
                def _(sp):
                    for dst, src in pairs:
                        sp.dma_start(dst, src).then_inc(loaded, 16)
                    sp.wait_ge(loaded, at(loaded, 16 * len(pairs)))
            advance((loaded, 16 * len(pairs)))

        def transpose_weights(pairs):
            with nc.Block() as block:
                @block.tensor
                def _(pe):
                    for n, (dst, src) in enumerate(pairs):
                        if n >= 4:
                            pe.wait_ge(evac, at(evac, 2 * (n - 3)))
                        for ki in range(KD):
                            for ko in range(KD):
                                ins = nc.tensor.transpose(ps[:, (n % 4) * 2 + ki, ko * P:(ko + 1) * P],
                                                          src[:, ko, ki * P:(ki + 1) * P], ident[:, :])
                            ins.then_inc(pe_out, 1)

                @block.scalar
                def _(act):
                    for n, (dst, src) in enumerate(pairs):
                        for ki in range(KD):
                            act.wait_ge(pe_out, at(pe_out, 2 * n + ki + 1))
                            nc.scalar.copy(dst[:, ki, :], ps[:, (n % 4) * 2 + ki, 0:D]).then_inc(evac, 1)
            advance((pe_out, 2 * len(pairs)), (evac, 2 * len(pairs)))

        def keys_values(KB, VM, VT, heads, mask, scale, wkA, wv, wkB=None, bkA=None, bkB=None, bv=None, cosk=None, sink=None, kr=None):
            ch_n = H // heads
            n_ps = B * 2
            with nc.Block() as block:
                @block.tensor
                def _(pe):
                    flat = CT[:, :, :, :].rearrange("p k b l -> p k (b l)")
                    for ch in range(ch_n):
                        if ch >= 2:
                            pe.wait_ge(evac, at(evac, ch - 1))
                        for bank, w, bias in ((ch % 2, wkA, bkA), (2 + ch % 2, wkB, bkB)):
                            if w is None:
                                continue
                            for k in range(KD):
                                ins = nc.tensor.matmul(ps[:, bank, 0:B * L], w[:, k, ch * P:(ch + 1) * P], flat[:, k, :],
                                                       start=(k == 0), stop=(k == KD - 1 and bias is None))
                            if bias is not None:
                                ins = nc.tensor.matmul(ps[:, bank, 0:B * L], bias[0:1, ch * P:(ch + 1) * P], ones[0:1, 0:B * L],
                                                       start=False, stop=True)
                        ins.then_inc(pe_out, 1)
                    for b in range(B):
                        for k in range(KD):
                            ins = nc.tensor.matmul(ps[:, 4 + b, 0:D], CT[:, k, b, 0:P], wv[:, k, :],
                                                   start=(k == 0), stop=(k == KD - 1 and bv is None))
                        if bv is not None:
                            ins = nc.tensor.matmul(ps[:, 4 + b, 0:D], ones[0:1, 0:P], bv[0:1, :], start=False, stop=True)
                        ins.then_inc(v_out, 1)
                        for k in range(KD):
                            ins = nc.tensor.matmul(ps[0:TR, 6 + b, 0:D], CTT[:, k, b, :, :].rearrange("p l g -> p (l g)"), wv[:, k, :],
                                                   start=(k == 0), stop=(k == KD - 1 and bv is None))
                        if bv is not None:
                            ins = nc.tensor.matmul(ps[0:TR, 6 + b, 0:D], ones[0:1, 0:TR], bv[0:1, :], start=False, stop=True)
                        ins.then_inc(v_out, 1)

                @block.vector
                def _(dve):
                    step = Steps()
                    for ch in range(ch_n):
                        dve.wait_ge(pe_out, at(pe_out, ch + 1))
                        src = ps[:, ch % 2, 0:B * L].rearrange("p (b l) -> p b l", b=B)
                        if cosk is not None:
                            cb = cosk[:, :].unsqueeze(1).broadcast_to([P, B, L])
                            sb_ = sink[:, :].unsqueeze(1).broadcast_to([P, B, L])
                            nc.vector.tensor_tensor(kr[:, 0], src, cb, ALU.mult)
                            nc.vector.tensor_tensor(kr[:, 1], ps[:, 2 + ch % 2, 0:B * L].rearrange("p (b l) -> p b l", b=B),
                                                         sb_, ALU.mult).then_inc(dve_step, 1)
                            dve.wait_ge(dve_step, at(dve_step, step.next()))
                            nc.vector.tensor_tensor(kr[:, 0], kr[:, 0], kr[:, 1], ALU.add).then_inc(dve_step, 1)
                            dve.wait_ge(dve_step, at(dve_step, step.next()))
                            src = kr[:, 0]
                        for hh in range(heads):
                            ins = nc.vector.tensor_scalar(KB[:, (ch * heads + hh) // HG, :, :, hh % HG], src, mask[:, hh:hh + 1], scale, ALU.mult, ALU.mult)
                        ins.then_inc(evac, 1)
                        dve.wait_ge(evac, at(evac, ch + 1))
                    nc.vector.memset(VM[:, :, :, HD:VW], 1.0)
                    for b in range(B):
                        dve.wait_ge(v_out, at(v_out, 2 * b + 1))
                        nc.vector.tensor_copy(VM[:, b, :, 0:HD], ps[:, 4 + b, 0:D].rearrange("p (h w) -> p h w", h=H))
                        dve.wait_ge(v_out, at(v_out, 2 * b + 2))
                        nc.vector.tensor_tensor(VT[:, b, :, 0:HD], ps[0:TR, 6 + b, 0:D].rearrange("p (h w) -> p h w", h=H),
                                                tailmask[:, :, 0:HD], ALU.mult)
                        nc.vector.tensor_copy(VT[:, b, :, HD:VW], tailmask[:, :, HD:VW])
                    advance((dve_step, step.total))
            advance((pe_out, ch_n), (evac, ch_n), (v_out, 2 * B))

        def attention0():
            with ExitStack() as own:
                def tmp(name, shape, dt=F32):
                    return own.enter_context(sbuf(name, shape, dt))
                W = [tmp(f"a0w{i}", [P, KD, D]) for i in range(4)]
                KB = tmp("a0KB", [P, NG, B, L, HG])
                VM = tmp("a0VM", [P, B, H, VW])
                VT = tmp("a0VT", [TR, B, H, VW])
                with ExitStack() as own2:
                    R = [own2.enter_context(sbuf(f"a0r{i}", [P, KD, D], F32)) for i in range(4)]
                    load_weights([(R[i][:, :, :], a[f"L0_xattn_W{c}"].rearrange("(k p) d -> p k d", p=P))
                                  for i, c in enumerate("qkvo")])
                    transpose_weights([(W[i], R[i]) for i in range(4)])
                wq, wk, wv, wo = W
                keys_values(KB, VM, VT, 8, hm8, float(D) ** -0.5, wk, wv)
                normalise(X, XN, True, 1e-5)
                AT = XN[:, :, :].rearrange("p c d -> p (c d)").rearrange("p (k t) -> p k t", k=KD)
                QT = tmp("a0QT", [P, KD, T])
                with nc.Block() as block:
                    @block.tensor
                    def _(pe):
                        for m in range(KD):
                            for n in range(4):
                                i = 4 * m + n
                                for k in range(KD):
                                    ins = nc.tensor.matmul(ps[:, i, :], wq[:, k, m * P:(m + 1) * P], XT[:, k, n * 512:(n + 1) * 512],
                                                           start=(k == 0), stop=(k == KD - 1))
                                ins.then_inc(pe_out, 1)

                    @block.scalar
                    def _(act):
                        for i in range(8):
                            act.wait_ge(pe_out, at(pe_out, i + 1))
                            nc.scalar.copy(QT[:, i // 4, (i % 4) * 512:(i % 4 + 1) * 512], ps[:, i, :])
                advance((pe_out, 8))

                EX = tmp("a0E", [P, H + NG, S])
                nm = tmp("a0nm", [P, H + NG])
                sm = tmp("a0sm", [P, H + NG])
                rc = tmp("a0rc", [P, H + NG])
                VB = XT[:, :, :].rearrange("p k t -> p (k t)")[:, 0:(H + NG) * P].rearrange("p (u c) -> p u c", c=P)
                NB = tmp("a0NB", [P, H + NG, P])
                dn = tmp("a0dn", [P, 2, 512])
                with nc.Block() as block:
                    @block.vector
                    def _(dve):
                        nc.vector.memset(VB[:, :, :], 0.0)
                        nc.vector.memset(NB[:, :, :], 0.0)
                units = [(u, P, u // 8, u % 8) for u in range(H)] + [(H + g, TR, g // 2, g) for g in range(NG)]
                for b in range(B):
                    with nc.Block() as block:
                        @block.tensor
                        def _(pe):
                            for u, rows, m, hh in units:
                                if u >= 2:
                                    pe.wait_ge(probs, at(probs, u - 1))
                                lhs = (KB[:, u // HG, b, 0:P, u % HG] if u < H else
                                       KB[:, hh, b, P:L, :].rearrange("p l h -> p (l h)"))
                                for n in range(2):
                                    ins = nc.tensor.matmul(ps[0:rows, 2 * (u % 2) + n, :], lhs,
                                                           QT[:, m, b * S + n * 512:b * S + (n + 1) * 512], start=True, stop=True)
                                ins.then_inc(scores_made, 1)
                            pe.wait_ge(v_scaled, at(v_scaled, 1))
                            for i in range(4):
                                m, n = i // 2, i % 2
                                if i >= 2:
                                    pe.wait_ge(att, at(att, i - 1))
                                us = [8 * m + j for j in range(8)] + [H + 2 * m, H + 2 * m + 1]
                                for bank, lhs in ((4 + i % 2, VB), (6 + i % 2, NB)):
                                    for j, u in enumerate(us):
                                        rows = P if u < H else TR
                                        ins = nc.tensor.matmul(ps[:, bank, :], lhs[0:rows, u, :],
                                                               EX[0:rows, u, n * 512:(n + 1) * 512], start=(j == 0), stop=(j == 9))
                                ins.then_inc(pv, 1)

                        @block.vector
                        def _(dve):
                            step = Steps()
                            for u, rows, m, hh in units:
                                dve.wait_ge(scores_made, at(scores_made, u + 1))
                                nc.vector.tensor_reduce(nm[0:rows, u:u + 1], ps[0:rows, 2 * (u % 2):2 * (u % 2) + 2, :],
                                                            mybir.AxisListType.XY, ALU.max, negate=True).then_inc(max_ready, 1)
                            dve.wait_ge(probs, at(probs, H + NG))
                            nc.vector.reciprocal(rc[:, 0:H], sm[:, 0:H])
                            nc.vector.reciprocal(rc[0:TR, H:], sm[0:TR, H:]).then_inc(dve_step, 1)
                            dve.wait_ge(dve_step, at(dve_step, step.next()))
                            for h in range(H):
                                col = (h % 8) * HD
                                nc.vector.tensor_scalar(VB[:, h, col:col + HD], VM[:, b, h, 0:HD], rc[:, h:h + 1], None, ALU.mult)
                                nc.vector.tensor_scalar(NB[:, h, col:col + HD], ones[:, 0:HD], rc[:, h:h + 1], None, ALU.mult)
                            for g in range(NG):
                                col = (g % 2) * HG * HD
                                v = VB[0:TR, H + g, col:col + HG * HD].rearrange("p (h w) -> p h w", h=HG)
                                w = NB[0:TR, H + g, col:col + HG * HD].rearrange("p (h w) -> p h w", h=HG)
                                nc.vector.tensor_scalar(v, VT[:, b, g * HG:(g + 1) * HG, 0:HD], rc[0:TR, H + g:H + g + 1], None, ALU.mult)
                                ins = nc.vector.tensor_scalar(w, tailmask[:, g * HG:(g + 1) * HG, 0:HD], rc[0:TR, H + g:H + g + 1], None, ALU.mult)
                            ins.then_inc(v_scaled, 1)
                            for i in range(4):
                                m, n = i // 2, i % 2
                                dve.wait_ge(pv, at(pv, i + 1))
                                nc.vector.reciprocal(dn[:, i % 2, :], ps[:, 6 + i % 2, :]).then_inc(dve_step, 1)
                                dve.wait_ge(dve_step, at(dve_step, step.next()))
                                nc.vector.tensor_tensor(AT[:, m, b * S + n * 512:b * S + (n + 1) * 512], ps[:, 4 + i % 2, :],
                                                            dn[:, i % 2, :], ALU.mult).then_inc(att, 1)
                            advance((dve_step, step.total))

                        @block.scalar
                        def _(act):
                            for u, rows, m, hh in units:
                                act.wait_ge(max_ready, at(max_ready, u + 1))
                                nc.scalar.activation(EX[0:rows, u, :].rearrange("p (n q) -> p n q", n=2), ps[0:rows, 2 * (u % 2):2 * (u % 2) + 2, :],
                                                         ACT.Exp, bias=nm[0:rows, u:u + 1], accum_out=sm[0:rows, u:u + 1]).then_inc(probs, 1)
                    advance((scores_made, H + NG), (max_ready, H + NG), (probs, H + NG), (v_scaled, 1), (pv, 4), (att, 4))
                with nc.Block() as block:
                    @block.tensor
                    def _(pe):
                        for c in range(NT):
                            if c >= 4:
                                pe.wait_ge(x_used, at(x_used, c - 3))
                            for k in range(KD):
                                ins = nc.tensor.matmul(ps[:, c % 4, 0:D], AT[:, k, c * P:(c + 1) * P], wo[:, k, :],
                                                       start=(k == 0), stop=(k == KD - 1))
                            ins.then_inc(pe_out, 1)

                    @block.vector
                    def _(dve):
                        for c in range(NT):
                            dve.wait_ge(pe_out, at(pe_out, c + 1))
                            nc.vector.scalar_tensor_tensor(X[:, c, :], ps[:, c % 4, 0:D], tg[:, 0:1], X[:, c, :],
                                                               ALU.mult, ALU.add).then_inc(x_used, 1)
                advance((pe_out, NT), (x_used, NT))

        def route(mode, n_exp, wr, gate, plan, bias=None, capacity=None):
            R = n_exp * NT
            ks, n_tiles = plan.ks, plan.n_tiles
            with ExitStack() as own:
                def tmp(name, shape, dt=F32):
                    return own.enter_context(sbuf("r_" + name, shape, dt))
                firstof = tmp("firstof", [P, E8, NT])
                earlier = tmp("earlier", [P, P])
                sameexp = tmp("sameexp", [P, P])
                pr = tmp("pr", [P, n_exp, NT])
                w = tmp("w", [P, n_exp, NT])
                oh = [tmp(f"oh{i}", [P, n_exp, NT]) for i in range(2)]
                m = tmp("m", [P, 8, NT])
                ohT = [tmp(f"ohT{i}", [P, P]) for i in range(2)]
                cs = [tmp(f"cs{i}", [P, P]) for i in range(2)]
                keep = [tmp(f"keep{i}", [P, P]) for i in range(2)]
                col = tmp("col", [P, 8])
                thr = tmp("thr", [P, 4], I32)
                G = tmp("G", [P, n_exp, NT])
                taken = tmp("taken", [P, n_exp, NT])
                part = tmp("part", [P, n_exp, NT])
                before = tmp("before", [P, P])
                through = tmp("through", [P, P])
                first_tile = tmp("first_tile", [P, 1])
                tile_rows = tmp("tile_rows", [P, SLOT_TILES])
                begun_tiles = tmp("begun_tiles", [P, SLOT_TILES])
                spare = tmp("spare", [P, 2, NT])
                place = tmp("place", [P, 2, NT])

                def bc(v):
                    return v.unsqueeze(1).broadcast_to([P, n_exp, NT])

                def by_tile(v):
                    return v.rearrange("p e c -> p c e")

                with nc.Block() as block:
                    @block.sync
                    def _(sp):
                        sp.dma_start(firstof[:, :, :], a["firstof"].rearrange("p (e c) -> p e c", e=E8)).then_inc(loaded, 16)
                        sp.dma_start(earlier[:, :], a["earlier"]).then_inc(loaded, 16)
                        sp.dma_start(sameexp[:, :], a["sameexp"]).then_inc(loaded, 16)
                        sp.dma_start(before[:, :], a["experts_before"]).then_inc(loaded, 16)
                        sp.dma_start(through[:, :], a["experts_through"]).then_inc(loaded, 16)
                        sp.dma_start(first_tile[:, :], a["first_tile"]).then_inc(loaded, 16)
                        sp.dma_start(tile_rows[:, :], a["tile_rows"]).then_inc(loaded, 16)
                        sp.dma_start(spare[:, :, :], a["spare"].rearrange("p (i c) -> p i c", i=2)).then_inc(loaded, 16)

                    @block.tensor
                    def _(pe):
                        for c in range(NT):
                            for k in range(KD):
                                ins = nc.tensor.matmul(ps[:, 0, c * n_exp:(c + 1) * n_exp], XT[:, k, c * P:(c + 1) * P], wr[:, k, :],
                                                       start=(k == 0), stop=(k == KD - 1 and bias is None))
                            if bias is not None:
                                ins = nc.tensor.matmul(ps[:, 0, c * n_exp:(c + 1) * n_exp], ones[0:1, 0:P], bias[0:1, :],
                                                       start=False, stop=True)
                        ins.then_inc(pe_out, 1)
                        if mode == "first":
                            pe.wait_ge(loaded, at(loaded, 128))
                            for i in range(2):
                                pe.wait_ge(chosen, at(chosen, i + 1))
                                nc.tensor.transpose(ps[:, 1 + i, 0:P], oh[i][:, :, :].rearrange("p e c -> p (e c)"), ident[:, :]).then_inc(pe_out, 1)
                            for i in range(2):
                                pe.wait_ge(counted, at(counted, i + 1))
                                nc.tensor.matmul(ps[:, 3 + i, 0:1], earlier[:, :], cs[i][:, P - 1:P], start=True, stop=True).then_inc(pe_out, 1)
                            for i in range(2):
                                pe.wait_ge(kept_made, at(kept_made, i + 1))
                                nc.tensor.transpose(ps[:, 5 + i, 0:P], keep[i][:, :], ident[:, :]).then_inc(pe_out, 1)
                        if mode == "best":
                            pe.wait_ge(loaded, at(loaded, 128))
                            pe.wait_ge(chosen, at(chosen, 1))
                            nc.tensor.transpose(ps[:, 1, 0:P], w[:, :, :].rearrange("p e c -> p (e c)"), ident[:, :]).then_inc(pe_out, 1)
                            for i in range(31):
                                pe.wait_ge(counted, at(counted, i + 1))
                                nc.tensor.matmul(ps[:, 2 + i % 2, 0:1], sameexp[:, :], col[:, 0:1], start=True, stop=True).then_inc(pe_out, 1)
                            pe.wait_ge(counted, at(counted, 32))
                            nc.tensor.matmul(ps[:, 4, 0:1], earlier[:, :], cs[0][:, P - 1:P], start=True, stop=True).then_inc(pe_out, 1)
                            pe.wait_ge(kept_made, at(kept_made, 1))
                            nc.tensor.transpose(ps[:, 5, 0:P], keep[0][:, :], ident[:, :]).then_inc(pe_out, 1)

                        if mode == "top2" or mode == "top1":
                            pe.wait_ge(loaded, at(loaded, 128))
                        pe.wait_ge(placed, at(placed, 1))
                        nc.tensor.transpose(ps[0:R, 7, 0:P], taken[:, :, :].rearrange("p e c -> p (e c)"), ident[:, :]).then_inc(place_out, 1)
                        pe.wait_ge(placed, at(placed, 2))
                        nc.tensor.matmul(ps[0:R, 7, P:P + 1], earlier[0:R, 0:R], cs[0][0:R, P - 1:P], start=True, stop=True)
                        nc.tensor.matmul(ps[0:R, 7, P + 1:P + 2], sameexp[0:R, 0:R], cs[0][0:R, P - 1:P], start=True, stop=True).then_inc(place_out, 1)
                        pe.wait_ge(placed, at(placed, 3))
                        nc.tensor.matmul(ps[0:R, 7, P + 2:P + 3], before[0:R, 0:R], col[0:R, 2:3], start=True, stop=True)
                        nc.tensor.matmul(ps[0:R, 7, P + 3:P + 4], through[0:R, 0:R], col[0:R, 2:3], start=True, stop=True).then_inc(place_out, 1)
                        pe.wait_ge(placed, at(placed, 4))
                        nc.tensor.transpose(ps[:, 7, 0:R], cs[1][0:R, :], ident[0:R, 0:R])
                        nc.tensor.matmul(ps[0:1, 7, 256:256 + n_tiles], first_tile[0:R, 0:1], begun_tiles[0:R, 0:n_tiles],
                                         start=True, stop=True).then_inc(place_out, 1)

                    @block.scalar
                    def _(act):
                        act.wait_ge(logits, at(logits, 1))
                        nc.scalar.activation(pr[:, :, :], pr[:, :, :], ACT.Exp).then_inc(exps_made, 1)

                    @block.vector
                    def _(dve):
                        step = Steps()
                        dve.wait_ge(pe_out, at(pe_out, 1))
                        nc.vector.tensor_copy(pr[:, :, :], ps[:, 0, 0:NT * n_exp].rearrange("p (c e) -> p e c", c=NT)).then_inc(dve_step, 1)
                        dve.wait_ge(dve_step, at(dve_step, step.next()))
                        nc.vector.tensor_reduce(m[:, 0, :], by_tile(pr[:, :, :]), AX_X, ALU.max).then_inc(dve_step, 1)
                        dve.wait_ge(dve_step, at(dve_step, step.next()))
                        nc.vector.tensor_tensor(pr[:, :, :], pr[:, :, :], bc(m[:, 0, :]), ALU.subtract).then_inc(logits, 1)
                        dve.wait_ge(exps_made, at(exps_made, 1))
                        nc.vector.tensor_reduce(m[:, 0, :], by_tile(pr[:, :, :]), AX_X, ALU.add).then_inc(dve_step, 1)
                        dve.wait_ge(dve_step, at(dve_step, step.next()))
                        nc.vector.reciprocal(m[:, 1, :], m[:, 0, :]).then_inc(dve_step, 1)
                        dve.wait_ge(dve_step, at(dve_step, step.next()))
                        nc.vector.tensor_tensor(pr[:, :, :], pr[:, :, :], bc(m[:, 1, :]), ALU.mult).then_inc(dve_step, 1)
                        dve.wait_ge(dve_step, at(dve_step, step.next()))
                        dve.wait_ge(loaded, at(loaded, 128))
                        for i in range(ks):
                            nc.vector.tensor_reduce(m[:, 2 + i, :], by_tile(pr[:, :, :]), AX_X, ALU.max).then_inc(dve_step, 1)
                            dve.wait_ge(dve_step, at(dve_step, step.next()))
                            nc.vector.tensor_tensor(w[:, :, :], pr[:, :, :], bc(m[:, 2 + i, :]), ALU.is_equal).then_inc(dve_step, 1)
                            dve.wait_ge(dve_step, at(dve_step, step.next()))
                            nc.vector.tensor_tensor(w[:, :, :], w[:, :, :], firstof[:, 0:n_exp, :], ALU.mult).then_inc(dve_step, 1)
                            dve.wait_ge(dve_step, at(dve_step, step.next()))
                            nc.vector.tensor_reduce(m[:, 4, :], by_tile(w[:, :, :]), AX_X, ALU.max).then_inc(dve_step, 1)
                            dve.wait_ge(dve_step, at(dve_step, step.next()))
                            ins = nc.vector.tensor_tensor(oh[i][:, :, :], w[:, :, :], bc(m[:, 4, :]), ALU.is_equal)
                            ins.then_inc(dve_step, 1)
                            dve.wait_ge(dve_step, at(dve_step, step.next()))
                            if i == 0 and ks == 2:
                                nc.vector.scalar_tensor_tensor(pr[:, :, :], oh[0][:, :, :], -2.0, pr[:, :, :], ALU.mult, ALU.add).then_inc(dve_step, 1)
                                dve.wait_ge(dve_step, at(dve_step, step.next()))
                        if mode == "top1":
                            nc.vector.tensor_scalar(G[:, :, :], oh[0][:, :, :], gate, None, ALU.mult).then_inc(dve_step, 1)
                            dve.wait_ge(dve_step, at(dve_step, step.next()))
                        if mode in ("first", "top2"):
                            eps = 1e-9 if mode == "top2" else 0.0
                            nc.vector.scalar_tensor_tensor(m[:, 5, :], m[:, 2, :], eps, m[:, 3, :], ALU.add, ALU.add).then_inc(dve_step, 1)
                            dve.wait_ge(dve_step, at(dve_step, step.next()))
                            nc.vector.reciprocal(m[:, 6, :], m[:, 5, :]).then_inc(dve_step, 1)
                            dve.wait_ge(dve_step, at(dve_step, step.next()))
                            for i in range(2):
                                nc.vector.scalar_tensor_tensor(m[:, 2 + i, :], m[:, 2 + i, :], gate, m[:, 6, :], ALU.mult, ALU.mult).then_inc(dve_step, 1)
                                dve.wait_ge(dve_step, at(dve_step, step.next()))
                        kept = [oh[0][:, :, :], oh[1][:, :, :]]
                        if mode == "first":
                            nc.vector.engine_nop().then_inc(chosen, 2)
                            for i in range(2):
                                dve.wait_ge(pe_out, at(pe_out, 2 + i))
                                nc.vector.tensor_copy(ohT[i][:, :], ps[:, 1 + i, 0:P]).then_inc(dve_step, 1)
                                dve.wait_ge(dve_step, at(dve_step, step.next()))
                                nc.vector.tensor_tensor_scan(cs[i][:, :], ones[:, 0:P], ohT[i][:, :], 0.0, ALU.mult, ALU.add).then_inc(counted, 1)
                            for i in range(2):
                                dve.wait_ge(counted, at(counted, i + 1))
                                dve.wait_ge(pe_out, at(pe_out, 4 + i))
                                nc.vector.tensor_scalar(cs[i][:, :], cs[i][:, :], ps[:, 3 + i, 0:1], float(capacity), ALU.add, ALU.is_le).then_inc(dve_step, 1)
                                dve.wait_ge(dve_step, at(dve_step, step.next()))
                                nc.vector.tensor_tensor(keep[i][:, :], cs[i][:, :], ohT[i][:, :], ALU.mult).then_inc(kept_made, 1)
                            for i in range(2):
                                dve.wait_ge(pe_out, at(pe_out, 6 + i))
                                kept[i] = ps[:, 5 + i, 0:P].rearrange("p (e c) -> p e c", e=n_exp)
                        if mode in ("first", "top2", "best"):
                            dst = w if mode == "best" else G
                            nc.vector.tensor_tensor(part[:, :, :], kept[0], bc(m[:, 2, :]), ALU.mult)
                            nc.vector.tensor_tensor(taken[:, :, :], kept[1], bc(m[:, 3, :]), ALU.mult).then_inc(dve_step, 1)
                            dve.wait_ge(dve_step, at(dve_step, step.next()))
                            nc.vector.tensor_tensor(dst[:, :, :], part[:, :, :], taken[:, :, :], ALU.add).then_inc(dve_step, 1)
                            dve.wait_ge(dve_step, at(dve_step, step.next()))
                        if mode == "best":
                            nc.vector.engine_nop().then_inc(chosen, 1)
                            gT = ohT[0]
                            dve.wait_ge(pe_out, at(pe_out, 2))
                            nc.vector.memset(thr[:, 0:1], 0)
                            nc.vector.tensor_copy(gT[:, :], ps[:, 1, 0:P]).then_inc(dve_step, 1)
                            dve.wait_ge(dve_step, at(dve_step, step.next()))
                            for i in range(30):
                                bit = 1 << (29 - i)
                                nc.vector.tensor_scalar(thr[:, 1:2], thr[:, 0:1], bit, None, ALU.bitwise_or).then_inc(dve_step, 1)
                                dve.wait_ge(dve_step, at(dve_step, step.next()))
                                nc.vector.tensor_scalar(cs[1][:, :], gT[:, :], thr[:, 1:2].bitcast(F32), None, ALU.is_ge, ALU.add,
                                                            accum_out=col[:, 0:1]).then_inc(counted, 1)
                                dve.wait_ge(pe_out, at(pe_out, 3 + i))
                                nc.vector.tensor_scalar(thr[:, 2:3], ps[:, 2 + i % 2, 0:1], float(capacity), float(bit), ALU.is_ge, ALU.mult).then_inc(dve_step, 1)
                                dve.wait_ge(dve_step, at(dve_step, step.next()))
                                nc.vector.tensor_tensor(thr[:, 0:1], thr[:, 0:1], thr[:, 2:3], ALU.bitwise_or).then_inc(dve_step, 1)
                                dve.wait_ge(dve_step, at(dve_step, step.next()))
                            t32 = thr[:, 0:1].bitcast(F32)
                            nc.vector.tensor_scalar(keep[1][:, :], gT[:, :], t32, None, ALU.is_gt, ALU.add, accum_out=col[:, 0:1]).then_inc(counted, 1)
                            nc.vector.tensor_scalar(ohT[1][:, :], gT[:, :], t32, None, ALU.is_equal).then_inc(dve_step, 1)
                            dve.wait_ge(dve_step, at(dve_step, step.next()))
                            nc.vector.tensor_tensor_scan(cs[0][:, :], ones[:, 0:P], ohT[1][:, :], 0.0, ALU.mult, ALU.add).then_inc(counted, 1)
                            dve.wait_ge(pe_out, at(pe_out, 33))
                            nc.vector.tensor_scalar(col[:, 1:2], ps[:, 2, 0:1], -1.0, float(capacity), ALU.mult, ALU.add).then_inc(dve_step, 1)
                            dve.wait_ge(dve_step, at(dve_step, step.next()))
                            dve.wait_ge(pe_out, at(pe_out, 34))
                            nc.vector.tensor_scalar(cs[1][:, :], cs[0][:, :], ps[:, 4, 0:1], col[:, 1:2], ALU.add, ALU.is_le).then_inc(dve_step, 1)
                            dve.wait_ge(dve_step, at(dve_step, step.next()))
                            nc.vector.tensor_tensor(cs[1][:, :], cs[1][:, :], ohT[1][:, :], ALU.mult).then_inc(dve_step, 1)
                            dve.wait_ge(dve_step, at(dve_step, step.next()))
                            nc.vector.tensor_tensor(cs[1][:, :], cs[1][:, :], keep[1][:, :], ALU.add).then_inc(dve_step, 1)
                            dve.wait_ge(dve_step, at(dve_step, step.next()))
                            nc.vector.tensor_tensor(keep[0][:, :], cs[1][:, :], gT[:, :], ALU.mult).then_inc(kept_made, 1)
                            dve.wait_ge(pe_out, at(pe_out, 35))
                            nc.vector.tensor_scalar(G[:, :, :], ps[:, 5, 0:P].rearrange("p (e c) -> p e c", e=n_exp), gate, None, ALU.mult).then_inc(dve_step, 1)
                            dve.wait_ge(dve_step, at(dve_step, step.next()))
                        nc.vector.tensor_scalar(taken[:, :, :], G[:, :, :], 0.0, None, ALU.not_equal).then_inc(placed, 1)
                        dve.wait_ge(place_out, at(place_out, 1))
                        nc.vector.tensor_copy(ohT[0][0:R, :], ps[0:R, 7, 0:P]).then_inc(dve_step, 1)
                        dve.wait_ge(dve_step, at(dve_step, step.next()))
                        nc.vector.tensor_tensor_scan(cs[0][0:R, :], ones[0:R, 0:P], ohT[0][0:R, :], 0.0, ALU.mult, ALU.add).then_inc(placed, 1)
                        dve.wait_ge(place_out, at(place_out, 2))
                        nc.vector.tensor_copy(col[0:R, 3:5], ps[0:R, 7, P:P + 2]).then_inc(dve_step, 1)
                        dve.wait_ge(dve_step, at(dve_step, step.next()))
                        nc.vector.tensor_scalar(ohT[1][0:R, 0:NT], tile_rows[0:R, 0:NT], col[0:R, 4:5], None, ALU.is_lt, ALU.add,
                                                accum_out=col[0:R, 2:3]).then_inc(placed, 1)
                        dve.wait_ge(place_out, at(place_out, 3))
                        nc.vector.tensor_copy(col[0:R, 5:7], ps[0:R, 7, P + 2:P + 4]).then_inc(dve_step, 1)
                        dve.wait_ge(dve_step, at(dve_step, step.next()))
                        nc.vector.tensor_scalar(cs[1][0:R, :], cs[0][0:R, :], col[0:R, 3:4], col[0:R, 5:6], ALU.add, ALU.add)
                        nc.vector.tensor_scalar(begun_tiles[0:R, 0:n_tiles], tile_rows[0:R, 0:n_tiles], col[0:R, 6:7], None, ALU.is_ge).then_inc(placed, 1)
                        dve.wait_ge(place_out, at(place_out, 4))
                        nc.vector.tensor_scalar(plan.offset[0:1, :], ps[0:1, 7, 256:256 + n_tiles], float(n_exp - 1), float(plan.stride), ALU.min, ALU.mult)
                        nc.vector.tensor_tensor(taken[:, :, :], taken[:, :, :], ps[:, 7, 0:R].rearrange("p (e c) -> p e c", e=n_exp), ALU.mult).then_inc(dve_step, 1)
                        dve.wait_ge(dve_step, at(dve_step, step.next()))
                        for i in range(ks):
                            nc.vector.tensor_tensor(part[:, :, :], taken[:, :, :], oh[i][:, :, :], ALU.mult)
                            nc.vector.tensor_tensor(w[:, :, :], G[:, :, :], oh[i][:, :, :], ALU.mult).then_inc(dve_step, 1)
                            dve.wait_ge(dve_step, at(dve_step, step.next()))
                            nc.vector.tensor_reduce(place[:, i, :], by_tile(part[:, :, :]), AX_X, ALU.add)
                            nc.vector.tensor_reduce(plan.weight[:, i, :], by_tile(w[:, :, :]), AX_X, ALU.add).then_inc(dve_step, 1)
                            dve.wait_ge(dve_step, at(dve_step, step.next()))
                        at_ = place[:, 0:ks, :]
                        nc.vector.scalar_tensor_tensor(spare[:, 0:ks, :], at_, 0.0, spare[:, 0:ks, :], ALU.is_equal, ALU.mult).then_inc(dve_step, 1)
                        dve.wait_ge(dve_step, at(dve_step, step.next()))
                        nc.vector.scalar_tensor_tensor(spare[:, 0:ks, :], at_, -1.0, spare[:, 0:ks, :], ALU.add, ALU.add).then_inc(dve_step, 1)
                        dve.wait_ge(dve_step, at(dve_step, step.next()))
                        nc.vector.tensor_copy(plan.to[:, 0:ks, :], spare[:, 0:ks, :])
                        nc.vector.tensor_scalar(plan.back[:, 0:ks, :], spare[:, 0:ks, :], float(n_tiles * P - 1), None, ALU.min).then_inc(dve_step, 1)
                        dve.wait_ge(dve_step, at(dve_step, step.next()))
                        advance((dve_step, step.total))
            advance((loaded, 128), (logits, 1), (exps_made, 1), (pe_out, {"first": 7, "best": 35}.get(mode, 1)), (chosen, {"first": 2, "best": 1}.get(mode, 0)), (counted, {"first": 2, "best": 32}.get(mode, 0)), (kept_made, {"first": 2, "best": 1}.get(mode, 0)), (placed, 4), (place_out, 4))

        def experts(ff, w1d, w2d, func, plan, rows, gcol=None, b1d=None, b2d=None):
            n_exp, ks, n_tiles, stride = plan.n_exp, plan.ks, plan.n_tiles, plan.stride
            fc = ff // P
            put, result = a["expert_rows"], a["expert_results"][0:n_tiles * P, :]
            with ExitStack() as own:
                def tmp(name, shape, dt=F32):
                    return own.enter_context(sbuf("e_" + name, shape, dt))
                w1 = tmp("w1", [P, n_exp, KD, ff])
                w2 = tmp("w2", [P, n_exp, fc, D])
                w1_ = w1[:, :, :, :].rearrange("p e k f -> p (e k f)")
                w2_ = w2[:, :, :, :].rearrange("p e f d -> p (e f d)")
                xr = XN[:, 0:4, :]
                h = XN[:, 8:16, :].rearrange("p c d -> p (c d)").rearrange("p (i f) -> p i f", i=2)[:, :, 0:ff]
                xt = tmp("xt", [P, 2, KD, P])
                hT = tmp("hT", [P, fc, P])
                y = XN[:, 4:6, :]
                b1 = b2 = None
                if b1d is not None:
                    bs = tmp("bs", [1, n_exp, stride])
                    b_ = bs[:, :, :].rearrange("o e f -> o (e f)")
                with nc.Block() as block:
                    @block.sync
                    def _(sp):
                        w1v = w1d.rearrange("e (k p) f -> e p k f", p=P)
                        w2v = w2d.rearrange("e (f p) d -> e p f d", p=P)
                        for e in range(n_exp):
                            sp.dma_start(w1[:, e], w1v[e]).then_inc(loaded, 16)
                            sp.dma_start(w2[:, e], w2v[e]).then_inc(loaded, 16)
                        if b1d is not None:
                            sp.dma_start(bs[:, :, 0:ff], b1d.rearrange("(o e) f -> o e f", o=1)).then_inc(loaded, 16)
                            sp.dma_start(bs[:, :, ff:ff + D], b2d.rearrange("(o e) d -> o e d", o=1)).then_inc(loaded, 16)

                    @block.gpsimd
                    def _(pool):
                        for c in range(NT):
                            for i in range(ks):
                                nc.gpsimd.indirect_dma_start(put, bass.IndirectOffsetOnAxis(ap=plan.to[:, i, c:c + 1], axis=0),
                                                             rows[:, c, :], None).then_inc(rows_put, 16)
                        pool.wait_ge(rows_put, at(rows_put, 16 * ks * NT))
                n_loaded = 16 * (2 * n_exp + (2 if b1d is not None else 0))
                advance((rows_put, 16 * ks * NT))

                X_IN, Y_OUT, H_OUT, H_TURNED = 0, 1, 2, 6
                hb = max(1, ff // 512)
                tb = max(1, fc // 4)
                with nc.Block() as block:
                    @block.sync
                    def _(sp):
                        def fetch(t, slot):
                            sp.dma_start(xr[:, slot, :], put[bass.ds(t * P, P), :]).then_inc(x_in[slot], 16)

                        for t in range(4):
                            fetch(t, t)
                        with sp.Fori(0, n_tiles // 4 - 1) as q:
                            for u in range(4):
                                sp.wait_ge(x_turned, at(x_turned, 4 * q + u + 1))
                                fetch(4 * q + u + 4, u)

                    @block.tensor
                    def _(pe):
                        def turn_rows(t, slot, turn):
                            pe.wait_ge(x_in[slot], at(x_in[slot], 16 * turn + 16))
                            if not isinstance(t, int) or t > 0:
                                pe.wait_ge(xt_ready, at(xt_ready, t))
                            for k in range(KD):
                                ins = nc.tensor.transpose(ps[:, X_IN, k * P:(k + 1) * P], xr[:, slot, k * P:(k + 1) * P], ident[:, :])
                            ins.then_inc(x_turned, 1)

                        def hidden(t, par):
                            pe.wait_ge(xt_ready, at(xt_ready, t + 1))
                            if not isinstance(t, int) or t > 1:
                                pe.wait_ge(h_ready, at(h_ready, t - 1))
                            e = pe.value_load(plan.offset[0:1, bass.ds(t, 1)], min_val=0, max_val=(n_exp - 1) * stride)
                            for n in range(hb):
                                wd = min(512, ff)
                                for k in range(KD):
                                    ins = nc.tensor.matmul(ps[:, H_OUT + par * 2 + n, 0:wd], xt[:, par, k, :],
                                                           w1_[:, bass.ds(e + (k * ff + n * wd), wd)],
                                                           start=(k == 0), stop=(k == KD - 1 and b1d is None))
                                if b1d is not None:
                                    ins = nc.tensor.matmul(ps[:, H_OUT + par * 2 + n, 0:wd], ones[0:1, 0:P],
                                                           b_[0:1, bass.ds(e + n * wd, wd)], start=False, stop=True)
                            ins.then_inc(h_out, 1)

                        def turn_hidden(t, par):
                            pe.wait_ge(h_ready, at(h_ready, t + 1))
                            for n in range(tb):
                                if not isinstance(t, int) or t > 0:
                                    pe.wait_ge(hT_free, at(hT_free, tb * (t - 1) + n + 1))
                                for f in range(4):
                                    ins = nc.tensor.transpose(ps[:, H_TURNED + n, f * P:(f + 1) * P],
                                                              h[:, par, (4 * n + f) * P:(4 * n + f + 1) * P], ident[:, :])
                                ins.then_inc(h_turned, 1)

                        def results(t, par):
                            e = pe.value_load(plan.offset[0:1, bass.ds(t, 1)], min_val=0, max_val=(n_exp - 1) * stride)
                            if not isinstance(t, int) or t > 0:
                                pe.wait_ge(y_ready, at(y_ready, t))
                            for f in range(fc):
                                if f % 4 == 0:
                                    pe.wait_ge(hT_free, at(hT_free, tb * t + f // 4 + 1))
                                ins = nc.tensor.matmul(ps[:, Y_OUT, 0:D], hT[:, f, :], w2_[:, bass.ds(e + f * D, D)],
                                                       start=(f == 0), stop=(f == fc - 1 and b1d is None))
                            if b1d is not None:
                                ins = nc.tensor.matmul(ps[:, Y_OUT, 0:D], ones[0:1, 0:P], b_[0:1, bass.ds(e + ff, D)], start=False, stop=True)
                            ins.then_inc(y_out, 1)

                        turn_rows(0, 0, 0)
                        turn_rows(1, 1, 0)
                        pe.wait_ge(loaded, at(loaded, n_loaded))
                        hidden(0, 0)

                        def tile(t, u, turn):
                            hidden(t + 1, (u + 1) % 2)
                            turn_hidden(t, u % 2)
                            turn_rows(t + 2, (u + 2) % 4, turn)
                            results(t, u % 2)

                        for u in range(2):
                            tile(u, u, 0)
                        with pe.Fori(0, n_tiles // 4 - 1) as q:
                            for u in range(4):
                                tile(4 * q + u + 2, (u + 2) % 4, q + 1)
                        t = n_tiles - 2
                        hidden(t + 1, 1)
                        turn_hidden(t, 0)
                        results(t, 0)
                        turn_hidden(t + 1, 1)
                        results(t + 1, 1)

                    @block.scalar
                    def _(act):
                        def activate(t, par):
                            act.wait_ge(h_out, at(h_out, t + 1))
                            if not isinstance(t, int) or t > 1:
                                act.wait_ge(h_turned, at(h_turned, tb * (t - 1)))
                            nc.scalar.activation(h[:, par, :], ps[:, H_OUT + par * 2:H_OUT + par * 2 + hb, 0:min(512, ff)].rearrange("p n f -> p (n f)"),
                                                 func).then_inc(h_ready, 1)

                        for t in range(2):
                            activate(t, t)
                        with act.Fori(0, n_tiles // 2 - 1) as q:
                            for u in range(2):
                                activate(2 * q + u + 2, u)

                    @block.vector
                    def _(dve):
                        def turned_rows(t, par):
                            dve.wait_ge(x_turned, at(x_turned, t + 1))
                            if not isinstance(t, int) or t > 1:
                                dve.wait_ge(h_out, at(h_out, t - 1))
                            for k in range(KD):
                                src = ps[:, X_IN, k * P:(k + 1) * P]
                                if gcol is None:
                                    ins = nc.vector.tensor_copy(xt[:, par, k, :], src)
                                else:
                                    ins = nc.vector.tensor_scalar(xt[:, par, k, :], src, gcol[:, k:k + 1], None, ALU.mult)
                            ins.then_inc(xt_ready, 1)

                        def turned_hidden(t):
                            for n in range(tb):
                                dve.wait_ge(h_turned, at(h_turned, tb * t + n + 1))
                                if n == 0 and (not isinstance(t, int) or t > 0):
                                    dve.wait_ge(y_out, at(y_out, t))
                                nc.vector.tensor_copy(hT[:, 4 * n:4 * n + 4, :], ps[:, H_TURNED + n, :].rearrange("p (f q) -> p f q", f=4)).then_inc(hT_free, 1)

                        def results(t, par, stored):
                            dve.wait_ge(y_out, at(y_out, t + 1))
                            if stored is not None:
                                dve.wait_ge(y_stored[par], at(y_stored[par], 16 * stored))
                            nc.vector.tensor_copy(y[:, par, :], ps[:, Y_OUT, 0:D]).then_inc(y_ready, 1)

                        turned_rows(0, 0)
                        turned_rows(1, 1)
                        for t in range(2):
                            turned_hidden(t)
                            turned_rows(t + 2, t)
                            results(t, t, None)
                        with dve.Fori(0, (n_tiles - 4) // 2) as q:
                            for u in range(2):
                                t = 2 * q + u + 2
                                turned_hidden(t)
                                turned_rows(t + 2, u)
                                results(t, u, q + 1)
                        for t in (n_tiles - 2, n_tiles - 1):
                            turned_hidden(t)
                            results(t, t % 2, n_tiles // 2 - 1)

                    @block.gpsimd
                    def _(pool):
                        def store(t, par):
                            pool.wait_ge(y_ready, at(y_ready, t + 1))
                            nc.gpsimd.dma_start(result[bass.ds(t * P, P), :], y[:, par, :]).then_inc(y_stored[par], 16)

                        with pool.Fori(0, n_tiles // 2) as q:
                            for u in range(2):
                                store(2 * q + u, u)
                        for par in range(2):
                            pool.wait_ge(y_stored[par], at(y_stored[par], 8 * n_tiles))
                advance((loaded, n_loaded), *((x, 4 * n_tiles) for x in x_in), (x_turned, n_tiles), (xt_ready, n_tiles), (h_out, n_tiles), (h_ready, n_tiles),
                        (h_turned, tb * n_tiles), (hT_free, tb * n_tiles), (y_out, n_tiles), (y_ready, n_tiles), *((x, 8 * n_tiles) for x in y_stored))

                back = [XN, XT[:, :, :].rearrange("p k t -> p (k t)").rearrange("p (c d) -> p c d", c=NT)]
                with nc.Block() as block:
                    @block.gpsimd
                    def _(pool):
                        for c in range(NT):
                            for i in range(ks):
                                nc.gpsimd.indirect_dma_start(back[i][:, c, :], None, result,
                                                             bass.IndirectOffsetOnAxis(ap=plan.back[:, i, c:c + 1], axis=0)).then_inc(rows_in, 16)

                    @block.vector
                    def _(dve):
                        step = Steps()
                        for i in range(ks):
                            dve.wait_ge(rows_in, at(rows_in, 16 * ks * NT))
                            for c in range(NT):
                                ins = nc.vector.scalar_tensor_tensor(X[:, c, :], back[i][:, c, :], plan.weight[:, i, c:c + 1], X[:, c, :], ALU.mult, ALU.add)
                            ins.then_inc(dve_step, 1)
                            dve.wait_ge(dve_step, at(dve_step, step.next()))
                        advance((dve_step, step.total))
                advance((rows_in, 16 * ks * NT))

        def experts_layer0():
            with ExitStack() as own:
                def tmp(name, shape, dt=F32):
                    return own.enter_context(sbuf(name, shape, dt))
                plan = Plan(tmp, E8, 2, SLOT_TILES, KD * 1024)
                wr = tmp("wr0", [P, KD, E8])
                routers(wr, a["L0_ffn_router_w"])
                normalise(X, XN, True, 1e-5)
                route("first", E8, wr, tg[:, 4:5], plan, capacity=max(1, int(1.25 * T / E8 * 2)))
                experts(1024, a["L0_ffn_w1"], a["L0_ffn_w2"], ACT.Gelu, plan, XN)

        def routers(wr, src):
            with ExitStack() as own:
                rows = own.enter_context(sbuf("rrows", [E8, D], F32))
                with nc.Block() as block:
                    @block.sync
                    def _(sp):
                        sp.dma_start(rows[:, :], src).then_inc(loaded, 16)

                    @block.tensor
                    def _(pe):
                        pe.wait_ge(loaded, at(loaded, 16))
                        for k in range(KD):
                            ins = nc.tensor.transpose(ps[:, 0, k * E8:(k + 1) * E8], rows[:, k * P:(k + 1) * P], ident[0:E8, 0:E8])
                        ins.then_inc(pe_out, 1)

                    @block.scalar
                    def _(act):
                        act.wait_ge(pe_out, at(pe_out, 1))
                        nc.scalar.copy(wr[:, :, :], ps[:, 0, 0:KD * E8].rearrange("p (k e) -> p k e", k=KD))
                advance((loaded, 16), (pe_out, 1))

        def rope_forms(eng, dst, src, kind):
            def swap(out_):
                eng.tensor_scalar(out_.rearrange("p n h (i two) -> p n h i two", two=2)[:, :, :, :, 0],
                                  src.rearrange("p n h (i two) -> p n h i two", two=2)[:, :, :, :, 1], -1.0, None, ALU.mult)
                return eng.tensor_copy(out_.rearrange("p n h (i two) -> p n h i two", two=2)[:, :, :, :, 1],
                                       src.rearrange("p n h (i two) -> p n h i two", two=2)[:, :, :, :, 0])
            lo, hi = dst[:, :, :, 0:HD], dst[:, :, :, HD:2 * HD]
            if kind == "stack":
                eng.tensor_copy(lo, src)
                return swap(hi)
            if kind == "same":
                eng.tensor_copy(lo, src)
                return eng.tensor_copy(hi, src)
            swap(lo)
            return swap(hi)

        def context_attention(name, gate, wq, bq, wo, bo, KB, VM, VT, mask, rows, table=None):
            ch_n = H * rows // P
            gpc = P // rows // HG
            with ExitStack() as own:
                def tmp(nm_, shape, dt=F32):
                    return own.enter_context(sbuf(name + nm_, shape, dt))
                Q = tmp("Q", [P, ch_n, P])
                PR = tmp("PR", [P, NG, L, HG])
                nm = tmp("nm", [P, NG, HG])
                PT = tmp("PT", [P, H, P])
                PTT = tmp("PTT", [TR, NG, P])
                rs = tmp("rs", [P, H])
                AO = tmp("AO", [P, H, HD])
                AOT = tmp("AOT", [P, KD, P])
                with nc.Block() as block:
                    @block.tensor
                    def _(pe):
                        def scores(i, b, g):
                            pe.wait_ge(s_free, at(s_free, i * NG + g + 1))
                            for half in range(2):
                                lo = half * L // 2
                                ins = nc.tensor.matmul(ps[:, 2 * (g % 2) + half, 0:L // 2 * HG], Q[:, g // gpc, :],
                                                       KB[:, g, bass.ds(b, 1), lo:lo + L // 2, :].rearrange("p b l h -> p (b l h)"),
                                                       start=True, stop=True)
                            ins.then_inc(scores_made, 1)

                        def turn(g, i):
                            pe.wait_ge(probs, at(probs, i * NG + g + 1))
                            pe.wait_ge(pt_ready, at(pt_ready, i * NG + g))
                            for hh in range(HG):
                                ins = nc.tensor.transpose(ps[:, 4, hh * P:(hh + 1) * P], PR[:, g, 0:P, hh], ident[:, :])
                            ins.then_inc(turned, 1)
                            if g == 0:
                                pe.wait_ge(ptt_ready, at(ptt_ready, i))
                            ins = nc.tensor.transpose(ps[0:TR, 5, g * P:(g + 1) * P], PR[:, g, P:L, :].rearrange("p l h -> p (l h)"), ident[:, :])
                            ins.then_inc(tails_turned, 1)

                        with pe.Fori(0, NT) as i:
                            b = i // TPB
                            pe.wait_ge(x_used, at(x_used, i))
                            for ch in range(ch_n):
                                for k in range(KD):
                                    ins = nc.tensor.matmul(ps[:, 7, ch * P:(ch + 1) * P], wq[:, k, ch * P:(ch + 1) * P],
                                                           XT[:, k, bass.ds(i * P, P)], start=(k == 0), stop=(k == KD - 1 and bq is None))
                                if bq is not None:
                                    ins = nc.tensor.matmul(ps[:, 7, ch * P:(ch + 1) * P], bq[0:1, ch * P:(ch + 1) * P], ones[0:1, 0:P],
                                                           start=False, stop=True)
                            ins.then_inc(q_out, 1)
                            pe.wait_ge(q_ready, at(q_ready, i + 1))
                            scores(i, b, 0)
                            scores(i, b, 1)
                            for g in range(NG):
                                turn(g, i)
                                if g + 2 < NG:
                                    scores(i, b, g + 2)
                            pe.wait_ge(pt_ready, at(pt_ready, i * NG + NG))
                            pe.wait_ge(ptt_ready, at(ptt_ready, i + 1))
                            for g in range(NG):
                                nc.tensor.matmul(ps[:, 6, g * HG * VW:(g + 1) * HG * VW], PTT[:, g, :],
                                                 VT[:, bass.ds(b, 1), g * HG:(g + 1) * HG, :].rearrange("p b h w -> p (b h w)"),
                                                 start=(g == 0), stop=False, skip_group_check=True)
                            for h in range(H):
                                ins = nc.tensor.matmul(ps[:, 6, h * VW:(h + 1) * VW], PT[:, h, :],
                                                       VM[:, bass.ds(b, 1), h, :].rearrange("p b w -> p (b w)"),
                                                       start=False, stop=True, skip_group_check=True)
                            ins.then_inc(pv, 1)
                            pe.wait_ge(ao_ready, at(ao_ready, i + 1))
                            for k in range(KD):
                                ins = nc.tensor.transpose(ps[:, 7, k * P:(k + 1) * P],
                                                          AO[:, :, :].rearrange("p h w -> p (h w)")[:, k * P:(k + 1) * P], ident[:, :])
                            ins.then_inc(ao_turned, 1)
                            pe.wait_ge(aot_ready, at(aot_ready, i + 1))
                            for k in range(KD):
                                ins = nc.tensor.matmul(ps[:, 7, D:2 * D], AOT[:, k, :], wo[:, k, :], start=(k == 0), stop=(k == KD - 1 and bo is None))
                            if bo is not None:
                                ins = nc.tensor.matmul(ps[:, 7, D:2 * D], ones[0:1, 0:P], bo[0:1, :], start=False, stop=True)
                            ins.then_inc(y_out, 1)

                    @block.vector
                    def _(dve):
                        dve.sem_inc(s_free, 2)
                        step = Steps()
                        with dve.Fori(0, NT) as i:
                            step.turn(i, 1)
                            dve.wait_ge(q_out, at(q_out, i + 1))
                            src = ps[:, 7, 0:ch_n * P].rearrange("p (c q) -> p c q", c=ch_n)
                            if table is None:
                                ins = nc.vector.tensor_copy(Q[:, :, :], src)
                            else:
                                tb = table[:, bass.ds((i % TPB) * P, P)].unsqueeze(1).broadcast_to([P, ch_n, P])
                                ins = nc.vector.tensor_tensor(Q[:, :, :], src, tb, ALU.mult)
                            ins.then_inc(q_ready, 1)
                            for g in range(NG):
                                dve.wait_ge(scores_made, at(scores_made, i * NG + g + 1))
                                mrow = mask(i)
                                for half in range(2):
                                    lo = half * L // 2
                                    ins = nc.vector.tensor_tensor(PR[:, g, lo:lo + L // 2, :],
                                                                  ps[:, 2 * (g % 2) + half, 0:L // 2 * HG].rearrange("p (l h) -> p l h", h=HG),
                                                                  mrow[:, lo:lo + L // 2].unsqueeze(2).broadcast_to([P, L // 2, HG]), ALU.add)
                                ins.then_inc(s_free, 1)
                                dve.wait_ge(s_free, at(s_free, i * NG + g + 1 + 2))
                                nc.vector.tensor_reduce(nm[:, g, :], PR[:, g, :, :].rearrange("p l h -> p h l"), AX_X, ALU.max, negate=True).then_inc(max_ready, 1)
                            dve.wait_ge(tails_turned, at(tails_turned, i * NG + NG))
                            nc.vector.tensor_copy(PTT[:, :, :], ps[0:TR, 5, :].rearrange("p (g q) -> p g q", g=NG)).then_inc(ptt_ready, 1)
                            dve.wait_ge(pv, at(pv, i + 1))
                            o = ps[:, 6, 0:H * VW].rearrange("p (h w) -> p h w", h=H)
                            nc.vector.reciprocal(rs[:, :], o[:, :, HD]).then_inc(dve_step, 1)
                            dve.wait_ge(dve_step, at(dve_step, step.next()))
                            nc.vector.tensor_tensor(AO[:, :, :], o[:, :, 0:HD], rs[:, :].unsqueeze(2).broadcast_to([P, H, HD]), ALU.mult).then_inc(ao_ready, 1)
                            dve.wait_ge(y_out, at(y_out, i + 1))
                            x = X[:, bass.ds(i, 1), :].rearrange("p c d -> p (c d)")
                            nc.vector.scalar_tensor_tensor(x, ps[:, 7, D:2 * D], gate, x, ALU.mult, ALU.add).then_inc(x_used, 1)
                        step.end(NT)
                        advance((dve_step, step.total))

                    @block.scalar
                    def _(act):
                        with act.Fori(0, NT) as i:
                            def exps(g):
                                act.wait_ge(max_ready, at(max_ready, i * NG + g + 1))
                                for hh in range(HG):
                                    ins = nc.scalar.activation(PR[:, g, :, hh], PR[:, g, :, hh], ACT.Exp, bias=nm[:, g, hh:hh + 1])
                                ins.then_inc(probs, 1)

                            def copied(g):
                                act.wait_ge(turned, at(turned, i * NG + g + 1))
                                if g == 0:
                                    act.wait_ge(pv, at(pv, i))
                                nc.scalar.copy(PT[:, g * HG:(g + 1) * HG, :], ps[:, 4, :].rearrange("p (h q) -> p h q", h=HG)).then_inc(pt_ready, 1)

                            exps(0)
                            exps(1)
                            copied(0)
                            exps(2)
                            copied(1)
                            exps(3)
                            copied(2)
                            copied(3)
                            act.wait_ge(ao_turned, at(ao_turned, i + 1))
                            nc.scalar.copy(AOT[:, :, :], ps[:, 7, 0:D].rearrange("p (k q) -> p k q", k=KD)).then_inc(aot_ready, 1)
                advance((s_free, 2 + NT * NG), (scores_made, NT * NG), (probs, NT * NG), (pt_ready, NT * NG), (turned, NT * NG), (tails_turned, NT * NG), (ptt_ready, NT), (x_used, NT), (q_out, NT), (q_ready, NT), (pv, NT), (ao_ready, NT), (ao_turned, NT), (aot_ready, NT), (y_out, NT), (max_ready, NT * NG))

        def attention1():
            with ExitStack() as own:
                def tmp(name, shape, dt=F32):
                    return own.enter_context(sbuf(name, shape, dt))
                wqs = tmp("a1wqs", [P, KD, 2 * D])
                wo = tmp("a1wo", [P, KD, D])
                rowb = tmp("a1rowb", [1, 3, 2 * D])
                bo = tmp("a1bo", [1, D])
                KB = tmp("a1KB", [P, NG, B, L, HG])
                VM = tmp("a1VM", [P, B, H, VW])
                VT = tmp("a1VT", [TR, B, H, VW])
                mb = tmp("a1mask", [P, B, L])
                tq = tmp("a1tq", [P, S])
                with ExitStack() as own2:
                    def tmp2(name, shape, dt=F32):
                        return own2.enter_context(sbuf(name, shape, dt))
                    wq = tmp2("a1wq", [P, KD, D])
                    wkv = tmp2("a1wkv", [P, KD, 2 * D])
                    wv = tmp2("a1wv", [P, KD, D])
                    wkA = tmp2("a1wkA", [P, KD, 2 * D])
                    wkB = tmp2("a1wkB", [P, KD, 2 * D])
                    bq = tmp2("a1bq", [1, D])
                    bkv = tmp2("a1bkv", [1, 2 * D])
                    bv = tmp2("a1bv", [1, D])
                    m8 = tmp2("a1m8", [1, B * L], U8)
                    mf = tmp2("a1mf", [1, B * L])
                    cosk = tmp2("a1cos", [P, L])
                    sink = tmp2("a1sin", [P, L])
                    kr = tmp2("a1kr", [P, 2, B, L])
                    load_weights([
                        (wq[:, :, :], a["L1_xattn_Wq"].rearrange("(k p) d -> p k d", p=P)),
                        (wkv[:, :, :], a["L1_xattn_Wkv"].rearrange("(k p) d -> p k d", p=P)),
                        (wo[:, :, :], a["L1_xattn_Wo"].rearrange("(k p) d -> p k d", p=P)),
                        (bq[:, :], a["L1_xattn_bq"]), (bkv[:, :], a["L1_xattn_bkv"]), (bo[:, :], a["L1_xattn_bo"]),
                        (m8[:, :], a["ctx_mask"]), (cosk[:, :], a["cos1k"]), (sink[:, :], a["sin1k"]), (tq[:, :], a["stack1q"])])
                    with nc.Block() as block:
                        @block.vector
                        def _(dve):
                            def h4(t, p=P):
                                return t.rearrange("p n (h w) -> p n h w", h=H)
                            q1 = bq[:, :].unsqueeze(1)
                            k1 = bkv[:, 0:D].unsqueeze(1)
                            rope_forms(nc.vector, h4(wqs[:, :, :]), h4(wq[:, :, :]), "stack")
                            rope_forms(nc.vector, h4(wkA[:, :, :]), h4(wkv[:, :, 0:D]), "same")
                            rope_forms(nc.vector, h4(wkB[:, :, :]), h4(wkv[:, :, 0:D]), "swap")
                            rope_forms(nc.vector, h4(rowb[:, 0:1, :]), h4(q1), "stack")
                            rope_forms(nc.vector, h4(rowb[:, 1:2, :]), h4(k1), "same")
                            rope_forms(nc.vector, h4(rowb[:, 2:3, :]), h4(k1), "swap")
                            nc.vector.tensor_copy(wv[:, :, :], wkv[:, :, D:2 * D])
                            nc.vector.tensor_copy(bv[:, :], bkv[:, D:2 * D])
                            nc.vector.tensor_copy(mf[:, :], m8[:, :]).then_inc(cst, 1)
                            dve.wait_ge(cst, at(cst, 1))
                            nc.vector.tensor_scalar(mf[:, :], mf[:, :], -1.0, None, ALU.add).then_inc(cst, 1)
                            dve.wait_ge(pe_out, at(pe_out, 1))
                            nc.vector.tensor_scalar(mb[:, :, :], ps[:, 0, 0:B * L].rearrange("p (b l) -> p b l", b=B), 3e38, 10.0, ALU.mult, ALU.mult)

                        @block.tensor
                        def _(pe):
                            pe.wait_ge(cst, at(cst, 2))
                            nc.tensor.matmul(ps[:, 0, 0:B * L], ones[0:1, 0:P], mf[:, :], start=True, stop=True).then_inc(pe_out, 1)
                    advance((cst, 2), (pe_out, 1))
                    keys_values(KB, VM, VT, HG, hm4, 64 ** -0.5, wkA, wv, wkB, rowb[:, 1, :], rowb[:, 2, :], bv, cosk, sink, kr)
                normalise(X, XN, True, 1e-5)
                context_attention("a1", tg[:, 1:2], wqs, rowb[:, 0, :], wo, bo, KB, VM, VT,
                                  lambda i: mb[:, bass.ds(i // TPB, 1), :].rearrange("p b l -> p (b l)"), 32, tq)

        def attention3():
            with ExitStack() as own:
                def tmp(name, shape, dt=F32):
                    return own.enter_context(sbuf(name, shape, dt))
                w = [tmp(f"a3w{i}", [P, KD, D]) for i in range(4)]
                bias = [tmp(f"a3b{i}", [1, D]) for i in range(4)]
                KB = tmp("a3KB", [P, NG, B, L, HG])
                VM = tmp("a3VM", [P, B, H, VW])
                VT = tmp("a3VT", [TR, B, H, VW])
                m8 = tmp("a3m8", [P, NT, L], U8)
                mb = tmp("a3mask", [P, NT, L])
                load_weights([(w[i][:, :, :], a[f"L3_xattn_W{c}"].rearrange("(k p) d -> p k d", p=P)) for i, c in enumerate("qkvo")]
                             + [(bias[i][:, :], a[f"L3_xattn_b{c}"]) for i, c in enumerate("qkvo")]
                             + [(m8[:, :, :], a["q_mask"].rearrange("(t p) l -> p t l", p=P))])
                with nc.Block() as block:
                    @block.vector
                    def _(dve):
                        nc.vector.tensor_scalar(mb[:, :, :], m8[:, :, :], -1e15, None, ALU.mult)
                keys_values(KB, VM, VT, 8, hm8, HD ** -0.5, w[1], w[2], bkA=bias[1], bv=bias[2])
                normalise(X, XN, True, 1e-5)
                context_attention("a3", tg[:, 3:4], w[0], bias[0], w[3], bias[3], KB, VM, VT,
                                  lambda i: mb[:, bass.ds(i, 1), :].rearrange("p b l -> p (b l)"), 16)

        def block1():
            with ExitStack() as own:
                def tmp(name, shape, dt=F32):
                    return own.enter_context(sbuf(name, shape, dt))
                Z = XN
                gc = tmp("f1gc", [P, 2, KD])
                plan = Plan(tmp, E8, 2, CAPACITY1_TILES * E8, KD * 512)
                wr = tmp("wr1", [P, KD, E8])
                with ExitStack() as own2:
                    def tmp2(name, shape, dt=F32):
                        return own2.enter_context(sbuf(name, shape, dt))
                    scratch = tmp2("f1n", [P, NT, D])
                    grows = tmp2("f1g", [1, 2, D])
                    load_weights([(grows[:, 0, :], a["L1_ffn_g1"]), (grows[:, 1, :], a["L1_ffn_g2"]),
                                  (wr[:, :, :], a["L1_ffn_w_router"].rearrange("(k p) e -> p k e", p=P))])
                    with nc.Block() as block:
                        @block.tensor
                        def _(pe):
                            for i in range(2):
                                for k in range(KD):
                                    ins = nc.tensor.matmul(ps[:, 0, 2 * i + k:2 * i + k + 1], grows[:, i, k * P:(k + 1) * P], ones[0:1, 0:1],
                                                           start=True, stop=True)
                            ins.then_inc(pe_out, 1)

                        @block.scalar
                        def _(act):
                            act.wait_ge(pe_out, at(pe_out, 1))
                            nc.scalar.copy(gc[:, :, :], ps[:, 0, 0:4].rearrange("p (i k) -> p i k", i=2))
                    advance((pe_out, 1))
                    normalise(X, Z, True, 1e-5)
                    normalise(Z, scratch, False, 1e-6, gcol=gc[:, 0, :])
                self_attention(Z)
                rows = tmp("f1n2", [P, NT, D])
                normalise(Z, rows, False, 1e-6, gcol=gc[:, 1, :])
                route("best", E8, wr, tg[:, 5:6], plan, capacity=CAPACITY1)
                with nc.Block() as block:
                    @block.vector
                    def _(dve):
                        for c in range(NT):
                            nc.vector.scalar_tensor_tensor(X[:, c, :], Z[:, c, :], tg[:, 5:6], X[:, c, :], ALU.mult, ALU.add)
                experts(512, a["L1_ffn_w1"], a["L1_ffn_w2"], ACT.Relu, plan, rows, gc[:, 1, :])

        def self_attention(Z):
            with ExitStack() as own:
                def tmp(name, shape, dt=F32):
                    return own.enter_context(sbuf("s_" + name, shape, dt))
                wqs = tmp("wqs", [P, KD, 2 * D])
                wo = tmp("wo", [P, KD, D])
                tq = tmp("tq", [P, S])
                causal = tmp("causal", [P, P])
                KT = tmp("KT", [P, 4, T])
                V = tmp("V", [P, NT, H, VW])
                with ExitStack() as own2:
                    def tmp2(name, shape, dt=F32):
                        return own2.enter_context(sbuf("s_" + name, shape, dt))
                    w = tmp2("w", [P, KD, 3 * D])
                    wkA = tmp2("wkA", [P, KD, 2 * D])
                    wkB = tmp2("wkB", [P, KD, 2 * D])
                    cosk = tmp2("cos", [P, S])
                    sink = tmp2("sin", [P, S])
                    kr = tmp2("kr", [P, 2, 512])
                    load_weights([(w[:, :, :], a["L1_ffn_w_qkv"].rearrange("(k p) d -> p k d", p=P)),
                                  (wo[:, :, :], a["L1_ffn_w_o"].rearrange("(k p) d -> p k d", p=P)),
                                  (tq[:, :], a["stack2"]), (cosk[:, :], a["cos2"]), (sink[:, :], a["sin2"]),
                                  (causal[:, :], a["causal"])])
                    with nc.Block() as block:
                        @block.vector
                        def _(dve):
                            def h4(t):
                                return t.rearrange("p n (h w) -> p n h w", h=H)
                            rope_forms(nc.vector, h4(wqs[:, :, :]), h4(w[:, :, 0:D]), "stack")
                            rope_forms(nc.vector, h4(wkA[:, :, :]), h4(w[:, :, D:2 * D]), "same")
                            rope_forms(nc.vector, h4(wkB[:, :, :]), h4(w[:, :, D:2 * D]), "swap").then_inc(cst, 1)
                            dve.wait_ge(cst, at(cst, 1))
                            nc.vector.tensor_scalar(wqs[:, :, :], wqs[:, :, :], HD ** -0.5, None, ALU.mult)
                            nc.vector.memset(V[:, :, :, HD:VW], 1.0)
                    advance((cst, 1))
                    with nc.Block() as block:
                        @block.tensor
                        def _(pe):
                            for n in range(16):
                                ch, t = n // 4, n % 4
                                if n >= 2:
                                    pe.wait_ge(evac, at(evac, n - 1))
                                for bank, wk in ((n % 2, wkA), (2 + n % 2, wkB)):
                                    for k in range(KD):
                                        ins = nc.tensor.matmul(ps[:, bank, :], wk[:, k, ch * P:(ch + 1) * P], XT[:, k, t * 512:(t + 1) * 512],
                                                               start=(k == 0), stop=(k == KD - 1))
                                ins.then_inc(pe_out, 1)
                            for c in range(NT):
                                if c >= 4:
                                    pe.wait_ge(v_ready, at(v_ready, c - 3))
                                for k in range(KD):
                                    ins = nc.tensor.matmul(ps[:, 4 + c % 4, 0:D], XT[:, k, c * P:(c + 1) * P], w[:, k, 2 * D:3 * D],
                                                           start=(k == 0), stop=(k == KD - 1))
                                ins.then_inc(v_out, 1)

                        @block.vector
                        def _(dve):
                            step = Steps()
                            for n in range(16):
                                ch, t = n // 4, n % 4
                                dve.wait_ge(pe_out, at(pe_out, n + 1))
                                pos = slice((t % 2) * 512, (t % 2) * 512 + 512)
                                nc.vector.tensor_tensor(kr[:, 0, :], ps[:, n % 2, :], cosk[:, pos], ALU.mult)
                                ins = nc.vector.tensor_tensor(kr[:, 1, :], ps[:, 2 + n % 2, :], sink[:, pos], ALU.mult)
                                ins.then_inc(evac, 1)
                                dve.wait_ge(evac, at(evac, n + 1))
                                nc.vector.tensor_tensor(KT[:, ch, t * 512:(t + 1) * 512], kr[:, 0, :], kr[:, 1, :], ALU.add).then_inc(dve_step, 1)
                                dve.wait_ge(dve_step, at(dve_step, step.next()))
                            advance((dve_step, step.total))

                        @block.scalar
                        def _(act):
                            for c in range(NT):
                                act.wait_ge(v_out, at(v_out, c + 1))
                                nc.scalar.copy(V[:, c, :, 0:HD], ps[:, 4 + c % 4, 0:D].rearrange("p (h w) -> p h w", h=H)).then_inc(v_ready, 1)
                    advance((pe_out, 16), (evac, 16), (v_out, NT), (v_ready, NT))

                Q = tmp("Q", [P, 4, 4, P])
                PR = tmp("PR", [P, 2, S])
                PT = tmp("PT", [P, 2, TPB, P])
                nm = tmp("nm", [P, 2])
                rs = tmp("rs", [P, H])
                AO = tmp("AO", [P, H, HD])
                AOT = tmp("AOT", [P, KD, P])
                for j in range(TPB):
                    nk = j + 1
                    n_piece = -(-nk // 4)
                    with nc.Block() as block:
                        @block.tensor
                        def _(pe):
                            def scores(i, h):
                                if h >= 2:
                                    pe.wait_ge(probs, at(probs, i * H + h - 1))
                                for half in range(0, nk * P, 512):
                                    n = min(512, nk * P - half)
                                    ins = nc.tensor.matmul(ps[:, 2 * (h % 2) + half // 512, 0:n], Q[:, h // 4, h % 4, :],
                                                           KT[:, h // 4, bass.ds(i * S + half, n)], start=True, stop=True)
                                ins.then_inc(scores_made, 1)

                            def turn(i, h):
                                pe.wait_ge(probs, at(probs, i * H + h + 1))
                                for q in range(n_piece):
                                    piece = h * n_piece + q
                                    if piece >= 2:
                                        pe.wait_ge(pt_ready, at(pt_ready, i * H * n_piece + piece - 1))
                                    for t in range(4 * q, min(4 * q + 4, nk)):
                                        ins = nc.tensor.transpose(ps[:, 4 + piece % 2, (t % 4) * P:(t % 4 + 1) * P],
                                                                  PR[:, h % 2, t * P:(t + 1) * P], ident[:, :])
                                    ins.then_inc(turned, 1)

                            def values(i, h):
                                pe.wait_ge(pt_ready, at(pt_ready, i * H * n_piece + (h + 1) * n_piece))
                                for t in range(nk):
                                    ins = nc.tensor.matmul(ps[:, 6, h * VW:(h + 1) * VW], PT[:, h % 2, t, :],
                                                           V[:, bass.ds(i * TPB + t, 1), h, :].rearrange("p b w -> p (b w)"),
                                                           start=(t == 0), stop=(t == nk - 1))
                                ins.then_inc(pv, 1)

                            with pe.Fori(0, B) as i:
                                pe.wait_ge(x_used, at(x_used, i))
                                for ch in range(4):
                                    for k in range(KD):
                                        ins = nc.tensor.matmul(ps[:, 7, ch * P:(ch + 1) * P], wqs[:, k, ch * P:(ch + 1) * P],
                                                               XT[:, k, bass.ds(i * S + j * P, P)], start=(k == 0), stop=(k == KD - 1))
                                ins.then_inc(q_out, 1)
                                pe.wait_ge(q_ready, at(q_ready, i + 1))
                                scores(i, 0)
                                for h in range(H):
                                    if h + 1 < H:
                                        scores(i, h + 1)
                                    turn(i, h)
                                    if h >= 1:
                                        values(i, h - 1)
                                values(i, H - 1)
                                pe.wait_ge(ao_ready, at(ao_ready, i + 1))
                                for k in range(KD):
                                    ins = nc.tensor.transpose(ps[:, 7, k * P:(k + 1) * P],
                                                              AO[:, :, :].rearrange("p h w -> p (h w)")[:, k * P:(k + 1) * P], ident[:, :])
                                ins.then_inc(ao_turned, 1)
                                pe.wait_ge(aot_ready, at(aot_ready, i + 1))
                                for k in range(KD):
                                    ins = nc.tensor.matmul(ps[:, 7, D:2 * D], AOT[:, k, :], wo[:, k, :], start=(k == 0), stop=(k == KD - 1))
                                ins.then_inc(y_out, 1)

                        @block.vector
                        def _(dve):
                            step = Steps()
                            with dve.Fori(0, B) as i:
                                step.turn(i, H + 1)
                                dve.wait_ge(q_out, at(q_out, i + 1))
                                tb = tq[:, j * P:(j + 1) * P].unsqueeze(1).broadcast_to([P, 4, P])
                                for hh in range(4):
                                    ins = nc.vector.scalar_tensor_tensor(Q[:, :, hh, :], ps[:, 7, :].rearrange("p (c q) -> p c q", c=4),
                                                                         hm4[:, hh:hh + 1], tb, ALU.mult, ALU.mult)
                                ins.then_inc(q_ready, 1)

                                def copied(h):
                                    for q in range(n_piece):
                                        piece = h * n_piece + q
                                        n = min(4, nk - 4 * q)
                                        dve.wait_ge(turned, at(turned, i * H * n_piece + piece + 1))
                                        if q == 0 and h >= 2:
                                            dve.wait_ge(pv, at(pv, i * H + h - 1))
                                        nc.vector.tensor_copy(PT[:, h % 2, 4 * q:4 * q + n, :],
                                                                  ps[:, 4 + piece % 2, 0:n * P].rearrange("p (t q) -> p t q", t=n)).then_inc(pt_ready, 1)

                                for h in range(H):
                                    dve.wait_ge(scores_made, at(scores_made, i * H + h + 1))
                                    last = ps[:, 2 * (h % 2) + j // 4, (j % 4) * P:(j % 4 + 1) * P]
                                    nc.vector.tensor_tensor(last, last, causal[:, :], ALU.add).then_inc(dve_step, 1)
                                    dve.wait_ge(dve_step, at(dve_step, step.next()))
                                    src = (ps[:, 2 * (h % 2):2 * (h % 2) + 2, :].rearrange("p n q -> p (n q)"))[:, 0:nk * P]
                                    nc.vector.tensor_reduce(nm[:, h % 2:h % 2 + 1], src, AX_X, ALU.max, negate=True).then_inc(max_ready, 1)
                                    if h >= 1:
                                        copied(h - 1)
                                copied(H - 1)
                                dve.wait_ge(pv, at(pv, i * H + H))
                                o = ps[:, 6, 0:H * VW].rearrange("p (h w) -> p h w", h=H)
                                nc.vector.reciprocal(rs[:, :], o[:, :, HD]).then_inc(dve_step, 1)
                                dve.wait_ge(dve_step, at(dve_step, step.next()))
                                nc.vector.tensor_tensor(AO[:, :, :], o[:, :, 0:HD], rs[:, :].unsqueeze(2).broadcast_to([P, H, HD]), ALU.mult).then_inc(ao_ready, 1)
                                dve.wait_ge(y_out, at(y_out, i + 1))
                                z = Z[:, bass.ds(i * TPB + j, 1), :].rearrange("p c d -> p (c d)")
                                nc.vector.tensor_tensor(z, ps[:, 7, D:2 * D], z, ALU.add).then_inc(x_used, 1)
                            step.end(B)
                            advance((dve_step, step.total))

                        @block.scalar
                        def _(act):
                            with act.Fori(0, B) as i:
                                for h in range(H):
                                    act.wait_ge(max_ready, at(max_ready, i * H + h + 1))
                                    if h >= 2:
                                        act.wait_ge(turned, at(turned, i * H * n_piece + (h - 1) * n_piece))
                                    src = (ps[:, 2 * (h % 2):2 * (h % 2) + 2, :].rearrange("p n q -> p (n q)"))[:, 0:nk * P]
                                    nc.scalar.activation(PR[:, h % 2, 0:nk * P], src, ACT.Exp, bias=nm[:, h % 2:h % 2 + 1]).then_inc(probs, 1)
                                act.wait_ge(ao_turned, at(ao_turned, i + 1))
                                nc.scalar.copy(AOT[:, :, :], ps[:, 7, 0:D].rearrange("p (k q) -> p k q", k=KD)).then_inc(aot_ready, 1)
                    advance((scores_made, B * H), (probs, B * H), (turned, B * H * n_piece), (pt_ready, B * H * n_piece), (pv, B * H), (x_used, B), (q_out, B), (q_ready, B), (ao_ready, B), (ao_turned, B), (aot_ready, B), (y_out, B), (max_ready, B * H))

        def experts_layer2():
            with ExitStack() as own:
                plan = Plan(lambda n, shape, dt=F32: own.enter_context(sbuf(n, shape, dt)), E8, 2, SLOT_TILES, KD * 1024)
                wr = own.enter_context(sbuf("wr2", [P, KD, E8], F32))
                routers(wr, a["L2_ffn_router_w"])
                normalise(X, XN, True, 1e-5)
                route("top2", E8, wr, tg[:, 6:7], plan)
                experts(1024, a["L2_ffn_w1"], a["L2_ffn_w2"], ACT.Gelu, plan, XN)

        def experts_layer3():
            E4, FF = 4, 1024
            with ExitStack() as own:
                def tmp(name, shape, dt=F32):
                    return own.enter_context(sbuf(name, shape, dt))
                plan = Plan(tmp, E4, 1, T // P + E4, KD * FF)
                wr = tmp("wr3", [P, KD, E4])
                bg = tmp("bg3", [1, E4])
                load_weights([(wr[:, :, :], a["L3_ffn_Wg"].rearrange("(k p) e -> p k e", p=P)), (bg[:, :], a["L3_ffn_bg"])])
                normalise(X, XN, True, 1e-5)
                route("top1", E4, wr, tg[:, 7:8], plan, bias=bg)
                experts(FF, a["L3_ffn_W1"], a["L3_ffn_W2"], ACT.Gelu, plan, XN, None, a["L3_ffn_b1"], a["L3_ffn_b2"])

        def alignment():
            NC = 16
            W = S // NC
            NSTEP = L + NC - 1
            NF = -(-NSTEP // 4) * 4
            LN = 32 * B
            down = [max(l - 1, 0) for l in range(32)]
            up = [min(l + 1, 31) for l in range(32)]
            cost_d, path_d = a["dtw_cost"], a["dtw_path"]
            with ExitStack() as own:
                def tmp(name, shape, dt=F32):
                    return own.enter_context(sbuf("t_" + name, shape, dt))
                CD = tmp("CD", [LN, NF, W])
                NL = tmp("NL", [LN, NF, W + 1])
                CC = tmp("CC", [LN, NF, W])
                R = tmp("R", [LN, 4, W + 1])
                M = tmp("M", [LN, 4, W])
                PA = tmp("PA", [LN, NF, 2])
                V = tmp("V", [LN, 2, W + 2])
                seed = tmp("seed", [LN, W])
                hv = tmp("hv", [LN, 2])
                normalise(X, XN, True, 1e-5)
                SQ = XN[:, :, :].rearrange("p c d -> p (c d)").rearrange("p (k t) -> p k t", k=KD)
                with ExitStack() as own2:
                    def tmp2(name, shape, dt=F32):
                        return own2.enter_context(sbuf("t_" + name, shape, dt))
                    C2 = tmp2("C2", [P, KD, B, L])
                    DD = tmp2("DD", [P, 4, 512])
                    aa = tmp2("aa", [P, 2 * B])
                    with nc.Block() as block:
                        outs = [(b, r, n) for b in range(B) for r in range(2) for n in range(2)]

                        @block.scalar
                        def _(act):
                            for k in range(KD):
                                ins = nc.scalar.activation(SQ[:, k, :], XT[:, k, :], ACT.Square)
                            ins.then_inc(squares, 1)
                            for b in range(B):
                                nc.scalar.activation(DD[:, b, 0:D], CR[:, b, :], ACT.Square, accum_out=aa[:, b:b + 1])
                                ins = nc.scalar.activation(DD[0:TAIL, B + b, 0:D], CRT[:, b, :], ACT.Square, accum_out=aa[0:TAIL, B + b:B + b + 1])
                            ins.then_inc(norms, 1)
                            for m, (b, r, n) in enumerate(outs):
                                rows = TAIL if r else P
                                act.wait_ge(dist2, at(dist2, m + 1))
                                nc.scalar.activation(DD[0:rows, m % 4, :], DD[0:rows, m % 4, :], ACT.Sqrt).then_inc(dist, 1)

                        @block.tensor
                        def _(pe):
                            pe.wait_ge(squares, at(squares, 1))
                            pe.wait_ge(cst, at(cst, 1))
                            for m, (b, r, n) in enumerate(outs):
                                rows, lo, hi = (TAIL, P, L) if r else (P, 0, P)
                                for k in range(KD):
                                    cols = slice(b * S + n * 512, b * S + (n + 1) * 512)
                                    nc.tensor.matmul(ps[0:rows, m, :], C2[:, k, b, lo:hi], XT[:, k, cols], start=(k == 0), stop=False)
                                    ins = nc.tensor.matmul(ps[0:rows, m, :], ones[:, 0:rows], SQ[:, k, cols], start=False, stop=(k == KD - 1))
                                ins.then_inc(pe_out, 1)

                        @block.vector
                        def _(dve):
                            nc.vector.tensor_scalar(C2[:, :, :, :], CT[:, :, :, :], -2.0, None, ALU.mult).then_inc(cst, 1)
                            nc.vector.memset(CD[:, :, :], 0.0).then_inc(cleared, 1)
                            nc.vector.memset(NL[:, :, 0:1], 0.0)
                            dve.wait_ge(norms, at(norms, 1))
                            for m, (b, r, n) in enumerate(outs):
                                rows = TAIL if r else P
                                dve.wait_ge(pe_out, at(pe_out, m + 1))
                                if m >= 4:
                                    dve.wait_ge(dist_stored, at(dist_stored, 16 * (m - 3)))
                                nc.vector.tensor_scalar(DD[0:rows, m % 4, :], ps[0:rows, m, :], aa[0:rows, r * B + b:r * B + b + 1], 0.0,
                                                            ALU.add, ALU.max).then_inc(dist2, 1)

                        @block.sync
                        def _(sp):
                            for m, (b, r, n) in enumerate(outs):
                                rows, lo, hi = (TAIL, P, L) if r else (P, 0, P)
                                sp.wait_ge(dist, at(dist, m + 1))
                                sp.dma_start(cost_d[b * L + lo:b * L + hi, n * 512:(n + 1) * 512], DD[0:rows, m % 4, :]).then_inc(dist_stored, 16)
                                sp.wait_ge(dist_stored, at(dist_stored, 16 * (m + 1)))
                            sp.wait_ge(cleared, at(cleared, 1))
                            for b in range(B):
                                for k in range(NC):
                                    lane = 32 * b + 1 + k
                                    sp.dma_start(CD[lane:lane + 1, k:k + L, :],
                                                     cost_d[b * L:(b + 1) * L, k * W:(k + 1) * W].rearrange("(o i) w -> o i w", o=1)).then_inc(skewed, 16)
                            sp.dma_start(R[:, 3, :], a["dtw_start"]).then_inc(skewed, 16)
                            sp.dma_start(seed[:, :], a["dtw_end"]).then_inc(skewed, 16)
                            sp.wait_ge(skewed, at(skewed, 16 * (B * NC + 2)))
                    advance((squares, 1), (norms, 1), (dist2, 8), (dist, 8), (pe_out, 8), (cst, 1), (cleared, 1), (dist_stored, 16 * 8), (skewed, 16 * (B * NC + 2)))

                with nc.Block() as block:
                    @block.vector
                    def _(dve):
                        dve.sem_inc(row_free, 3)
                        step = Steps()
                        with dve.Fori(0, NF // 4) as t:
                            step.turn(t, 4)
                            for q in range(4):
                                prev = (q + 3) % 4
                                dve.wait_ge(row_free, at(row_free, t * 4 + q + 1))
                                nc.vector.tensor_tensor(M[:, q, :], R[:, prev, 0:W], R[:, prev, 1:W + 1], ALU.min)
                                nc.vector.stream_shuffle(R[:, q, 0:1], R[:, prev, W:W + 1], down).then_inc(dve_step, 1)
                                dve.wait_ge(dve_step, at(dve_step, step.next()))
                                nc.vector.tensor_tensor_scan(R[:, q, 1:W + 1], M[:, q, :],
                                                                 CD[:, bass.ds(t * 4 + q, 1), :].rearrange("p s w -> p (s w)"),
                                                                 R[:, q, 0:1], ALU.min, ALU.add).then_inc(row_made, 1)
                                dve.wait_ge(row_made, at(row_made, t * 4 + q + 1))
                        step.end(NF // 4)
                        dve.wait_ge(row_free, at(row_free, 3 + NF))
                        nc.vector.tensor_scalar(NL[:, :, 1:W + 1], NL[:, :, 1:W + 1], 0.0, None, ALU.is_ge)
                        nc.vector.tensor_scalar(CC[:, :, :], CC[:, :, :], 0.0, 2.0, ALU.is_gt, ALU.mult).then_inc(dve_step, 1)
                        dve.wait_ge(dve_step, at(dve_step, step.next()))
                        nc.vector.scalar_tensor_tensor(CC[:, :, :], CC[:, :, :], -1.0, NL[:, :, 1:W + 1], ALU.add, ALU.mult).then_inc(dve_step, 1)
                        dve.wait_ge(dve_step, at(dve_step, step.next()))
                        nc.vector.tensor_copy(PA[:, :, 1:2], CC[:, :, W - 1:W])
                        nc.vector.tensor_scalar(PA[:, :, 0:1], NL[:, :, W:W + 1], -1.0, 1.0, ALU.mult, ALU.add)
                        nc.vector.memset(V[:, :, :], 0.0).then_inc(dve_step, 1)
                        dve.wait_ge(dve_step, at(dve_step, step.next()))

                        def back(s, now):
                            p = CD[:, bass.ds(s, 1), :].rearrange("p s w -> p (s w)")
                            nl = NL[:, bass.ds(s, 1), :].rearrange("p s w -> p (s w)")
                            c = CC[:, bass.ds(s, 1), :].rearrange("p s w -> p (s w)")
                            pa = PA[:, bass.ds(s, 1), :].rearrange("p s w -> p (s w)")
                            nc.vector.tensor_tensor_scan(p, nl[:, 0:W], seed[:, :], V[:, now, 0:1],
                                                              ALU.is_lt, ALU.max).then_inc(dve_step, 1)
                            dve.wait_ge(dve_step, at(dve_step, step.next()))
                            nc.vector.tensor_scalar(hv[:, :], pa, p[:, W - 1:W], None, ALU.mult)
                            nc.vector.tensor_tensor(V[:, now, 2:W + 2], p, c, ALU.mult).then_inc(dve_step, 1)
                            dve.wait_ge(dve_step, at(dve_step, step.next()))
                            nc.vector.scalar_tensor_tensor(seed[:, :], V[:, now, 1:W + 1], -1.0, V[:, now, 2:W + 2], ALU.mult, ALU.max)
                            nc.vector.stream_shuffle(V[:, 1 - now, 0:2], hv[:, :], up).then_inc(dve_step, 1)
                            dve.wait_ge(dve_step, at(dve_step, step.next()))

                        back(NSTEP - 1, 1)
                        n = (NSTEP - 1) // 4
                        with dve.Fori(0, n) as t:
                            step.turn(t, 12)
                            for q in range(4):
                                back((n - 1 - t) * 4 + 3 - q, q % 2)
                        step.end(n)
                        advance((dve_step, step.total))

                    @block.gpsimd
                    def _(pool):
                        with pool.Fori(0, NF // 4) as t:
                            for q in range(4):
                                prev = (q + 3) % 4
                                pool.wait_ge(row_made, at(row_made, t * 4 + q + 1))
                                nc.gpsimd.tensor_tensor(NL[:, bass.ds(t * 4 + q, 1), 1:W + 1].rearrange("p s w -> p (s w)"),
                                                        R[:, q, 0:W][:, ::-1], M[:, q, :][:, ::-1], ALU.subtract)
                                nc.gpsimd.tensor_tensor(CC[:, bass.ds(t * 4 + q, 1), :].rearrange("p s w -> p (s w)"),
                                                            R[:, prev, 0:W][:, ::-1], R[:, prev, 1:W + 1][:, ::-1], ALU.subtract).then_inc(row_free, 1)
                advance((row_free, 3 + NF), (row_made, NF))

                RAWT = XN[0:TAIL, 0:8, :].rearrange("p c d -> p (c d)")
                TAILP = XN[0:TAIL, 8:16, :].rearrange("p c d -> p (c d)")
                with nc.Block() as block:
                    @block.sync
                    def _(sp):
                        for b in range(B):
                            for k in range(NC):
                                lane = 32 * b + 1 + k
                                sp.dma_start(path_d[b * L:(b + 1) * L, k * W:(k + 1) * W].rearrange("(o i) w -> o i w", o=1),
                                                 CD[lane:lane + 1, k:k + L, :]).then_inc(path_stored, 16)
                        sp.wait_ge(path_stored, at(path_stored, 16 * B * NC))
                        src = path_d.rearrange("(b i) t -> i b t", b=B)
                        sp.dma_start(XT[:, 0, :].rearrange("p (b t) -> p b t", b=B), src[0:P]).then_inc(loaded, 16)
                        sp.dma_start(RAWT.rearrange("p (b t) -> p b t", b=B), src[P:L]).then_inc(loaded, 16)

                    @block.tensor
                    def _(pe):
                        pe.wait_ge(turned, at(turned, 2))
                        for c in range(NT):
                            b = c // TPB
                            if c >= 8:
                                pe.wait_ge(x_used, at(x_used, c - 7))
                            nc.tensor.matmul(ps[:, c % 8, 0:D], XT[:, 1, c * P:(c + 1) * P], CR[:, b, :], start=True, stop=False)
                            nc.tensor.matmul(ps[:, c % 8, 0:D], TAILP[:, c * P:(c + 1) * P], CRT[:, b, :], start=False, stop=True).then_inc(pe_out, 1)

                    @block.vector
                    def _(dve):
                        dve.wait_ge(loaded, at(loaded, 32))
                        for to, raw in ((XT[:, 1, :], XT[:, 0, :]), (TAILP, RAWT)):
                            nc.vector.tensor_copy(to.rearrange("p (k w) -> p k w", w=W),
                                                      raw.rearrange("p (k w) -> p k w", w=W)[:, :, ::-1]).then_inc(turned, 1)
                        for c in range(NT):
                            dve.wait_ge(pe_out, at(pe_out, c + 1))
                            nc.vector.scalar_tensor_tensor(X[:, c, :], ps[:, c % 8, 0:D], tg[:, 2:3], X[:, c, :], ALU.mult, ALU.add).then_inc(x_used, 1)
                advance((path_stored, 16 * B * NC), (loaded, 32), (pe_out, NT), (x_used, NT), (turned, 2))

        def store():
            with nc.Block() as block:
                @block.sync
                def _(sp):
                    sp.dma_start(out.rearrange("(t p) d -> p t d", p=P), X[:, :, :]).then_inc(stored, 16)
                    sp.wait_ge(stored, at(stored, 16))

        prepare()
        for layer in (attention0, experts_layer0, attention1, block1, alignment, experts_layer2, attention3, experts_layer3):
            layer()
        store()


_INPUTS = ['g_xattn', 'g_ffn', 'L0_xattn_Wq', 'L0_xattn_Wk', 'L0_xattn_Wv', 'L0_xattn_Wo', 'L0_ffn_router_w', 'L0_ffn_w1', 'L0_ffn_w2', 'L1_xattn_Wq', 'L1_xattn_bq', 'L1_xattn_Wkv', 'L1_xattn_bkv', 'L1_xattn_Wo', 'L1_xattn_bo',
           'L3_xattn_Wq', 'L3_xattn_bq', 'L3_xattn_Wk', 'L3_xattn_bk', 'L3_xattn_Wv', 'L3_xattn_bv', 'L3_xattn_Wo', 'L3_xattn_bo',
           'L1_ffn_g1', 'L1_ffn_w_qkv', 'L1_ffn_w_o', 'L1_ffn_g2', 'L1_ffn_w_router', 'L1_ffn_w1', 'L1_ffn_w2', 'L2_ffn_router_w', 'L2_ffn_w1', 'L2_ffn_w2',
           'L3_ffn_W1', 'L3_ffn_b1', 'L3_ffn_W2', 'L3_ffn_b2', 'L3_ffn_Wg', 'L3_ffn_bg']


def kernel(**inputs):
    import concourse.bacc as _bacc
    from concourse.bass_utils import run_bass_kernel_spmd as _run

    nc = _bacc.Bacc("TRN2", target_bir_lowering=False, num_devices=1)
    arrays = {}
    arrays["x"] = np.ascontiguousarray(inputs["x"]).reshape(T, D)
    arrays["ctx"] = np.ascontiguousarray(inputs["ctx_1024"]).reshape(B * L, D)
    arrays["ctx_mask"] = np.ascontiguousarray(inputs["mask_BxS2_bf1"]).reshape(1, B * L)
    arrays["q_mask"] = np.ascontiguousarray(inputs["mask_Bx1xSxS2_bk1"]).reshape(T, L)
    for name in _INPUTS:
        v = np.ascontiguousarray(inputs[name])
        arrays[name] = v.reshape(1, -1) if v.ndim == 1 else v
    arrays.update(shape_constants())
    aps = {k: nc.dram_tensor(f"in_{k}_dram", v.shape, mybir.dt.uint8 if v.dtype == np.bool_ else mybir.dt.from_np(v.dtype), kind="ExternalInput").ap() for k, v in arrays.items()}
    aps["expert_rows"] = nc.dram_tensor("expert_rows", (SLOT_TILES * P + 2 * T, D), F32).ap()
    aps["expert_results"] = nc.dram_tensor("expert_results", (SLOT_TILES * P, D), F32).ap()
    for name in ("dtw_cost", "dtw_path"):
        aps[name] = nc.dram_tensor(name, (B * L, S), F32).ap()
    out = nc.dram_tensor("out_0_dram", (T, D), F32, kind="ExternalOutput").ap()
    build(nc, aps, out)
    r = _run(nc, [{f"in_{k}_dram": v for k, v in arrays.items()}], core_ids=[0])
    return np.asarray(r.results[0]["out_0_dram"]).reshape(B, S, D)
```

```python
from contextlib import ExitStack

import numpy as np

import concourse.bass as bass
from concourse import mybir

ALU = mybir.AluOpType
ACT = mybir.ActivationFunctionType
F32 = mybir.dt.float32
BF16 = mybir.dt.bfloat16
I32 = mybir.dt.int32
U8 = mybir.dt.uint8
AX_X = mybir.AxisListType.X

P = 128
B = 2
S = 1024
L = 154
D = 256
H = 16
HD = D // H
KD = D // P
T = B * S
NT = T // P
TPB = S // P
TAIL = L - P
HG = 4
NG = H // HG
TR = HG * TAIL
QW = S // 4
VW = HD + 1
E8 = 8
BIG = 1e30
CAPACITY1 = -(-2 * 512 * 2 * 5 // (4 * E8))
CAPACITY1_TILES = -(-CAPACITY1 // P)
SLOT_TILES = 2 * T // P + E8


class Plan:

    def __init__(self, tmp, n_exp, ks, n_tiles, stride, tables):
        self.tables = tables
        self.n_exp, self.ks, self.n_tiles, self.stride = n_exp, ks, n_tiles, stride
        self.to = tmp("to", [P, 2, NT], I32)
        self.back = tmp("back", [P, 2, NT], I32)
        self.weight = tmp("weight", [P, 2, NT])
        self.offset = tmp("offset", [1, n_tiles], I32)


class Steps:

    def __init__(self):
        self.total, self.earlier = 0, 0

    def next(self):
        self.total += 1
        return self.total + self.earlier

    def turn(self, i, per):
        self.first, self.earlier, self.per = self.total, i * per, per

    def end(self, turns):
        assert self.total - self.first == self.per, (self.total - self.first, self.per)
        self.total, self.earlier = self.first + self.per * turns, 0


def shape_constants():
    f = np.float32
    row = np.arange(P)
    ec, cc = row // NT, row % NT
    out = {
        "ident": np.eye(P, dtype=f),
        "earlier": ((ec[:, None] == ec[None, :]) & (cc[:, None] < cc[None, :])).astype(f),
        "sameexp": (ec[:, None] == ec[None, :]).astype(f),
        "experts_before": np.where((cc[:, None] == 0) & (ec[:, None] < ec[None, :]), f(P), f(0)).astype(f),
        "experts_through": np.where((cc[:, None] == 0) & (ec[:, None] <= ec[None, :]), f(P), f(0)).astype(f),
        "first_tile": (cc == 0).astype(f).reshape(P, 1),
        "tile_rows": np.broadcast_to(P * np.arange(SLOT_TILES, dtype=f), (P, SLOT_TILES)).copy(),
        "spare": (SLOT_TILES * P + row[:, None] + P * np.arange(2 * NT)[None, :] + 1).astype(f),
        "ones_row": np.ones((1, T), mybir.dt.np(BF16)),
        "spread": (np.arange(D)[None, :] // HD == np.arange(3 * H)[:, None] % H).astype(mybir.dt.np(BF16)),
        "hm8": (row[:, None] // 16 == np.arange(8)[None, :]).astype(f),
        "hm4": (row[:, None] // 32 == np.arange(4)[None, :]).astype(f),
        "causal": np.where(row[None, :] > row[:, None], f(-BIG), f(0)).astype(f),
        "tailmask": np.broadcast_to((np.arange(TR)[:, None] % HG == np.arange(H)[None, :] % HG)[:, :, None], (TR, H, VW)).astype(f).reshape(TR, H * VW),
        "firstof": np.broadcast_to((E8 - np.arange(E8))[None, :, None], (P, E8, NT)).astype(f).reshape(P, E8 * NT).copy(),
    }

    start = np.full((B, 32, S // 16 + 1), f(BIG))
    start[:, 1, 0] = 0
    out["dtw_start"] = start.reshape(B * 32, -1)
    end = np.zeros((B, 32, S // 16), f)
    end[:, 16, -1] = 1
    out["dtw_end"] = end.reshape(B * 32, -1)[:, ::-1]

    def rope(freq, pos):
        ang = (pos[:, None] * freq[None, :]).astype(f)
        return np.cos(ang).astype(f), np.sin(ang).astype(f)

    pair = (row % HD) // 2
    f1 = (f(1) / np.power(f(10000), np.arange(0, HD, 2, dtype=f) / f(HD))).astype(f)
    f2 = np.power(f(10000), f(-2) * (np.arange(HD // 2, dtype=f) / f(HD))).astype(f)
    for name, freq, pos in (
        ("1q", f1, f(10) * (np.arange(S, dtype=f) / f(S))),
        ("1k", f1, f(10) * (np.arange(L, dtype=f) / f(L))),
        ("2", f2, np.arange(S, dtype=f)),
    ):
        c, s = rope(freq, pos)
        c, s = c[:, pair].T, s[:, pair].T
        out["cos" + name], out["sin" + name] = np.ascontiguousarray(c), np.ascontiguousarray(s)
    return {k: np.ascontiguousarray(v) for k, v in out.items()}


def build(nc, a, out):
    ctx = ExitStack()

    def sb(name, shape, dt=F32):
        return ctx.enter_context(nc.sbuf_tensor(name, shape, dt))

    begun = {}

    def semaphore(name):
        handle = ctx.enter_context(nc.semaphore(name))
        begun[handle] = 0
        return handle

    def at(sem, n):
        return begun[sem] + n

    def advance(*grown):
        for sem, n in grown:
            begun[sem] += n

    dve_step = semaphore("dve_step")
    chosen = semaphore("chosen")
    cleared = semaphore("cleared")
    counted = semaphore("counted")
    cst = semaphore("cst")
    dist = semaphore("dist")
    dist2 = semaphore("dist2")
    dist_stored = semaphore("dist_stored")
    evac = semaphore("evac")
    exps_made = semaphore("exps_made")
    hT_free = semaphore("hT_free")
    h_out = semaphore("h_out")
    h_ready = semaphore("h_ready")
    kept_made = semaphore("kept_made")
    loaded = semaphore("loaded")
    logits = semaphore("logits")
    max_ready = semaphore("max_ready")
    norms = semaphore("norms")
    path_stored = semaphore("path_stored")
    pe_out = semaphore("pe_out")
    by_query_out = semaphore("by_query_out")
    max_found = semaphore("max_found")
    max_step = semaphore("max_step")
    split_ready = semaphore("split_ready")
    max_turned = semaphore("max_turned")
    max_stacked = semaphore("max_stacked")
    by_key_out = semaphore("by_key_out")
    exp_made = semaphore("exp_made")
    sums_out = semaphore("sums_out")
    recip_made = semaphore("recip_made")
    recip_stored = semaphore("recip_stored")
    sums_loaded = semaphore("sums_loaded")
    divided = semaphore("divided")
    f_ready = semaphore("f_ready")
    first_cast = semaphore("first_cast")
    rest_ready = semaphore("rest_ready")
    second_cast = semaphore("second_cast")
    parts_ready = semaphore("parts_ready")
    parts_stored = [semaphore(f"parts_stored{i}") for i in range(4)]
    stack_in = [semaphore(f"stack_in{i}") for i in range(2)]
    stack_zero = [semaphore(f"stack_zero{i}") for i in range(2)]
    sums_copied = semaphore("sums_copied")
    values_in = semaphore("values_in")
    heads_stored = [semaphore(f"heads_stored{i}") for i in range(2)]
    result_stored = [semaphore(f"result_stored{i}") for i in range(2)]
    att_in = [semaphore(f"att_in{i}") for i in range(KD)]
    weights_in = semaphore("weights_in")
    tables_in = semaphore("tables_in")
    member = semaphore("member")
    membership_kept = semaphore("membership_kept")
    placed = semaphore("placed")
    place_out = semaphore("place_out")
    rows_put = semaphore("rows_put")
    filled = semaphore("filled")
    rows_in = [semaphore(f"rows_in{i}") for i in range(NT // 4)]
    x_in = [semaphore(f"x_in{i}") for i in range(4)]
    x_turned = semaphore("x_turned")
    xt_ready = semaphore("xt_ready")
    h_turned = semaphore("h_turned")
    y_ready = semaphore("y_ready")
    y_stored = [semaphore(f"y_stored{i}") for i in range(2)]
    probs = semaphore("probs")
    pv = semaphore("pv")
    row_made = semaphore("row_made")
    row_free = semaphore("row_free")
    row_ready = semaphore("row_ready")
    scores_made = semaphore("scores_made")
    skewed = semaphore("skewed")
    squares = semaphore("squares")
    std_ready = semaphore("std_ready")
    stored = semaphore("stored")
    turned = semaphore("turned")
    v_out = semaphore("v_out")
    v_ready = semaphore("v_ready")
    v_scaled = semaphore("v_scaled")
    var_ready = semaphore("var_ready")
    x_loaded = semaphore("x_loaded")
    x_used = semaphore("x_used")
    y_out = semaphore("y_out")
    named = {}

    def sbuf(name, shape, dt=F32):
        named[name] = named.get(name, 0) + 1
        return nc.sbuf_tensor(name + (str(named[name]) if named[name] > 1 else ""), shape, dt)

    with ctx:
        ps = ctx.enter_context(nc.psum_tensor("banks", [P, 8, 512], F32))
        X = sb("X", [P, NT, D])
        XT = sb("XT", [P, KD, T])
        XN = sb("XN", [P, NT, D])
        ident = sb("ident", [P, P])
        identb = sb("identb", [P, P], BF16)
        ones = sb("ones", [P, 512])
        CR = sb("CR", [P, B, D])
        CRT = sb("CRT", [TAIL, B, D])
        CT = sb("CT", [P, KD, B, L])
        CTT = sb("CTT", [P, KD, B, TAIL, HG])
        tg = sb("tg", [P, 8])
        hm8 = sb("hm8", [P, 8])
        hm4 = sb("hm4", [P, 4])
        tailmask = sb("tailmask", [TR, H, VW])
        stats = sb("stats", [P, NT, 6])
        mv = sb("mv", [P, NT, 2])
        nrm = sb("nrm", [P, 4, NT])

        def prepare():
            with ExitStack() as own:
                def tmp(name, shape, dt=F32):
                    return own.enter_context(sbuf(name, shape, dt))
                grow = tmp("grow", [1, 8])
                with nc.Block() as block:
                    @block.sync
                    def _(sp):
                        sp.dma_start(CR[:, :, :], a["ctx"].rearrange("(b l) d -> l b d", b=B)[0:P]).then_inc(loaded, 16)
                        sp.dma_start(CRT[:, :, :], a["ctx"].rearrange("(b l) d -> l b d", b=B)[P:L]).then_inc(loaded, 16)
                        sp.dma_start(ident[:, :], a["ident"]).then_inc(loaded, 16)
                        sp.dma_start(hm8[:, :], a["hm8"]).then_inc(loaded, 16)
                        sp.dma_start(hm4[:, :], a["hm4"]).then_inc(loaded, 16)
                        sp.dma_start(tailmask[:, :, :], a["tailmask"].rearrange("p (h w) -> p h w", h=H)).then_inc(loaded, 16)
                        sp.dma_start(grow[:, 0:4], a["g_xattn"]).then_inc(loaded, 16)
                        sp.dma_start(grow[:, 4:8], a["g_ffn"]).then_inc(loaded, 16)
                        sp.dma_start(X[:, :, :], a["x"].rearrange("(t p) d -> p t d", p=P)).then_inc(x_loaded, 16)
                        sp.wait_ge(cleared, at(cleared, 1))
                        for lo in range(0, SLOT_TILES, NT):
                            n = min(NT, SLOT_TILES - lo)
                            sp.dma_start(a["expert_rows"][lo * P:(lo + n) * P, :].rearrange("(p c) d -> p c d", p=P), XN[:, 0:n, :]).then_inc(filled, 16)
                        sp.wait_ge(filled, at(filled, 16 * -(-SLOT_TILES // NT)))
                        sp.wait_ge(x_loaded, at(x_loaded, 16))

                    @block.gpsimd
                    def _(pool):
                        nc.gpsimd.memset(XN[:, :, :], 0.0).then_inc(cleared, 1)

                    @block.tensor
                    def _(pe):
                        pe.wait_ge(loaded, at(loaded, 16 * 8))
                        pe.wait_ge(cst, at(cst, 1))
                        for b in range(B):
                            for k in range(KD):
                                nc.tensor.transpose(ps[:, b, k * L:k * L + P], CR[:, b, k * P:(k + 1) * P], ident[:, :])
                                ins = nc.tensor.transpose(ps[:, b, k * L + P:(k + 1) * L], CRT[:, b, k * P:(k + 1) * P],
                                                          ident[0:TAIL, 0:TAIL])
                            ins.then_inc(pe_out, 1)
                        nc.tensor.matmul(ps[:, 2, 0:8], ones[0:1, 0:P], grow[:, :], start=True, stop=True).then_inc(pe_out, 1)

                    @block.vector
                    def _(dve):
                        nc.vector.memset(ones[:, :], 1.0).then_inc(cst, 1)

                    @block.scalar
                    def _(act):
                        for b in range(B):
                            act.wait_ge(pe_out, at(pe_out, b + 1))
                            src = ps[:, b, 0:KD * L].rearrange("p (k l) -> p k l", k=KD)
                            nc.scalar.copy(CT[:, :, b, :], src)
                            for k in range(KD):
                                nc.scalar.copy(CTT[:, k, b, :, :],
                                               src[:, k, P:L].unsqueeze(2).broadcast_to([P, TAIL, HG]))
                        nc.scalar.copy(identb[:, :], ident[:, :])
                        act.wait_ge(pe_out, at(pe_out, 3))
                        nc.scalar.activation(tg[:, :], ps[:, 2, 0:8], ACT.Tanh)
            advance((loaded, 16 * 8), (x_loaded, 16), (pe_out, 3), (cst, 1), (cleared, 1), (filled, 16 * -(-SLOT_TILES // NT)))

        def normalise(src, dst, mean, eps, gcol=None, also=None):
            with nc.Block() as block:
                @block.vector
                def _(dve):
                    step = Steps()
                    for c in range(NT):
                        ins = nc.vector.bn_stats(stats[:, c, :], src[:, c, :])
                    ins.then_inc(dve_step, 1)
                    dve.wait_ge(dve_step, at(dve_step, step.next()))
                    for c in range(NT):
                        ins = nc.vector.bn_aggr(mv[:, c, :], stats[:, c, :])
                    ins.then_inc(dve_step, 1)
                    dve.wait_ge(dve_step, at(dve_step, step.next()))
                    if mean:
                        nc.vector.tensor_scalar(nrm[:, 0, :], mv[:, :, 1], eps, None, ALU.add).then_inc(dve_step, 1)
                        dve.wait_ge(dve_step, at(dve_step, step.next()))
                    else:
                        nc.vector.tensor_tensor(nrm[:, 1, :], mv[:, :, 0], mv[:, :, 0], ALU.mult).then_inc(dve_step, 1)
                        dve.wait_ge(dve_step, at(dve_step, step.next()))
                        nc.vector.scalar_tensor_tensor(nrm[:, 0, :], mv[:, :, 1], eps, nrm[:, 1, :], ALU.add, ALU.add).then_inc(dve_step, 1)
                        dve.wait_ge(dve_step, at(dve_step, step.next()))
                    nc.vector.engine_nop().then_inc(var_ready, 1)
                    dve.wait_ge(std_ready, at(std_ready, 1))
                    nc.vector.reciprocal(nrm[:, 3, :], nrm[:, 2, :]).then_inc(dve_step, 1)
                    dve.wait_ge(dve_step, at(dve_step, step.next()))
                    for c in range(NT):
                        if mean:
                            ins = nc.vector.tensor_scalar(dst[:, c, :], src[:, c, :], mv[:, c, 0:1], nrm[:, 3, c:c + 1],
                                                          ALU.subtract, ALU.mult)
                        else:
                            ins = nc.vector.tensor_scalar(dst[:, c, :], src[:, c, :], nrm[:, 3, c:c + 1], None, ALU.mult)
                        ins.then_inc(row_ready, 1)
                    advance((dve_step, step.total))

                @block.scalar
                def _(act):
                    act.wait_ge(var_ready, at(var_ready, 1))
                    nc.scalar.activation(nrm[:, 2, :], nrm[:, 0, :], ACT.Sqrt).then_inc(std_ready, 1)
                    for c2 in range(NT // 2):
                        act.wait_ge(pe_out, at(pe_out, c2 + 1))
                        for k in range(KD):
                            src_ = ps[:, c2 % 4, k * D:(k + 1) * D]
                            d_ = XT[:, k, c2 * D:(c2 + 1) * D]
                            if gcol is None:
                                ins = nc.scalar.copy(d_, src_)
                            else:
                                ins = nc.scalar.activation(d_, src_, ACT.Copy, scale=gcol[:, k:k + 1])
                        ins.then_inc(evac, 1)

                @block.tensor
                def _(pe):
                    for c2 in range(NT // 2):
                        pe.wait_ge(row_ready, at(row_ready, 2 * c2 + 2))
                        if c2 >= 4:
                            pe.wait_ge(evac, at(evac, c2 - 3))
                        for k in range(KD):
                            for j in range(2):
                                ins = nc.tensor.transpose(ps[:, c2 % 4, k * D + j * P:k * D + (j + 1) * P],
                                                          dst[:, 2 * c2 + j, k * P:(k + 1) * P], ident[:, :])
                        ins.then_inc(pe_out, 1)
            advance((var_ready, 1), (std_ready, 1), (row_ready, NT), (pe_out, NT // 2), (evac, NT // 2))

        def load_weights(pairs, meanwhile=None):
            with nc.Block() as block:
                @block.sync
                def _(sp):
                    for dst, src in pairs:
                        sp.dma_start(dst, src).then_inc(loaded, 16)
            if meanwhile is not None:
                meanwhile()
            with nc.Block() as block:
                @block.sync
                def _(sp):
                    sp.wait_ge(loaded, at(loaded, 16 * len(pairs)))
            advance((loaded, 16 * len(pairs)))

        def transpose_weights(pairs):
            with nc.Block() as block:
                @block.tensor
                def _(pe):
                    for n, (dst, src) in enumerate(pairs):
                        if n >= 4:
                            pe.wait_ge(evac, at(evac, 2 * (n - 3)))
                        for ki in range(KD):
                            for ko in range(KD):
                                ins = nc.tensor.transpose(ps[:, (n % 4) * 2 + ki, ko * P:(ko + 1) * P],
                                                          src[:, ko, ki * P:(ki + 1) * P], ident[:, :])
                            ins.then_inc(pe_out, 1)

                @block.scalar
                def _(act):
                    for n, (dst, src) in enumerate(pairs):
                        for ki in range(KD):
                            act.wait_ge(pe_out, at(pe_out, 2 * n + ki + 1))
                            nc.scalar.copy(dst[:, ki, :], ps[:, (n % 4) * 2 + ki, 0:D]).then_inc(evac, 1)
            advance((pe_out, 2 * len(pairs)), (evac, 2 * len(pairs)))

        def keys_values(KB, VM, VT, heads, mask, scale, wkA, wv, wkB=None, bkA=None, bkB=None, bv=None, cosk=None, sink=None, kr=None):
            ch_n = H // heads
            with nc.Block() as block:
                @block.tensor
                def _(pe):
                    flat = CT[:, :, :, :].rearrange("p k b l -> p k (b l)")
                    for ch in range(ch_n):
                        if ch >= 2:
                            pe.wait_ge(evac, at(evac, ch - 1))
                        for bank, w, bias in ((ch % 2, wkA, bkA), (2 + ch % 2, wkB, bkB)):
                            if w is None:
                                continue
                            for k in range(KD):
                                ins = nc.tensor.matmul(ps[:, bank, 0:B * L], w[:, k, ch * P:(ch + 1) * P], flat[:, k, :],
                                                       start=(k == 0), stop=(k == KD - 1 and bias is None))
                            if bias is not None:
                                ins = nc.tensor.matmul(ps[:, bank, 0:B * L], bias[0:1, ch * P:(ch + 1) * P], ones[0:1, 0:B * L],
                                                       start=False, stop=True)
                        ins.then_inc(pe_out, 1)
                    for b in range(B):
                        for k in range(KD):
                            ins = nc.tensor.matmul(ps[:, 4 + b, 0:D], CT[:, k, b, 0:P], wv[:, k, :],
                                                   start=(k == 0), stop=(k == KD - 1 and bv is None))
                        if bv is not None:
                            ins = nc.tensor.matmul(ps[:, 4 + b, 0:D], ones[0:1, 0:P], bv[0:1, :], start=False, stop=True)
                        ins.then_inc(v_out, 1)
                        for k in range(KD):
                            ins = nc.tensor.matmul(ps[0:TR, 6 + b, 0:D], CTT[:, k, b, :, :].rearrange("p l g -> p (l g)"), wv[:, k, :],
                                                   start=(k == 0), stop=(k == KD - 1 and bv is None))
                        if bv is not None:
                            ins = nc.tensor.matmul(ps[0:TR, 6 + b, 0:D], ones[0:1, 0:TR], bv[0:1, :], start=False, stop=True)
                        ins.then_inc(v_out, 1)

                @block.vector
                def _(dve):
                    step = Steps()
                    for ch in range(ch_n):
                        dve.wait_ge(pe_out, at(pe_out, ch + 1))
                        src = ps[:, ch % 2, 0:B * L].rearrange("p (b l) -> p b l", b=B)
                        if cosk is not None:
                            cb = cosk[:, :].unsqueeze(1).broadcast_to([P, B, L])
                            sb_ = sink[:, :].unsqueeze(1).broadcast_to([P, B, L])
                            nc.vector.tensor_tensor(kr[:, 0], src, cb, ALU.mult)
                            nc.vector.tensor_tensor(kr[:, 1], ps[:, 2 + ch % 2, 0:B * L].rearrange("p (b l) -> p b l", b=B),
                                                         sb_, ALU.mult).then_inc(dve_step, 1)
                            dve.wait_ge(dve_step, at(dve_step, step.next()))
                            nc.vector.tensor_tensor(kr[:, 0], kr[:, 0], kr[:, 1], ALU.add).then_inc(dve_step, 1)
                            dve.wait_ge(dve_step, at(dve_step, step.next()))
                            src = kr[:, 0]
                        for hh in range(heads):
                            ins = nc.vector.tensor_scalar(KB[:, (ch * heads + hh) // HG, :, :, hh % HG], src, mask[:, hh:hh + 1], scale, ALU.mult, ALU.mult)
                        ins.then_inc(evac, 1)
                        dve.wait_ge(evac, at(evac, ch + 1))
                    nc.vector.memset(VM[:, :, :, HD:VW], 1.0)
                    for b in range(B):
                        dve.wait_ge(v_out, at(v_out, 2 * b + 1))
                        nc.vector.tensor_copy(VM[:, b, :, 0:HD], ps[:, 4 + b, 0:D].rearrange("p (h w) -> p h w", h=H))
                        dve.wait_ge(v_out, at(v_out, 2 * b + 2))
                        nc.vector.tensor_tensor(VT[:, b, :, 0:HD], ps[0:TR, 6 + b, 0:D].rearrange("p (h w) -> p h w", h=H),
                                                tailmask[:, :, 0:HD], ALU.mult)
                        nc.vector.tensor_copy(VT[:, b, :, HD:VW], tailmask[:, :, HD:VW])
                    advance((dve_step, step.total))
            advance((pe_out, ch_n), (evac, ch_n), (v_out, 2 * B))

        def attention0():
            with ExitStack() as own:
                def tmp(name, shape, dt=F32):
                    return own.enter_context(sbuf(name, shape, dt))
                W = [tmp(f"a0w{i}", [P, KD, D]) for i in range(4)]
                KB = tmp("a0KB", [P, NG, B, L, HG])
                VM = tmp("a0VM", [P, B, H, VW])
                VT = tmp("a0VT", [TR, B, H, VW])
                with ExitStack() as own2:
                    R = [own2.enter_context(sbuf(f"a0r{i}", [P, KD, D], F32)) for i in range(4)]
                    load_weights([(R[i][:, :, :], a[f"L0_xattn_W{c}"].rearrange("(k p) d -> p k d", p=P))
                                  for i, c in enumerate("qkvo")])
                    transpose_weights([(W[i], R[i]) for i in range(4)])
                wq, wk, wv, wo = W
                keys_values(KB, VM, VT, 8, hm8, float(D) ** -0.5, wk, wv)
                normalise(X, XN, True, 1e-5)
                QT = tmp("a0QT", [P, KD, T])
                with nc.Block() as block:
                    @block.tensor
                    def _(pe):
                        for m in range(KD):
                            for n in range(4):
                                i = 4 * m + n
                                for k in range(KD):
                                    ins = nc.tensor.matmul(ps[:, i, :], wq[:, k, m * P:(m + 1) * P], XT[:, k, n * 512:(n + 1) * 512],
                                                           start=(k == 0), stop=(k == KD - 1))
                                ins.then_inc(pe_out, 1)

                    @block.scalar
                    def _(act):
                        for i in range(8):
                            act.wait_ge(pe_out, at(pe_out, i + 1))
                            nc.scalar.copy(QT[:, i // 4, (i % 4) * 512:(i % 4 + 1) * 512], ps[:, i, :])
                advance((pe_out, 8))

                EX = tmp("a0E", [P, H + NG, S])
                nm = tmp("a0nm", [P, H + NG])
                sm = tmp("a0sm", [P, H + NG])
                rc = tmp("a0rc", [P, H + NG])
                VB = tmp("a0VB", [P, H, VW])
                VTB = tmp("a0VTB", [TR, H, VW])
                SB = [tmp(f"a0SB{i}", [3 * 32 + VW, 512]) for i in range(2)]
                rows_of = a["attended"].rearrange("(h b g r) c -> h b r g c", h=H, b=B, g=4)
                units = [(u, P, u // 8, u % 8) for u in range(H)] + [(H + g, TR, g // 2, g) for g in range(NG)]
                for b in range(B):
                    with nc.Block() as block:
                        @block.tensor
                        def _(pe):
                            for u, rows, m, hh in units:
                                if u >= 2:
                                    pe.wait_ge(probs, at(probs, u - 1))
                                lhs = (KB[:, u // HG, b, 0:P, u % HG] if u < H else
                                       KB[:, hh, b, P:L, :].rearrange("p l h -> p (l h)"))
                                for n in range(2):
                                    ins = nc.tensor.matmul(ps[0:rows, 2 * (u % 2) + n, :], lhs,
                                                           QT[:, m, b * S + n * 512:b * S + (n + 1) * 512], start=True, stop=True)
                                ins.then_inc(scores_made, 1)
                            pe.wait_ge(v_scaled, at(v_scaled, 1))
                            for i in range(8):
                                g4, n = i // 2, i % 2
                                if i >= 4:
                                    pe.wait_ge(sums_copied, at(sums_copied, i - 3))
                                for lhs, rows, last in ((VB, P, False), (VTB, TR, True)):
                                    for g in range(HG):
                                        h = HG * g4 + g
                                        ins = nc.tensor.matmul(ps[32 * g:32 * g + VW, 4 + i % 4, :], lhs[0:rows, h, :],
                                                               EX[0:rows, H + g4 if last else h, n * 512:(n + 1) * 512], start=not last, stop=last)
                                ins.then_inc(pv, 1)

                        @block.vector
                        def _(dve):
                            step = Steps()
                            for u, rows, m, hh in units:
                                dve.wait_ge(scores_made, at(scores_made, u + 1))
                                nc.vector.tensor_reduce(nm[0:rows, u:u + 1], ps[0:rows, 2 * (u % 2):2 * (u % 2) + 2, :],
                                                            mybir.AxisListType.XY, ALU.max, negate=True).then_inc(max_ready, 1)
                            dve.wait_ge(probs, at(probs, H + NG))
                            nc.vector.reciprocal(rc[:, 0:H], sm[:, 0:H])
                            nc.vector.reciprocal(rc[0:TR, H:], sm[0:TR, H:]).then_inc(dve_step, 1)
                            dve.wait_ge(dve_step, at(dve_step, step.next()))
                            nc.vector.tensor_tensor(VB[:, :, :], VM[:, b, :, :], rc[:, 0:H].unsqueeze(2).broadcast_to([P, H, VW]), ALU.mult)
                            nc.vector.tensor_tensor(VTB[:, :, :].rearrange("p (g h) w -> p g (h w)", h=HG), VT[:, b, :, :].rearrange("p (g h) w -> p g (h w)", h=HG),
                                                    rc[0:TR, H:H + NG].unsqueeze(2).broadcast_to([TR, NG, HG * VW]), ALU.mult).then_inc(v_scaled, 1)
                            for i in range(8):
                                dve.wait_ge(pv, at(pv, i + 1))
                                if i >= 2:
                                    dve.wait_ge(heads_stored[i % 2], at(heads_stored[i % 2], 64 * (i // 2)))
                                nc.vector.tensor_copy(SB[i % 2][:, :], ps[0:3 * 32 + VW, 4 + i % 4, :]).then_inc(sums_copied, 1)
                            advance((dve_step, step.total))

                        @block.sync
                        def _(sp):
                            for i in range(8):
                                sp.wait_ge(sums_copied, at(sums_copied, i + 1))
                                for g in range(HG):
                                    sp.dma_start(rows_of[HG * (i // 2) + g, b, 0:VW, 2 * (i % 2):2 * (i % 2) + 2, :],
                                                 SB[i % 2][32 * g:32 * g + VW, :].rearrange("v (g c) -> v g c", g=2)).then_inc(heads_stored[i % 2], 64 // HG)
                            for j in range(2):
                                sp.wait_ge(heads_stored[j], at(heads_stored[j], 256))

                        @block.scalar
                        def _(act):
                            for u, rows, m, hh in units:
                                act.wait_ge(max_ready, at(max_ready, u + 1))
                                nc.scalar.activation(EX[0:rows, u, :].rearrange("p (n q) -> p n q", n=2), ps[0:rows, 2 * (u % 2):2 * (u % 2) + 2, :],
                                                         ACT.Exp, bias=nm[0:rows, u:u + 1], accum_out=sm[0:rows, u:u + 1]).then_inc(probs, 1)
                    advance((scores_made, H + NG), (max_ready, H + NG), (probs, H + NG), (v_scaled, 1), (pv, 8), (sums_copied, 8),
                            *((s_, 256) for s_ in heads_stored))
                project_out(wo, None, tg[:, 0:1])

        def route(mode, n_exp, wr, gate, plan, bias=None, capacity=None):
            R = n_exp * NT
            ks, n_tiles = plan.ks, plan.n_tiles
            with ExitStack() as own:
                def tmp(name, shape, dt=F32):
                    return own.enter_context(sbuf("r_" + name, shape, dt))
                pr = tmp("pr", [P, n_exp, NT])
                w = tmp("w", [P, n_exp, NT])
                oh = [tmp(f"oh{i}", [P, n_exp, NT]) for i in range(2)]
                m = tmp("m", [P, 8, NT])
                ohT = [tmp(f"ohT{i}", [P, P]) for i in range(2)]
                cs = [tmp(f"cs{i}", [P, P]) for i in range(2)]
                keep = [tmp(f"keep{i}", [P, P]) for i in range(2)]
                col = tmp("col", [P, 8])
                thr = tmp("thr", [P, 5], I32)
                reached = tmp("reached", [P, 4])
                G = tmp("G", [P, n_exp, NT])
                taken = tmp("taken", [P, n_exp, NT])
                part = tmp("part", [P, n_exp, NT])
                firstof, earlier, sameexp, before, through, first_tile, tile_rows, spare = plan.tables
                begun_tiles = tmp("begun_tiles", [P, SLOT_TILES])
                place = tmp("place", [P, 2, NT])

                def bc(v):
                    return v.unsqueeze(1).broadcast_to([P, n_exp, NT])

                def by_tile(v):
                    return v.rearrange("p e c -> p c e")

                with nc.Block() as block:
                    @block.tensor
                    def _(pe):
                        for c in range(NT):
                            for k in range(KD):
                                ins = nc.tensor.matmul(ps[:, 0, c * n_exp:(c + 1) * n_exp], XT[:, k, c * P:(c + 1) * P], wr[:, k, :],
                                                       start=(k == 0), stop=(k == KD - 1 and bias is None))
                            if bias is not None:
                                ins = nc.tensor.matmul(ps[:, 0, c * n_exp:(c + 1) * n_exp], ones[0:1, 0:P], bias[0:1, :],
                                                       start=False, stop=True)
                        ins.then_inc(pe_out, 1)
                        if mode == "first":
                            pe.wait_ge(tables_in, at(tables_in, 128))
                            for i in range(2):
                                pe.wait_ge(chosen, at(chosen, i + 1))
                                nc.tensor.transpose(ps[:, 1 + i, 0:P], oh[i][:, :, :].rearrange("p e c -> p (e c)"), ident[:, :]).then_inc(pe_out, 1)
                            for i in range(2):
                                pe.wait_ge(counted, at(counted, i + 1))
                                nc.tensor.matmul(ps[:, 3 + i, 0:1], earlier[:, :], cs[i][:, P - 1:P], start=True, stop=True).then_inc(pe_out, 1)
                            for i in range(2):
                                pe.wait_ge(kept_made, at(kept_made, i + 1))
                                nc.tensor.transpose(ps[:, 5 + i, 0:P], keep[i][:, :], ident[:, :]).then_inc(pe_out, 1)
                        if mode == "best":
                            pe.wait_ge(tables_in, at(tables_in, 128))
                            pe.wait_ge(chosen, at(chosen, 1))
                            nc.tensor.transpose(ps[:, 1, 0:P], w[:, :, :].rearrange("p e c -> p (e c)"), ident[:, :]).then_inc(pe_out, 1)
                            for i in range(16):
                                pe.wait_ge(counted, at(counted, i + 1))
                                nc.tensor.matmul(ps[:, 2 + i % 2, 0:3], sameexp[:, :], col[:, 5:8], start=True, stop=True).then_inc(pe_out, 1)
                            pe.wait_ge(counted, at(counted, 17))
                            nc.tensor.matmul(ps[:, 4, 0:1], earlier[:, :], cs[0][:, P - 1:P], start=True, stop=True).then_inc(pe_out, 1)
                            pe.wait_ge(kept_made, at(kept_made, 1))
                            nc.tensor.transpose(ps[:, 5, 0:P], keep[0][:, :], ident[:, :]).then_inc(pe_out, 1)

                        if mode == "top2" or mode == "top1":
                            pe.wait_ge(tables_in, at(tables_in, 128))
                        pe.wait_ge(placed, at(placed, 1))
                        nc.tensor.transpose(ps[0:R, 7, 0:P], taken[:, :, :].rearrange("p e c -> p (e c)"), ident[:, :]).then_inc(place_out, 1)
                        pe.wait_ge(placed, at(placed, 2))
                        nc.tensor.matmul(ps[0:R, 7, P:P + 1], earlier[0:R, 0:R], cs[0][0:R, P - 1:P], start=True, stop=True)
                        nc.tensor.matmul(ps[0:R, 7, P + 1:P + 2], sameexp[0:R, 0:R], cs[0][0:R, P - 1:P], start=True, stop=True).then_inc(place_out, 1)
                        pe.wait_ge(placed, at(placed, 3))
                        nc.tensor.matmul(ps[0:R, 7, P + 2:P + 3], before[0:R, 0:R], col[0:R, 2:3], start=True, stop=True)
                        nc.tensor.matmul(ps[0:R, 7, P + 3:P + 4], through[0:R, 0:R], col[0:R, 2:3], start=True, stop=True).then_inc(place_out, 1)
                        pe.wait_ge(placed, at(placed, 4))
                        nc.tensor.transpose(ps[:, 7, 0:R], cs[1][0:R, :], ident[0:R, 0:R])
                        nc.tensor.matmul(ps[0:1, 7, 256:256 + n_tiles], first_tile[0:R, 0:1], begun_tiles[0:R, 0:n_tiles],
                                         start=True, stop=True).then_inc(place_out, 1)

                    @block.scalar
                    def _(act):
                        act.wait_ge(logits, at(logits, 1))
                        nc.scalar.activation(pr[:, :, :], pr[:, :, :], ACT.Exp).then_inc(exps_made, 1)

                    @block.vector
                    def _(dve):
                        step = Steps()
                        dve.wait_ge(pe_out, at(pe_out, 1))
                        nc.vector.tensor_copy(pr[:, :, :], ps[:, 0, 0:NT * n_exp].rearrange("p (c e) -> p e c", c=NT)).then_inc(dve_step, 1)
                        dve.wait_ge(dve_step, at(dve_step, step.next()))
                        nc.vector.tensor_reduce(m[:, 0, :], by_tile(pr[:, :, :]), AX_X, ALU.max).then_inc(dve_step, 1)
                        dve.wait_ge(dve_step, at(dve_step, step.next()))
                        nc.vector.tensor_tensor(pr[:, :, :], pr[:, :, :], bc(m[:, 0, :]), ALU.subtract).then_inc(logits, 1)
                        dve.wait_ge(exps_made, at(exps_made, 1))
                        nc.vector.tensor_reduce(m[:, 0, :], by_tile(pr[:, :, :]), AX_X, ALU.add).then_inc(dve_step, 1)
                        dve.wait_ge(dve_step, at(dve_step, step.next()))
                        nc.vector.reciprocal(m[:, 1, :], m[:, 0, :]).then_inc(dve_step, 1)
                        dve.wait_ge(dve_step, at(dve_step, step.next()))
                        nc.vector.tensor_tensor(pr[:, :, :], pr[:, :, :], bc(m[:, 1, :]), ALU.mult).then_inc(dve_step, 1)
                        dve.wait_ge(dve_step, at(dve_step, step.next()))
                        dve.wait_ge(tables_in, at(tables_in, 128))
                        for i in range(ks):
                            nc.vector.tensor_reduce(m[:, 2 + i, :], by_tile(pr[:, :, :]), AX_X, ALU.max).then_inc(dve_step, 1)
                            dve.wait_ge(dve_step, at(dve_step, step.next()))
                            nc.vector.tensor_tensor(w[:, :, :], pr[:, :, :], bc(m[:, 2 + i, :]), ALU.is_equal).then_inc(dve_step, 1)
                            dve.wait_ge(dve_step, at(dve_step, step.next()))
                            nc.vector.tensor_tensor(w[:, :, :], w[:, :, :], firstof[:, 0:n_exp, :], ALU.mult).then_inc(dve_step, 1)
                            dve.wait_ge(dve_step, at(dve_step, step.next()))
                            nc.vector.tensor_reduce(m[:, 4, :], by_tile(w[:, :, :]), AX_X, ALU.max).then_inc(dve_step, 1)
                            dve.wait_ge(dve_step, at(dve_step, step.next()))
                            ins = nc.vector.tensor_tensor(oh[i][:, :, :], w[:, :, :], bc(m[:, 4, :]), ALU.is_equal)
                            ins.then_inc(dve_step, 1)
                            dve.wait_ge(dve_step, at(dve_step, step.next()))
                            if i == 0 and ks == 2:
                                nc.vector.scalar_tensor_tensor(pr[:, :, :], oh[0][:, :, :], -2.0, pr[:, :, :], ALU.mult, ALU.add).then_inc(dve_step, 1)
                                dve.wait_ge(dve_step, at(dve_step, step.next()))
                        if mode == "top1":
                            nc.vector.tensor_scalar(G[:, :, :], oh[0][:, :, :], gate, None, ALU.mult).then_inc(dve_step, 1)
                            dve.wait_ge(dve_step, at(dve_step, step.next()))
                        if mode in ("first", "top2"):
                            eps = 1e-9 if mode == "top2" else 0.0
                            nc.vector.scalar_tensor_tensor(m[:, 5, :], m[:, 2, :], eps, m[:, 3, :], ALU.add, ALU.add).then_inc(dve_step, 1)
                            dve.wait_ge(dve_step, at(dve_step, step.next()))
                            nc.vector.reciprocal(m[:, 6, :], m[:, 5, :]).then_inc(dve_step, 1)
                            dve.wait_ge(dve_step, at(dve_step, step.next()))
                            for i in range(2):
                                nc.vector.scalar_tensor_tensor(m[:, 2 + i, :], m[:, 2 + i, :], gate, m[:, 6, :], ALU.mult, ALU.mult).then_inc(dve_step, 1)
                                dve.wait_ge(dve_step, at(dve_step, step.next()))
                        kept = [oh[0][:, :, :], oh[1][:, :, :]]
                        if mode == "first":
                            nc.vector.engine_nop().then_inc(chosen, 2)
                            for i in range(2):
                                dve.wait_ge(pe_out, at(pe_out, 2 + i))
                                nc.vector.tensor_copy(ohT[i][:, :], ps[:, 1 + i, 0:P]).then_inc(dve_step, 1)
                                dve.wait_ge(dve_step, at(dve_step, step.next()))
                                nc.vector.tensor_tensor_scan(cs[i][:, :], ones[:, 0:P], ohT[i][:, :], 0.0, ALU.mult, ALU.add).then_inc(counted, 1)
                            for i in range(2):
                                dve.wait_ge(counted, at(counted, i + 1))
                                dve.wait_ge(pe_out, at(pe_out, 4 + i))
                                nc.vector.tensor_scalar(cs[i][:, :], cs[i][:, :], ps[:, 3 + i, 0:1], float(capacity), ALU.add, ALU.is_le).then_inc(dve_step, 1)
                                dve.wait_ge(dve_step, at(dve_step, step.next()))
                                nc.vector.tensor_tensor(keep[i][:, :], cs[i][:, :], ohT[i][:, :], ALU.mult).then_inc(kept_made, 1)
                            for i in range(2):
                                dve.wait_ge(pe_out, at(pe_out, 6 + i))
                                kept[i] = ps[:, 5 + i, 0:P].rearrange("p (e c) -> p e c", e=n_exp)
                        if mode in ("first", "top2", "best"):
                            dst = w if mode == "best" else G
                            nc.vector.tensor_tensor(part[:, :, :], kept[0], bc(m[:, 2, :]), ALU.mult)
                            nc.vector.tensor_tensor(taken[:, :, :], kept[1], bc(m[:, 3, :]), ALU.mult).then_inc(dve_step, 1)
                            dve.wait_ge(dve_step, at(dve_step, step.next()))
                            nc.vector.tensor_tensor(dst[:, :, :], part[:, :, :], taken[:, :, :], ALU.add).then_inc(dve_step, 1)
                            dve.wait_ge(dve_step, at(dve_step, step.next()))
                        if mode == "best":
                            nc.vector.engine_nop().then_inc(chosen, 1)
                            gT = ohT[0]
                            dve.wait_ge(pe_out, at(pe_out, 2))
                            nc.vector.memset(thr[:, 0:1], 0)
                            nc.vector.tensor_copy(gT[:, :], ps[:, 1, 0:P]).then_inc(dve_step, 1)
                            dve.wait_ge(dve_step, at(dve_step, step.next()))
                            for i in range(15):
                                low = 1 << (28 - 2 * i)
                                for n in range(3):
                                    ins = nc.vector.tensor_scalar(thr[:, 2 + n:3 + n], thr[:, 0:1], (n + 1) * low, None, ALU.bitwise_or)
                                ins.then_inc(dve_step, 1)
                                dve.wait_ge(dve_step, at(dve_step, step.next()))
                                for n in range(3):
                                    ins = nc.vector.tensor_scalar((cs[0], cs[1], keep[0])[n][:, :], gT[:, :], thr[:, 2 + n:3 + n].bitcast(F32), None, ALU.is_ge, ALU.add,
                                                                  accum_out=col[:, 5 + n:6 + n])
                                ins.then_inc(counted, 1)
                                dve.wait_ge(pe_out, at(pe_out, 3 + i))
                                nc.vector.tensor_scalar(reached[:, 0:3], ps[:, 2 + i % 2, 0:3], float(capacity), None, ALU.is_ge, ALU.add,
                                                        accum_out=reached[:, 3:4]).then_inc(dve_step, 1)
                                dve.wait_ge(dve_step, at(dve_step, step.next()))
                                nc.vector.tensor_scalar(thr[:, 1:2], reached[:, 3:4], float(low), None, ALU.mult).then_inc(dve_step, 1)
                                dve.wait_ge(dve_step, at(dve_step, step.next()))
                                nc.vector.tensor_tensor(thr[:, 0:1], thr[:, 0:1], thr[:, 1:2], ALU.bitwise_or).then_inc(dve_step, 1)
                                dve.wait_ge(dve_step, at(dve_step, step.next()))
                            t32 = thr[:, 0:1].bitcast(F32)
                            nc.vector.tensor_scalar(keep[1][:, :], gT[:, :], t32, None, ALU.is_gt, ALU.add, accum_out=col[:, 5:6]).then_inc(counted, 1)
                            nc.vector.tensor_scalar(ohT[1][:, :], gT[:, :], t32, None, ALU.is_equal).then_inc(dve_step, 1)
                            dve.wait_ge(dve_step, at(dve_step, step.next()))
                            nc.vector.tensor_tensor_scan(cs[0][:, :], ones[:, 0:P], ohT[1][:, :], 0.0, ALU.mult, ALU.add).then_inc(counted, 1)
                            dve.wait_ge(pe_out, at(pe_out, 18))
                            nc.vector.tensor_scalar(col[:, 1:2], ps[:, 3, 0:1], -1.0, float(capacity), ALU.mult, ALU.add).then_inc(dve_step, 1)
                            dve.wait_ge(dve_step, at(dve_step, step.next()))
                            dve.wait_ge(pe_out, at(pe_out, 19))
                            nc.vector.tensor_scalar(cs[1][:, :], cs[0][:, :], ps[:, 4, 0:1], col[:, 1:2], ALU.add, ALU.is_le).then_inc(dve_step, 1)
                            dve.wait_ge(dve_step, at(dve_step, step.next()))
                            nc.vector.tensor_tensor(cs[1][:, :], cs[1][:, :], ohT[1][:, :], ALU.mult).then_inc(dve_step, 1)
                            dve.wait_ge(dve_step, at(dve_step, step.next()))
                            nc.vector.tensor_tensor(cs[1][:, :], cs[1][:, :], keep[1][:, :], ALU.add).then_inc(dve_step, 1)
                            dve.wait_ge(dve_step, at(dve_step, step.next()))
                            nc.vector.tensor_tensor(keep[0][:, :], cs[1][:, :], gT[:, :], ALU.mult).then_inc(kept_made, 1)
                            dve.wait_ge(pe_out, at(pe_out, 20))
                            nc.vector.tensor_scalar(G[:, :, :], ps[:, 5, 0:P].rearrange("p (e c) -> p e c", e=n_exp), gate, None, ALU.mult).then_inc(dve_step, 1)
                            dve.wait_ge(dve_step, at(dve_step, step.next()))
                        nc.vector.tensor_scalar(taken[:, :, :], G[:, :, :], 0.0, None, ALU.not_equal).then_inc(placed, 1)
                        dve.wait_ge(place_out, at(place_out, 1))
                        nc.vector.tensor_copy(ohT[0][0:R, :], ps[0:R, 7, 0:P]).then_inc(dve_step, 1)
                        dve.wait_ge(dve_step, at(dve_step, step.next()))
                        nc.vector.tensor_tensor_scan(cs[0][0:R, :], ones[0:R, 0:P], ohT[0][0:R, :], 0.0, ALU.mult, ALU.add).then_inc(placed, 1)
                        dve.wait_ge(place_out, at(place_out, 2))
                        nc.vector.tensor_copy(col[0:R, 3:5], ps[0:R, 7, P:P + 2]).then_inc(dve_step, 1)
                        dve.wait_ge(dve_step, at(dve_step, step.next()))
                        nc.vector.tensor_scalar(ohT[1][0:R, 0:NT], tile_rows[0:R, 0:NT], col[0:R, 4:5], None, ALU.is_lt, ALU.add,
                                                accum_out=col[0:R, 2:3]).then_inc(placed, 1)
                        dve.wait_ge(place_out, at(place_out, 3))
                        nc.vector.tensor_copy(col[0:R, 5:7], ps[0:R, 7, P + 2:P + 4]).then_inc(dve_step, 1)
                        dve.wait_ge(dve_step, at(dve_step, step.next()))
                        nc.vector.tensor_scalar(cs[1][0:R, :], cs[0][0:R, :], col[0:R, 3:4], col[0:R, 5:6], ALU.add, ALU.add)
                        nc.vector.tensor_scalar(begun_tiles[0:R, 0:n_tiles], tile_rows[0:R, 0:n_tiles], col[0:R, 6:7], None, ALU.is_ge).then_inc(placed, 1)
                        dve.wait_ge(place_out, at(place_out, 4))
                        nc.vector.tensor_scalar(plan.offset[0:1, :], ps[0:1, 7, 256:256 + n_tiles], float(n_exp - 1), float(plan.stride), ALU.min, ALU.mult)
                        nc.vector.tensor_tensor(taken[:, :, :], taken[:, :, :], ps[:, 7, 0:R].rearrange("p (e c) -> p e c", e=n_exp), ALU.mult).then_inc(dve_step, 1)
                        dve.wait_ge(dve_step, at(dve_step, step.next()))
                        for i in range(ks):
                            nc.vector.tensor_tensor(part[:, :, :], taken[:, :, :], oh[i][:, :, :], ALU.mult)
                            nc.vector.tensor_tensor(w[:, :, :], G[:, :, :], oh[i][:, :, :], ALU.mult).then_inc(dve_step, 1)
                            dve.wait_ge(dve_step, at(dve_step, step.next()))
                            nc.vector.tensor_reduce(place[:, i, :], by_tile(part[:, :, :]), AX_X, ALU.add)
                            nc.vector.tensor_reduce(plan.weight[:, i, :], by_tile(w[:, :, :]), AX_X, ALU.add).then_inc(dve_step, 1)
                            dve.wait_ge(dve_step, at(dve_step, step.next()))
                        place_of = place[:, 0:ks, :]
                        nc.vector.scalar_tensor_tensor(spare[:, 0:ks, :], place_of, 0.0, spare[:, 0:ks, :], ALU.is_equal, ALU.mult).then_inc(dve_step, 1)
                        dve.wait_ge(dve_step, at(dve_step, step.next()))
                        nc.vector.scalar_tensor_tensor(spare[:, 0:ks, :], place_of, -1.0, spare[:, 0:ks, :], ALU.add, ALU.add).then_inc(dve_step, 1)
                        dve.wait_ge(dve_step, at(dve_step, step.next()))
                        nc.vector.tensor_copy(plan.to[:, 0:ks, :], spare[:, 0:ks, :])
                        nc.vector.tensor_scalar(plan.back[:, 0:ks, :], spare[:, 0:ks, :], float(n_tiles * P - 1), None, ALU.min).then_inc(dve_step, 1)
                        dve.wait_ge(dve_step, at(dve_step, step.next()))
                        advance((dve_step, step.total))
            advance((tables_in, 128), (logits, 1), (exps_made, 1), (pe_out, {"first": 7, "best": 20}.get(mode, 1)), (chosen, {"first": 2, "best": 1}.get(mode, 0)), (counted, {"first": 2, "best": 17}.get(mode, 0)), (kept_made, {"first": 2, "best": 1}.get(mode, 0)), (placed, 4), (place_out, 4))

        def load_experts(tmp, n_exp, ff, w1d, w2d, b1d=None, b2d=None):
            tables = [tmp("t_" + name, shape) for name, shape in (
                ("firstof", [P, E8, NT]), ("earlier", [P, P]), ("sameexp", [P, P]), ("before", [P, P]), ("through", [P, P]),
                ("first_tile", [P, 1]), ("tile_rows", [P, SLOT_TILES]), ("spare", [P, 2, NT]))]
            w1 = tmp("w1", [P, n_exp, KD, ff])
            w2 = tmp("w2", [P, n_exp, ff // P, D])
            bs = None if b1d is None else tmp("bs", [1, n_exp, KD * ff])
            with nc.Block() as block:
                @block.sync
                def _(sp):
                    for table, source in zip(tables, (a["firstof"].rearrange("p (e c) -> p e c", e=E8), a["earlier"], a["sameexp"],
                                                      a["experts_before"], a["experts_through"], a["first_tile"], a["tile_rows"],
                                                      a["spare"].rearrange("p (i c) -> p i c", i=2))):
                        sp.dma_start(table[...], source).then_inc(tables_in, 16)
                    w1v = w1d.rearrange("e (k p) f -> e p k f", p=P)
                    w2v = w2d.rearrange("e (f p) d -> e p f d", p=P)
                    for e in range(n_exp):
                        sp.dma_start(w1[:, e], w1v[e]).then_inc(weights_in, 16)
                        sp.dma_start(w2[:, e], w2v[e]).then_inc(weights_in, 16)
                    if b1d is not None:
                        sp.dma_start(bs[:, :, 0:ff], b1d.rearrange("(o e) f -> o e f", o=1)).then_inc(weights_in, 16)
                        sp.dma_start(bs[:, :, ff:ff + D], b2d.rearrange("(o e) d -> o e d", o=1)).then_inc(weights_in, 16)
            return (w1, w2, bs), tables

        def experts(ff, weights, func, plan, rows, gcol=None):
            n_exp, ks, n_tiles, stride = plan.n_exp, plan.ks, plan.n_tiles, plan.stride
            fc = ff // P
            put, result = a["expert_rows"], a["expert_results"][0:n_tiles * P, :]
            with ExitStack() as own:
                def tmp(name, shape, dt=F32):
                    return own.enter_context(sbuf("e_" + name, shape, dt))
                w1, w2, bs = weights
                w1_ = w1[:, :, :, :].rearrange("p e k f -> p (e k f)")
                w2_ = w2[:, :, :, :].rearrange("p e f d -> p (e f d)")
                xr = XN[:, 0:4, :]
                h = XN[:, 8:16, :].rearrange("p c d -> p (c d)").rearrange("p (i f) -> p i f", i=2)[:, :, 0:ff]
                xt = tmp("xt", [P, 2, KD, P])
                hT = tmp("hT", [P, fc, P])
                y = XN[:, 4:6, :]
                if bs is not None:
                    b_ = bs[:, :, :].rearrange("o e f -> o (e f)")
                with nc.Block() as block:
                    @block.gpsimd
                    def _(pool):
                        for c in range(NT):
                            for i in range(ks):
                                nc.gpsimd.indirect_dma_start(put, bass.IndirectOffsetOnAxis(ap=plan.to[:, i, c:c + 1], axis=0),
                                                             rows[:, c, :], None).then_inc(rows_put, 16)
                        pool.wait_ge(rows_put, at(rows_put, 16 * ks * NT))
                n_loaded = 16 * (2 * n_exp + (2 if bs is not None else 0))
                advance((rows_put, 16 * ks * NT))

                X_IN, Y_OUT, H_OUT, H_TURNED = 0, 1, 2, 6
                hb = max(1, ff // 512)
                tb = max(1, fc // 4)
                with nc.Block() as block:
                    @block.sync
                    def _(sp):
                        def fetch(t, slot):
                            sp.dma_start(xr[:, slot, :], put[bass.ds(t * P, P), :]).then_inc(x_in[slot], 16)

                        for t in range(4):
                            fetch(t, t)
                        with sp.Fori(0, n_tiles // 4 - 1) as q:
                            for u in range(4):
                                sp.wait_ge(x_turned, at(x_turned, 4 * q + u + 1))
                                fetch(4 * q + u + 4, u)

                    @block.tensor
                    def _(pe):
                        def turn_rows(t, slot, turn):
                            pe.wait_ge(x_in[slot], at(x_in[slot], 16 * turn + 16))
                            if not isinstance(t, int) or t > 0:
                                pe.wait_ge(xt_ready, at(xt_ready, t))
                            for k in range(KD):
                                ins = nc.tensor.transpose(ps[:, X_IN, k * P:(k + 1) * P], xr[:, slot, k * P:(k + 1) * P], ident[:, :])
                            ins.then_inc(x_turned, 1)

                        def hidden(t, par):
                            pe.wait_ge(xt_ready, at(xt_ready, t + 1))
                            if not isinstance(t, int) or t > 1:
                                pe.wait_ge(h_ready, at(h_ready, t - 1))
                            e = pe.value_load(plan.offset[0:1, bass.ds(t, 1)], min_val=0, max_val=(n_exp - 1) * stride)
                            for n in range(hb):
                                wd = min(512, ff)
                                for k in range(KD):
                                    ins = nc.tensor.matmul(ps[:, H_OUT + par * 2 + n, 0:wd], xt[:, par, k, :],
                                                           w1_[:, bass.ds(e + (k * ff + n * wd), wd)],
                                                           start=(k == 0), stop=(k == KD - 1 and bs is None))
                                if bs is not None:
                                    ins = nc.tensor.matmul(ps[:, H_OUT + par * 2 + n, 0:wd], ones[0:1, 0:P],
                                                           b_[0:1, bass.ds(e + n * wd, wd)], start=False, stop=True)
                            ins.then_inc(h_out, 1)

                        def turn_hidden(t, par):
                            pe.wait_ge(h_ready, at(h_ready, t + 1))
                            for n in range(tb):
                                if not isinstance(t, int) or t > 0:
                                    pe.wait_ge(hT_free, at(hT_free, tb * (t - 1) + n + 1))
                                for f in range(4):
                                    ins = nc.tensor.transpose(ps[:, H_TURNED + n, f * P:(f + 1) * P],
                                                              h[:, par, (4 * n + f) * P:(4 * n + f + 1) * P], ident[:, :])
                                ins.then_inc(h_turned, 1)

                        def results(t, par):
                            e = pe.value_load(plan.offset[0:1, bass.ds(t, 1)], min_val=0, max_val=(n_exp - 1) * stride)
                            if not isinstance(t, int) or t > 0:
                                pe.wait_ge(y_ready, at(y_ready, t))
                            for f in range(fc):
                                if f % 4 == 0:
                                    pe.wait_ge(hT_free, at(hT_free, tb * t + f // 4 + 1))
                                ins = nc.tensor.matmul(ps[:, Y_OUT, 0:D], hT[:, f, :], w2_[:, bass.ds(e + f * D, D)],
                                                       start=(f == 0), stop=(f == fc - 1 and bs is None))
                            if bs is not None:
                                ins = nc.tensor.matmul(ps[:, Y_OUT, 0:D], ones[0:1, 0:P], b_[0:1, bass.ds(e + ff, D)], start=False, stop=True)
                            ins.then_inc(y_out, 1)

                        turn_rows(0, 0, 0)
                        turn_rows(1, 1, 0)
                        pe.wait_ge(weights_in, at(weights_in, n_loaded))
                        hidden(0, 0)

                        def tile(t, u, turn):
                            hidden(t + 1, (u + 1) % 2)
                            turn_hidden(t, u % 2)
                            turn_rows(t + 2, (u + 2) % 4, turn)
                            results(t, u % 2)

                        for u in range(2):
                            tile(u, u, 0)
                        with pe.Fori(0, n_tiles // 4 - 1) as q:
                            for u in range(4):
                                tile(4 * q + u + 2, (u + 2) % 4, q + 1)
                        t = n_tiles - 2
                        hidden(t + 1, 1)
                        turn_hidden(t, 0)
                        results(t, 0)
                        turn_hidden(t + 1, 1)
                        results(t + 1, 1)

                    @block.scalar
                    def _(act):
                        def activate(t, par):
                            act.wait_ge(h_out, at(h_out, t + 1))
                            if not isinstance(t, int) or t > 1:
                                act.wait_ge(h_turned, at(h_turned, tb * (t - 1)))
                            nc.scalar.activation(h[:, par, :], ps[:, H_OUT + par * 2:H_OUT + par * 2 + hb, 0:min(512, ff)].rearrange("p n f -> p (n f)"),
                                                 func).then_inc(h_ready, 1)

                        for t in range(2):
                            activate(t, t)
                        with act.Fori(0, n_tiles // 2 - 1) as q:
                            for u in range(2):
                                activate(2 * q + u + 2, u)

                    @block.vector
                    def _(dve):
                        def turned_rows(t, par):
                            dve.wait_ge(x_turned, at(x_turned, t + 1))
                            if not isinstance(t, int) or t > 1:
                                dve.wait_ge(h_out, at(h_out, t - 1))
                            for k in range(KD):
                                src = ps[:, X_IN, k * P:(k + 1) * P]
                                if gcol is None:
                                    ins = nc.vector.tensor_copy(xt[:, par, k, :], src)
                                else:
                                    ins = nc.vector.tensor_scalar(xt[:, par, k, :], src, gcol[:, k:k + 1], None, ALU.mult)
                            ins.then_inc(xt_ready, 1)

                        def turned_hidden(t):
                            for n in range(tb):
                                dve.wait_ge(h_turned, at(h_turned, tb * t + n + 1))
                                if n == 0 and (not isinstance(t, int) or t > 0):
                                    dve.wait_ge(y_out, at(y_out, t))
                                nc.vector.tensor_copy(hT[:, 4 * n:4 * n + 4, :], ps[:, H_TURNED + n, :].rearrange("p (f q) -> p f q", f=4)).then_inc(hT_free, 1)

                        def results(t, par, stored):
                            dve.wait_ge(y_out, at(y_out, t + 1))
                            if stored is not None:
                                dve.wait_ge(y_stored[par], at(y_stored[par], 16 * stored))
                            nc.vector.tensor_copy(y[:, par, :], ps[:, Y_OUT, 0:D]).then_inc(y_ready, 1)

                        turned_rows(0, 0)
                        turned_rows(1, 1)
                        for t in range(2):
                            turned_hidden(t)
                            turned_rows(t + 2, t)
                            results(t, t, None)
                        with dve.Fori(0, (n_tiles - 4) // 2) as q:
                            for u in range(2):
                                t = 2 * q + u + 2
                                turned_hidden(t)
                                turned_rows(t + 2, u)
                                results(t, u, q + 1)
                        for t in (n_tiles - 2, n_tiles - 1):
                            turned_hidden(t)
                            results(t, t % 2, n_tiles // 2 - 1)

                    @block.gpsimd
                    def _(pool):
                        def store(t, par):
                            pool.wait_ge(y_ready, at(y_ready, t + 1))
                            nc.gpsimd.dma_start(result[bass.ds(t * P, P), :], y[:, par, :]).then_inc(y_stored[par], 16)

                        with pool.Fori(0, n_tiles // 2) as q:
                            for u in range(2):
                                store(2 * q + u, u)
                        for par in range(2):
                            pool.wait_ge(y_stored[par], at(y_stored[par], 8 * n_tiles))
                advance((weights_in, n_loaded), *((x, 4 * n_tiles) for x in x_in), (x_turned, n_tiles), (xt_ready, n_tiles), (h_out, n_tiles), (h_ready, n_tiles),
                        (h_turned, tb * n_tiles), (hT_free, tb * n_tiles), (y_out, n_tiles), (y_ready, n_tiles), *((x, 8 * n_tiles) for x in y_stored))

                back = [XN, XT[:, :, :].rearrange("p k t -> p (k t)").rearrange("p (c d) -> p c d", c=NT)]
                with nc.Block() as block:
                    @block.gpsimd
                    def _(pool):
                        for c in range(NT):
                            for i in range(ks):
                                nc.gpsimd.indirect_dma_start(back[i][:, c, :], None, result,
                                                             bass.IndirectOffsetOnAxis(ap=plan.back[:, i, c:c + 1], axis=0)).then_inc(rows_in[c // 4], 16)

                    @block.vector
                    def _(dve):
                        step = Steps()
                        for g in range(NT // 4):
                            dve.wait_ge(rows_in[g], at(rows_in[g], 64 * ks))
                            for i in range(ks):
                                for c in range(4 * g, 4 * g + 4):
                                    ins = nc.vector.scalar_tensor_tensor(X[:, c, :], back[i][:, c, :], plan.weight[:, i, c:c + 1], X[:, c, :], ALU.mult, ALU.add)
                                ins.then_inc(dve_step, 1)
                                dve.wait_ge(dve_step, at(dve_step, step.next()))
                        advance((dve_step, step.total))
                advance(*((s_, 64 * ks) for s_ in rows_in))

        def experts_layer0():
            with ExitStack() as own:
                def tmp(name, shape, dt=F32):
                    return own.enter_context(sbuf(name, shape, dt))
                wr = tmp("wr0", [P, KD, E8])
                routers(wr, a["L0_ffn_router_w"])
                weights, tables = load_experts(tmp, E8, 1024, a["L0_ffn_w1"], a["L0_ffn_w2"])
                plan = Plan(tmp, E8, 2, SLOT_TILES, KD * 1024, tables)
                normalise(X, XN, True, 1e-5)
                route("first", E8, wr, tg[:, 4:5], plan, capacity=max(1, int(1.25 * T / E8 * 2)))
                experts(1024, weights, ACT.Gelu, plan, XN)

        def routers(wr, src):
            with ExitStack() as own:
                rows = own.enter_context(sbuf("rrows", [E8, D], F32))
                with nc.Block() as block:
                    @block.sync
                    def _(sp):
                        sp.dma_start(rows[:, :], src).then_inc(loaded, 16)

                    @block.tensor
                    def _(pe):
                        pe.wait_ge(loaded, at(loaded, 16))
                        for k in range(KD):
                            ins = nc.tensor.transpose(ps[:, 0, k * E8:(k + 1) * E8], rows[:, k * P:(k + 1) * P], ident[0:E8, 0:E8])
                        ins.then_inc(pe_out, 1)

                    @block.scalar
                    def _(act):
                        act.wait_ge(pe_out, at(pe_out, 1))
                        nc.scalar.copy(wr[:, :, :], ps[:, 0, 0:KD * E8].rearrange("p (k e) -> p k e", k=KD))
                advance((loaded, 16), (pe_out, 1))

        def swap_pairs(eng, dst, src):
            d = dst.rearrange("p n (i two) -> p n i two", two=2)
            s_ = src.rearrange("p n (i two) -> p n i two", two=2)
            eng.tensor_scalar(d[:, :, :, 0], s_[:, :, :, 1], -1.0, None, ALU.mult)
            return eng.tensor_copy(d[:, :, :, 1], s_[:, :, :, 0])

        def context_values(VM, VT, wv, bv):
            with nc.Block() as block:
                @block.tensor
                def _(pe):
                    for b in range(B):
                        for n, (lo, hi) in enumerate(((0, P), (P, L))):
                            bank = ps[0:hi - lo, 2 * b + n, 0:D]
                            for k in range(KD):
                                nc.tensor.matmul(bank, CT[:, k, b, lo:hi], wv[:, k, :], start=(k == 0), stop=False)
                            nc.tensor.matmul(bank, ones[0:1, 0:hi - lo], bv[0:1, :], start=False, stop=True).then_inc(v_out, 1)

                @block.vector
                def _(dve):
                    for b in range(B):
                        for n, (dst, rows) in enumerate(((VM, P), (VT, TAIL))):
                            dve.wait_ge(v_out, at(v_out, 2 * b + n + 1))
                            nc.vector.tensor_copy(dst[:, b, :], ps[0:rows, 2 * b + n, 0:D])
            advance((v_out, 2 * B))

        def context_attention(name, gate, wq, wk, wv, wo, bq, bk, bv, bo, scale, rope=None, mask=None, mask_row=None):
            with ExitStack() as own:
                def tmp(nm_, shape, dt=F32):
                    return own.enter_context(sbuf(name + nm_, shape, dt))
                VM = tmp("VM", [P, B, D])
                VT = tmp("VT", [TAIL, B, D])
                context_values(VM, VT, wv, bv)
                wqx = wkx = cq = sq = None
                if rope is not None:
                    wqx, wkx = (rope[0], rope[2]), (rope[1], rope[3])
                    cq, sq, ck, sk = rope[4:]
                flat = CT[:, :, :, :].rearrange("p k b l -> p k (b l)")
                items = [(flat, B * L, ch, 0, (wk, bk), wkx, None if rope is None else ck[:, :].unsqueeze(1).broadcast_to([P, B, L]),
                             None if rope is None else sk[:, :].unsqueeze(1).broadcast_to([P, B, L]), a["ck_parts"], 1.0) for ch in range(KD)]
                bf16_parts(items + [(XT[:, :, t * 512:(t + 1) * 512], 512, ch, t * 512, (wq, bq), wqx,
                             None if rope is None else cq[:, (t % 2) * 512:(t % 2 + 1) * 512].unsqueeze(1),
                             None if rope is None else sq[:, (t % 2) * 512:(t % 2 + 1) * 512].unsqueeze(1), a["q_parts"], scale)
                            for ch in range(KD) for t in range(T // 512)])
                attention_by_heads(name, L, None, lambda h, b, to: [(to[:, 0, 0:HD], VM[:, b, bass.ds(h * HD, HD)]), (to[0:TAIL, 1, 0:HD], VT[:, b, bass.ds(h * HD, HD)])],
                                   mask, mask_row)
                project_out(wo, bo, gate)

        def attention1():
            with ExitStack() as own:
                def tmp(name, shape, dt=F32):
                    return own.enter_context(sbuf("a1" + name, shape, dt))
                wq = tmp("wq", [P, KD, D])
                wkv = tmp("wkv", [P, KD, 2 * D])
                wo = tmp("wo", [P, KD, D])
                wqx = tmp("wqx", [P, KD, D])
                wkx = tmp("wkx", [P, KD, D])
                bq = tmp("bq", [1, D])
                bkv = tmp("bkv", [1, 2 * D])
                bo = tmp("bo", [1, D])
                bx = tmp("bx", [1, 2, D])
                m8 = tmp("m8", [1, B * L], U8)
                mf = tmp("mf", [1, B * L])
                mrow = tmp("mrow", [1, B * L], BF16)
                tables = [tmp(n, [P, w_]) for n, w_ in (("cq", S), ("sq", S), ("ck", L), ("sk", L))]
                load_weights([
                    (wq[:, :, :], a["L1_xattn_Wq"].rearrange("(k p) d -> p k d", p=P)),
                    (wkv[:, :, :], a["L1_xattn_Wkv"].rearrange("(k p) d -> p k d", p=P)),
                    (wo[:, :, :], a["L1_xattn_Wo"].rearrange("(k p) d -> p k d", p=P)),
                    (bq[:, :], a["L1_xattn_bq"]), (bkv[:, :], a["L1_xattn_bkv"]), (bo[:, :], a["L1_xattn_bo"]),
                    (m8[:, :], a["ctx_mask"])] + [(t[:, :], a[n]) for t, n in zip(tables, ("cos1q", "sin1q", "cos1k", "sin1k"))],
                    lambda: normalise(X, XN, True, 1e-5))
                with nc.Block() as block:
                    @block.vector
                    def _(dve):
                        swap_pairs(nc.vector, wqx[:, :, :], wq[:, :, :])
                        swap_pairs(nc.vector, wkx[:, :, :], wkv[:, :, 0:D])
                        swap_pairs(nc.vector, bx[:, 0:1, :], bq[:, :].unsqueeze(1))
                        swap_pairs(nc.vector, bx[:, 1:2, :], bkv[:, 0:D].unsqueeze(1))
                        nc.vector.tensor_copy(mf[:, :], m8[:, :]).then_inc(cst, 1)
                        dve.wait_ge(cst, at(cst, 1))
                        nc.vector.tensor_scalar(mf[:, :], mf[:, :], -1.0, 3e38, ALU.add, ALU.mult).then_inc(cst, 1)
                        dve.wait_ge(cst, at(cst, 2))
                        nc.vector.tensor_scalar(mrow[:, :], mf[:, :], 10.0, None, ALU.mult)
                advance((cst, 2))
                context_attention("a1", tg[:, 1:2], wq, wkv[:, :, 0:D], wkv[:, :, D:2 * D], wo, bq, bkv[:, 0:D], bkv[:, D:2 * D], bo, 64 ** -0.5,
                                  rope=(wqx, wkx, bx[:, 0, :], bx[:, 1, :], *tables), mask_row=mrow[:, :])

        def attention3():
            with ExitStack() as own:
                def tmp(name, shape, dt=F32):
                    return own.enter_context(sbuf("a3" + name, shape, dt))
                w = [tmp(f"w{i}", [P, KD, D]) for i in range(4)]
                bias = [tmp(f"b{i}", [1, D]) for i in range(4)]
                m8 = tmp("m8", [P, NT, L], U8)
                mb = tmp("mask", [P, NT, L], BF16)
                load_weights([(w[i][:, :, :], a[f"L3_xattn_W{c}"].rearrange("(k p) d -> p k d", p=P)) for i, c in enumerate("qkvo")]
                             + [(bias[i][:, :], a[f"L3_xattn_b{c}"]) for i, c in enumerate("qkvo")]
                             + [(m8[:, :, :], a["q_mask"].rearrange("(t p) l -> p t l", p=P))],
                             lambda: normalise(X, XN, True, 1e-5))
                with nc.Block() as block:
                    @block.vector
                    def _(dve):
                        nc.vector.tensor_scalar(mb[:, :, :], m8[:, :, :], -float(2 ** 50), None, ALU.mult)
                context_attention("a3", tg[:, 3:4], w[0], w[1], w[2], w[3], *bias, HD ** -0.5, mask=mb)

        def bf16_parts(items):
            with ExitStack() as own:
                def tmp(name, shape, dt=F32):
                    return own.enter_context(sbuf("p_" + name, shape, dt))
                F = tmp("F", [P, 2, 512])
                turned2 = tmp("turned", [P, 2, 512])
                R = tmp("R", [P, 3, 512])
                PB = tmp("PB", [P, 4, 3, 512], BF16)
                n_items = len(items)
                with nc.Block() as block:
                    @block.tensor
                    def _(pe):
                        for i, (src, n, ch, _, wa, wb, *_) in enumerate(items):
                            if i >= 2:
                                pe.wait_ge(f_ready, at(f_ready, i - 1))
                            for half, wbias in enumerate((wa, wb)):
                                if wbias is None:
                                    continue
                                w, bias = wbias
                                for k in range(KD):
                                    ins = nc.tensor.matmul(ps[:, 2 * half + i % 2, 0:n], w[:, k, ch * P:(ch + 1) * P], src[:, k, :],
                                                           start=(k == 0), stop=(k == KD - 1 and bias is None))
                                if bias is not None:
                                    ins = nc.tensor.matmul(ps[:, 2 * half + i % 2, 0:n], bias[0:1, ch * P:(ch + 1) * P], ones[0:1, 0:n],
                                                           start=False, stop=True)
                            ins.then_inc(pe_out, 1)

                    @block.vector
                    def _(dve):
                        step = Steps()

                        def project(i):
                            src, n, ch, _, wa, wb, cos, sin, _, _ = items[i]
                            if i >= 2:
                                dve.wait_ge(rest_ready, at(rest_ready, i - 1))
                            dve.wait_ge(pe_out, at(pe_out, i + 1))
                            if wb is None:
                                nc.vector.tensor_copy(F[:, i % 2, 0:n], ps[:, i % 2, 0:n]).then_inc(f_ready, 1)
                                return
                            reps = cos.shape[1]
                            def view(x):
                                return x.rearrange("p (r n) -> p r n", r=reps)
                            nc.vector.tensor_tensor(view(turned2[:, 0, 0:n]), view(ps[:, i % 2, 0:n]), cos, ALU.mult)
                            nc.vector.tensor_tensor(view(turned2[:, 1, 0:n]), view(ps[:, 2 + i % 2, 0:n]), sin, ALU.mult).then_inc(dve_step, 1)
                            dve.wait_ge(dve_step, at(dve_step, step.next()))
                            nc.vector.tensor_tensor(F[:, i % 2, 0:n], turned2[:, 0, 0:n], turned2[:, 1, 0:n], ALU.add).then_inc(f_ready, 1)
                            dve.wait_ge(f_ready, at(f_ready, i + 1))

                        for i in range(n_items + 2):
                            if i < n_items:
                                project(i)
                            if 1 <= i <= n_items:
                                n = items[i - 1][1]
                                if i >= 4:
                                    dve.wait_ge(parts_ready, at(parts_ready, i - 3))
                                dve.wait_ge(first_cast, at(first_cast, i))
                                nc.vector.scalar_tensor_tensor(R[:, (i - 1) % 3, 0:n], F[:, (i - 1) % 2, 0:n], items[i - 1][9], PB[:, (i - 1) % 4, 0, 0:n],
                                                               ALU.mult, ALU.subtract).then_inc(rest_ready, 1)
                            if i >= 2:
                                n = items[i - 2][1]
                                dve.wait_ge(second_cast, at(second_cast, i - 1))
                                nc.vector.tensor_tensor(PB[:, (i - 2) % 4, 2, 0:n], R[:, (i - 2) % 3, 0:n], PB[:, (i - 2) % 4, 1, 0:n],
                                                        ALU.subtract).then_inc(parts_ready, 1)
                        advance((dve_step, step.total))

                    @block.scalar
                    def _(act):
                        for i in range(n_items + 1):
                            if i < n_items:
                                n = items[i][1]
                                act.wait_ge(f_ready, at(f_ready, i + 1))
                                if i >= 4:
                                    act.wait_ge(parts_stored[i % 4], at(parts_stored[i % 4], 16 * (i // 4)))
                                nc.scalar.activation(PB[:, i % 4, 0, 0:n], F[:, i % 2, 0:n], ACT.Copy, scale=items[i][9]).then_inc(first_cast, 1)
                            if i >= 1:
                                n = items[i - 1][1]
                                act.wait_ge(rest_ready, at(rest_ready, i))
                                nc.scalar.copy(PB[:, (i - 1) % 4, 1, 0:n], R[:, (i - 1) % 3, 0:n]).then_inc(second_cast, 1)

                    @block.sync
                    def _(sp):
                        for i, (_, n, ch, col, _, _, _, _, parts, _) in enumerate(items):
                            sp.wait_ge(parts_ready, at(parts_ready, i + 1))
                            sp.dma_start(parts.rearrange("(i r) t -> r i t", i=3)[ch * P:(ch + 1) * P, :, col:col + n],
                                         PB[:, i % 4, :, 0:n]).then_inc(parts_stored[i % 4], 16)
                        for j in range(4):
                            sp.wait_ge(parts_stored[j], at(parts_stored[j], 16 * len(range(j, n_items, 4))))
                advance((pe_out, n_items), (f_ready, n_items), (first_cast, n_items), (rest_ready, n_items), (second_cast, n_items),
                        (parts_ready, n_items), *((parts_stored[j], 16 * len(range(j, n_items, 4))) for j in range(4)))

        def attention_by_heads(name, nk, causal, values, mask=None, mask_row=None):
            kts = [(t * P, min(P, nk - t * P)) for t in range(-(-nk // P))]
            if causal is not None:
                by_query = [[(j, half * 512, min(512, (j + 1) * P - half * 512), 0)] for j in range(TPB) for half in range(1 + j // 4)]
                by_key = [(t, q0, min(S - q0, 512)) for t in range(TPB) for q0 in range(t * P, S, 512)]
                at_block = {t: sum(TPB - u for u in range(t)) for t in range(TPB)}
                n_blocks = at_block[TPB - 1] + 1
            else:
                per = 512 // nk
                by_query = [[(j, 0, nk, (j - j0) * nk) for j in range(j0, min(j0 + per, TPB))] for j0 in range(0, TPB, per)]
                by_key = [(t, q0, 512) for t in range(len(kts)) for q0 in range(0, S, 512)]
                at_block = {t: TPB * t for t in range(len(kts))}
                n_blocks = TPB * len(kts)
            n1, n2 = len(by_query), len(by_key)
            groups = [[(t, max(QW * g, t * P) if causal is not None else QW * g) for t in range(len(kts))
                       if causal is None or t * P < QW * (g + 1)] for g in range(4)]
            rounds = [[(g, t, q0, QW * (g + 1) - q0, n == len(groups[g]) - 1) for g in range(4) if n < len(groups[g])
                       for t, q0 in [groups[g][n]]] for n in range(max(map(len, groups)))]
            BY_QUERY, BY_KEY, SUMS, MAXIMA = 0, 2, 4, 6
            pairs = [(0, 0), (0, 1), (0, 2), (1, 0), (1, 1), (2, 0)]
            base = 32
            SR = 3 * 32 + HD + 1
            with ExitStack() as own:
                def tmp(nm_, shape, dt=F32):
                    return own.enter_context(sbuf(name + nm_, shape, dt))
                QS = [tmp(f"QS{i}", [P, T], BF16) for i in range(2)]
                KS = [tmp(f"KS{i}", [P, B * nk], BF16) for i in range(2)]
                PT = [tmp(f"PT{i}", [P, n_blocks, P]) for i in range(2)]
                part_max = tmp("part_max", [P, 2, TPB])
                rest = tmp("rest", [P, 2, TPB])
                N3 = tmp("N3", [P, B, TPB, 3], BF16)
                SB = [tmp(f"SB{i}", [SR, QW]) for i in range(2)]
                nought = tmp("nought", [3, 1], BF16)
                Vh = [tmp(f"Vh{i}", [P, len(kts), VW]) for i in range(2)]
                def load(sp, h, par, turn):
                    if not isinstance(turn, int) or turn > 0:
                        sp.wait_ge(by_key_out, at(by_key_out, (2 * h - 2) * n2))
                    for n, (i, j) in enumerate(pairs):
                        rows = slice(base + n * HD, base + (n + 1) * HD)
                        sp.dma_start(QS[par][rows, :], a["q_parts"][bass.ds(h * HD + i * D, HD), :]).then_inc(stack_in[par], 16)
                        sp.dma_start(KS[par][rows, :], (a["k_parts"] if nk == S else a["ck_parts"])[bass.ds(h * HD + j * D, HD), :]).then_inc(stack_in[par], 16)

                with nc.Block() as block:
                    @block.gpsimd
                    def _(pool):
                        nc.gpsimd.memset(nought[:, :], 0.0)
                        for i in range(2):
                            nc.gpsimd.memset(KS[i][0:32, :], 0.0).then_inc(cleared, 1)
                            pool.wait_ge(cleared, at(cleared, i + 1))
                            nc.gpsimd.memset(KS[i][0:3, :], 1.0).then_inc(cst, 1)

                    @block.vector
                    def _(dve):
                        for i in range(2):
                            nc.vector.memset(QS[i][0:32, :], 0.0).then_inc(cst, 1)
                            nc.vector.memset(Vh[i][:, :, HD:VW], 1.0)
                            nc.vector.memset(ps[:, SUMS + i, 0:QW], 0.0)

                    @block.sync
                    def _(sp):
                        load(sp, 0, 0, 0)
                        load(sp, 1, 1, 0)
                        if mask_row is not None:
                            sp.wait_ge(cst, at(cst, 4))
                            for i in range(2):
                                sp.dma_start(QS[i][3:4, :], a["ones_row"]).then_inc(loaded, 16)
                                sp.dma_start(KS[i][3:4, :], mask_row).then_inc(loaded, 16)
                            sp.wait_ge(loaded, at(loaded, 64))
                advance((cleared, 2), (cst, 4), (loaded, 64 if mask_row is not None else 0))

                with nc.Block() as block:
                    @block.sync
                    def _(sp):
                        with sp.Fori(0, H // 2 - 1) as i:
                            for par in range(2):
                                load(sp, 2 * i + par + 2, par, i + 1)

                    def by_heads(loop, step):
                        step(0, 0, 0, 0, True, False, False, False)
                        step(0, 0, 0, 1, True, True, False, False)
                        step(1, 1, 0, 0, True, True, True, False)
                        step(1, 1, 0, 1, True, True, True, True)
                        with loop(0, H // 2 - 1) as i:
                            for par in range(2):
                                for b in range(B):
                                    step(2 * i + 2 + par, par, i + 1, b, True, True, True, True)
                        step(H, 0, H // 2, 0, False, True, True, True)
                        step(H, 0, H // 2, 1, False, False, True, True)
                        step(H + 1, 1, H // 2, 0, False, False, False, True)

                    @block.tensor
                    def _(pe):
                        def step(h, par, turn, b, find, make, add, store):
                            u = 2 * h + b

                            def maxima(i):
                                q, k = QS[par], KS[par]
                                if i == 0 and b == 0:
                                    pe.wait_ge(stack_in[par], at(stack_in[par], 32 * len(pairs) * (turn + 1)))
                                    pe.wait_ge(stack_zero[par], at(stack_zero[par], turn + 1))
                                if not isinstance(u, int) or u * n1 + i >= 2:
                                    pe.wait_ge(max_found, at(max_found, u * n1 + i - 1))
                                bank = ps[:, BY_QUERY + (b * n1 + i) % 2, :]
                                if mask is not None:
                                    j0, jn = by_query[i][0][0], len(by_query[i])
                                    nc.tensor.matmul(bank[:, 0:jn * nk], identb[:, :],
                                                     mask[:, b * TPB + j0:b * TPB + j0 + jn, :].rearrange("p j l -> p (j l)"),
                                                     start=True, stop=False, skip_group_check=True)
                                for j, k0, n, col in by_query[i]:
                                    diagonal = causal is not None and k0 + n == (j + 1) * P
                                    ins = nc.tensor.matmul(bank[:, col:col + n], q[:, b * S + j * P:b * S + (j + 1) * P],
                                                           k[:, b * nk + k0:b * nk + k0 + n], start=(mask is None),
                                                           stop=not diagonal and (mask is None or j == by_query[i][-1][0]), skip_group_check=(mask is not None))
                                    if diagonal:
                                        ins = nc.tensor.matmul(bank[:, n - P:n], identb[:, :], causal, start=False, stop=True)
                                ins.then_inc(by_query_out, 1)

                            ub, upar = (b + 1) % 2, (par + 1) % 2 if b == 0 else par

                            def turn_maxima():
                                pe.wait_ge(split_ready, at(split_ready, u))
                                for j in range(TPB):
                                    ins = nc.tensor.matmul(ps[0:3, MAXIMA + j // 4, (j % 4) * P:(j % 4 + 1) * P], N3[:, ub, j, :], identb[:, :],
                                                           start=True, stop=True)
                                ins.then_inc(max_turned, 1)

                            def probabilities(i):
                                q, k = QS[upar], KS[upar]
                                if i == 0:
                                    pe.wait_ge(max_stacked, at(max_stacked, u))
                                if not isinstance(u, int) or (u - 1) * n2 + i >= 2:
                                    pe.wait_ge(exp_made, at(exp_made, (u - 1) * n2 + i - 1))
                                t, q0, n = by_key[i]
                                k0, kn = kts[t]
                                bank = ps[0:kn, BY_KEY + (ub * n2 + i) % 2, :]
                                diagonal = causal is not None and q0 == t * P
                                ins = nc.tensor.matmul(bank[:, 0:n], k[:, ub * nk + k0:ub * nk + k0 + kn], q[:, ub * S + q0:ub * S + q0 + n],
                                                       start=True, stop=not diagonal and mask is None)
                                if diagonal:
                                    ins = nc.tensor.matmul(bank[:, 0:P], causal, identb[:, :], start=False, stop=True)
                                if mask is not None:
                                    for j in range(n // P):
                                        ins = nc.tensor.matmul(bank[:, j * P:(j + 1) * P], mask[:, ub * TPB + q0 // P + j, k0:k0 + kn], identb[:, :],
                                                               start=False, stop=(j == n // P - 1))
                                ins.then_inc(by_key_out, 1)

                            def sums(i):
                                if i == 0:
                                    pe.wait_ge(exp_made, at(exp_made, (u - 1) * n2))
                                    pe.wait_ge(values_in, at(values_in, u - 1))
                                    if not isinstance(u, int) or u > 3:
                                        pe.wait_ge(sums_copied, at(sums_copied, u - 3))
                                for g, t, q0, n, last in rounds[i]:
                                    kn = kts[t][1]
                                    first_block = at_block[t] + (q0 // P - t if causal is not None else q0 // P)
                                    ins = nc.tensor.matmul(ps[32 * g:32 * g + VW, SUMS + b, q0 % QW:q0 % QW + n], Vh[b][0:kn, t, :],
                                                           PT[b][0:kn, first_block:first_block + n // P, :].rearrange("p c q -> p (c q)"),
                                                           start=(i == 0), stop=last)
                                if i == len(rounds) - 1:
                                    ins.then_inc(sums_out, 1)

                            ops = [("f", i, (i + .5) / n1) for i in range(n1) if find]
                            ops += [("m", i, .5 + .5 * (i + .5) / n2 if causal is None else .3 + .7 * (i + .5) / n2) for i in range(n2) if make]
                            ops += [("t", 0, .45 if causal is None else .25)] if make else []
                            ops += [("a", i, (i + .6) / len(rounds)) for i in range(len(rounds)) if add]
                            for kind, i, _ in sorted(ops, key=lambda o: o[2]):
                                if kind == "f":
                                    maxima(i)
                                elif kind == "t":
                                    turn_maxima()
                                elif kind == "m":
                                    probabilities(i)
                                else:
                                    sums(i)

                        by_heads(pe.Fori, step)

                    @block.vector
                    def _(dve):
                        def step(h, par, turn, b, find, make, add, store):
                            u = 2 * h + b
                            if make:
                                if not isinstance(u, int) or u > 2:
                                    dve.wait_ge(sums_out, at(sums_out, u - 2))
                                ub = (b + 1) % 2
                                for dst, src in values(h - 1 if b == 0 else h, ub, Vh[ub]):
                                    ins = nc.vector.tensor_copy(dst, src)
                                ins.then_inc(values_in, 1)
                            if find:
                                for i, piece in enumerate(by_query):
                                    dve.wait_ge(by_query_out, at(by_query_out, u * n1 + i + 1))
                                    j0, jn, n = piece[0][0], len(piece), piece[0][2]
                                    half = piece[0][1] // 512
                                    nc.vector.tensor_reduce(part_max[:, half, j0:j0 + jn],
                                                            ps[:, BY_QUERY + (b * n1 + i) % 2, 0:jn * n].rearrange("p (j l) -> p j l", j=jn),
                                                            AX_X, ALU.max, negate=True).then_inc(max_found, 1)
                                dve.wait_ge(max_found, at(max_found, (u + 1) * n1))
                                m = (5 if causal is not None else 4) * u
                                if causal is not None:
                                    nc.vector.tensor_tensor(part_max[:, 0, 4:TPB], part_max[:, 0, 4:TPB], part_max[:, 1, 4:TPB], ALU.min).then_inc(max_step, 1)
                                    m = m + 1
                                    dve.wait_ge(max_step, at(max_step, m))
                                nc.vector.tensor_copy(N3[:, b, :, 0], part_max[:, 0, :]).then_inc(max_step, 1)
                                dve.wait_ge(max_step, at(max_step, m + 1))
                                nc.vector.tensor_tensor(rest[:, 0, :], part_max[:, 0, :], N3[:, b, :, 0], ALU.subtract).then_inc(max_step, 1)
                                dve.wait_ge(max_step, at(max_step, m + 2))
                                nc.vector.tensor_copy(N3[:, b, :, 1], rest[:, 0, :]).then_inc(max_step, 1)
                                dve.wait_ge(max_step, at(max_step, m + 3))
                                nc.vector.tensor_tensor(rest[:, 1, :], rest[:, 0, :], N3[:, b, :, 1], ALU.subtract).then_inc(max_step, 1)
                                dve.wait_ge(max_step, at(max_step, m + 4))
                                nc.vector.tensor_copy(N3[:, b, :, 2], rest[:, 1, :]).then_inc(split_ready, 1)
                        by_heads(dve.Fori, step)

                    @block.scalar
                    def _(act):
                        def step(h, par, turn, b, find, make, add, store):
                            u = 2 * h + b
                            ub, upar = (b + 1) % 2, (par + 1) % 2 if b == 0 else par
                            if store:
                                act.wait_ge(sums_out, at(sums_out, u - 2))
                                if not isinstance(u, int) or u > 4:
                                    act.wait_ge(result_stored[ub], at(result_stored[ub], 16 * (h - 2 if b == 0 else h - 1)))
                                nc.scalar.copy(SB[ub][:, :], ps[0:SR, SUMS + ub, 0:QW]).then_inc(sums_copied, 1)
                            if not make:
                                return
                            act.wait_ge(max_turned, at(max_turned, u))
                            nc.scalar.copy(QS[upar][0:3, ub * S:(ub + 1) * S],
                                           ps[0:3, MAXIMA:MAXIMA + 2, :].rearrange("p n q -> p (n q)")).then_inc(max_stacked, 1)
                            for i, (t, q0, n) in enumerate(by_key):
                                act.wait_ge(by_key_out, at(by_key_out, (u - 1) * n2 + i + 1))
                                kn = kts[t][1]
                                first_block = at_block[t] + (q0 // P - t if causal is not None else q0 // P)
                                if i == 0 and (not isinstance(u, int) or u > 2):
                                    act.wait_ge(sums_out, at(sums_out, u - 2))
                                nc.scalar.activation(PT[ub][0:kn, first_block:first_block + n // P, :].rearrange("p c q -> p (c q)"),
                                                     ps[0:kn, BY_KEY + (ub * n2 + i) % 2, 0:n], ACT.Exp).then_inc(exp_made, 1)

                        by_heads(act.Fori, step)
                    @block.gpsimd
                    def _(pool):
                        def step(h, par, turn, b, find, make, add, store):
                            u = 2 * h + b
                            if store and b == 0:
                                pool.wait_ge(by_key_out, at(by_key_out, (u - 2) * n2))
                                nc.gpsimd.tensor_tensor(QS[par][0:3, :], zeros, zeros, ALU.add).then_inc(stack_zero[par], 1)
                            if store:
                                ub = (b + 1) % 2
                                pool.wait_ge(sums_copied, at(sums_copied, u - 2))
                                v = h - 2 if b == 0 else h - 1
                                nc.gpsimd.dma_start(a["attended"][bass.ds((2 * v + ub) * P, SR), :], SB[ub][:, :]).then_inc(result_stored[ub], 16)

                        zeros = nought[:, :].broadcast_to([3, T])
                        for par in range(2):
                            pool.sem_inc(stack_zero[par], 1)
                        by_heads(pool.Fori, step)
                        for b in range(B):
                            pool.wait_ge(result_stored[b], at(result_stored[b], 16 * H))
                U = B * H
                advance((by_query_out, U * n1), (max_found, U * n1), (max_step, (5 if causal is not None else 4) * U), (split_ready, U), (max_turned, U), (max_stacked, U),
                        (by_key_out, U * n2), (exp_made, U * n2), (sums_out, U), (sums_copied, U), (values_in, U),
                        *((s, 16 * len(pairs) * 2 * H // 2) for s in stack_in), *((s, H // 2 + 1) for s in stack_zero), *((s, 16 * H) for s in result_stored))

        def project_out(wo, bo, gate, Z=None):
            with ExitStack() as own:
                def tmp(name, shape, dt=F32):
                    return own.enter_context(sbuf("o_" + name, shape, dt))
                AT = XT
                rc = tmp("rc", [P, QW])
                rest = tmp("rest", [P, 2, QW])
                addends = tmp("addends", [P, 3, QW], BF16)
                rh = tmp("rh", [3 * H, T], BF16)
                spread = tmp("spread", [3 * H, D], BF16)
                sums = a["attended"].rearrange("(h n r) c -> h r n c", h=H, r=32)
                recip = a["reciprocals"]
                with nc.Block() as block:
                    @block.sync
                    def _(sp):
                        sp.dma_start(rc[:, :], a["attended"].rearrange("(n r) c -> n r c", r=32)[:, HD, :]).then_inc(sums_loaded, 16)
                        sp.dma_start(spread[:, :], a["spread"]).then_inc(loaded, 16)
                        sp.wait_ge(recip_made, at(recip_made, 6))
                        sp.dma_start(recip.rearrange("(i h) (c w) -> (h c) i w", i=3, w=QW), addends[:, :, :]).then_inc(recip_stored, 16)
                        sp.wait_ge(recip_stored, at(recip_stored, 16))
                        sp.dma_start(rh[:, :], recip).then_inc(loaded, 16)

                    @block.scalar
                    def _(act):
                        act.wait_ge(sums_loaded, at(sums_loaded, 16))
                        for h in range(H):
                            act.dma_start(AT[h % 8 * HD:(h % 8 + 1) * HD, h // 8, :].rearrange("v (n c) -> v n c", n=8), sums[h, 0:HD, :, :]).then_inc(att_in[h // 8], 16)

                    @block.tensor
                    def _(pe):
                        pe.wait_ge(loaded, at(loaded, 32))
                        for n in range(8):
                            if n >= 4:
                                pe.wait_ge(divided, at(divided, n - 3))
                            nc.tensor.matmul(ps[:, 4 + n % 4, :], spread[:, n // 4 * P:(n // 4 + 1) * P], rh[:, n % 4 * 512:(n % 4 + 1) * 512],
                                             start=True, stop=True).then_inc(pe_out, 1)
                        for c in range(NT):
                            if c % 4 == 0:
                                pe.wait_ge(divided, at(divided, 4 + c // 4 + 1))
                            if c >= 4:
                                pe.wait_ge(x_used, at(x_used, c - 3))
                            for k in range(KD):
                                ins = nc.tensor.matmul(ps[:, c % 4, 0:D], AT[:, k, c * P:(c + 1) * P], wo[:, k, :], start=(k == 0), stop=(k == KD - 1 and bo is None))
                            if bo is not None:
                                ins = nc.tensor.matmul(ps[:, c % 4, 0:D], ones[0:1, 0:P], bo[0:1, :], start=False, stop=True)
                            ins.then_inc(y_out, 1)

                    @block.vector
                    def _(dve):
                        dve.wait_ge(sums_loaded, at(sums_loaded, 16))
                        nc.vector.reciprocal(rc[:, :], rc[:, :]).then_inc(recip_made, 1)
                        for i in range(3):
                            left = rc[:, :] if i == 0 else rest[:, i - 1, :]
                            dve.wait_ge(recip_made, at(recip_made, 2 * i + 1))
                            nc.vector.tensor_copy(addends[:, i, :], left).then_inc(recip_made, 1)
                            if i < 2:
                                dve.wait_ge(recip_made, at(recip_made, 2 * i + 2))
                                nc.vector.tensor_tensor(rest[:, i, :], left, addends[:, i, :], ALU.subtract).then_inc(recip_made, 1)
                        for n in range(8):
                            k, cols = n // 4, slice(n % 4 * 512, (n % 4 + 1) * 512)
                            if n % 4 == 0:
                                dve.wait_ge(att_in[k], at(att_in[k], 128))
                            dve.wait_ge(pe_out, at(pe_out, n + 1))
                            nc.vector.tensor_tensor(AT[:, k, cols], AT[:, k, cols], ps[:, 4 + n % 4, :], ALU.mult).then_inc(divided, 1)
                        for c in range(NT):
                            dve.wait_ge(y_out, at(y_out, c + 1))
                            y = ps[:, c % 4, 0:D]
                            if Z is not None:
                                nc.vector.tensor_tensor(Z[:, c, :], y, Z[:, c, :], ALU.add).then_inc(x_used, 1)
                            else:
                                nc.vector.scalar_tensor_tensor(X[:, c, :], y, gate, X[:, c, :], ALU.mult, ALU.add).then_inc(x_used, 1)
            advance((sums_loaded, 16), (recip_made, 6), (recip_stored, 16), (loaded, 32), (pe_out, 8), (divided, 8), (y_out, NT), (x_used, NT),
                    (att_in[0], 128), (att_in[1], 128))

        def block1():
            with ExitStack() as own:
                def tmp(name, shape, dt=F32):
                    return own.enter_context(sbuf(name, shape, dt))
                Z = XN
                gc = tmp("f1gc", [P, 2, KD])
                wr = tmp("wr1", [P, KD, E8])
                with ExitStack() as own2:
                    def tmp2(name, shape, dt=F32):
                        return own2.enter_context(sbuf(name, shape, dt))
                    scratch = tmp2("f1n", [P, NT, D])
                    grows = tmp2("f1g", [1, 2, D])
                    load_weights([(grows[:, 0, :], a["L1_ffn_g1"]), (grows[:, 1, :], a["L1_ffn_g2"]),
                                  (wr[:, :, :], a["L1_ffn_w_router"].rearrange("(k p) e -> p k e", p=P))])
                    with nc.Block() as block:
                        @block.tensor
                        def _(pe):
                            for i in range(2):
                                for k in range(KD):
                                    ins = nc.tensor.matmul(ps[:, 0, 2 * i + k:2 * i + k + 1], grows[:, i, k * P:(k + 1) * P], ones[0:1, 0:1],
                                                           start=True, stop=True)
                            ins.then_inc(pe_out, 1)

                        @block.scalar
                        def _(act):
                            act.wait_ge(pe_out, at(pe_out, 1))
                            nc.scalar.copy(gc[:, :, :], ps[:, 0, 0:4].rearrange("p (i k) -> p i k", i=2))
                    advance((pe_out, 1))
                    normalise(X, Z, True, 1e-5)
                    normalise(Z, scratch, False, 1e-6, gcol=gc[:, 0, :])
                self_attention(Z)
                weights, tables = load_experts(tmp, E8, 512, a["L1_ffn_w1"], a["L1_ffn_w2"])
                plan = Plan(tmp, E8, 2, CAPACITY1_TILES * E8, KD * 512, tables)
                rows = tmp("f1n2", [P, NT, D])
                normalise(Z, rows, False, 1e-6, gcol=gc[:, 1, :])
                route("best", E8, wr, tg[:, 5:6], plan, capacity=CAPACITY1)
                with nc.Block() as block:
                    @block.vector
                    def _(dve):
                        for c in range(NT):
                            nc.vector.scalar_tensor_tensor(X[:, c, :], Z[:, c, :], tg[:, 5:6], X[:, c, :], ALU.mult, ALU.add)
                experts(512, weights, ACT.Relu, plan, rows, gc[:, 1, :])

        def self_attention(Z):
            with ExitStack() as own:
                def tmp(name, shape, dt=F32):
                    return own.enter_context(sbuf("s_" + name, shape, dt))
                wo = tmp("wo", [P, KD, D])
                causal = tmp("causal", [P, P])
                causalb = tmp("causalb", [P, P], BF16)
                V = tmp("V", [P, NT, D])
                with ExitStack() as own2:
                    def tmp2(name, shape, dt=F32):
                        return own2.enter_context(sbuf("s_" + name, shape, dt))
                    w = tmp2("w", [P, KD, 3 * D])
                    wx = tmp2("wx", [P, KD, 2 * D])
                    cos = tmp2("cos", [P, S])
                    sin = tmp2("sin", [P, S])
                    load_weights([(w[:, :, :], a["L1_ffn_w_qkv"].rearrange("(k p) d -> p k d", p=P)),
                                  (wo[:, :, :], a["L1_ffn_w_o"].rearrange("(k p) d -> p k d", p=P)),
                                  (cos[:, :], a["cos2"]), (sin[:, :], a["sin2"]), (causal[:, :], a["causal"])])
                    with nc.Block() as block:
                        @block.vector
                        def _(dve):
                            swap_pairs(nc.vector, wx[:, :, :], w[:, :, 0:2 * D])
                            nc.vector.tensor_copy(causalb[:, :], causal[:, :])

                        @block.tensor
                        def _(pe):
                            for c in range(NT):
                                if c >= 4:
                                    pe.wait_ge(v_ready, at(v_ready, c - 3))
                                for k in range(KD):
                                    ins = nc.tensor.matmul(ps[:, 4 + c % 4, 0:D], XT[:, k, c * P:(c + 1) * P], w[:, k, 2 * D:3 * D],
                                                           start=(k == 0), stop=(k == KD - 1))
                                ins.then_inc(v_out, 1)

                        @block.scalar
                        def _(act):
                            for c in range(NT):
                                act.wait_ge(v_out, at(v_out, c + 1))
                                nc.scalar.copy(V[:, c, :], ps[:, 4 + c % 4, 0:D]).then_inc(v_ready, 1)
                    advance((v_out, NT), (v_ready, NT))
                    bf16_parts([(XT[:, :, t * 512:(t + 1) * 512], 512, ch, t * 512, (w[:, :, which * D:(which + 1) * D], None),
                                 (wx[:, :, which * D:(which + 1) * D], None), cos[:, (t % 2) * 512:(t % 2 + 1) * 512].unsqueeze(1),
                                 sin[:, (t % 2) * 512:(t % 2 + 1) * 512].unsqueeze(1), parts, scale)
                                for which, parts, scale in ((0, a["q_parts"], HD ** -0.5), (1, a["k_parts"], 1.0))
                                for ch in range(KD) for t in range(T // 512)])
                attention_by_heads("s_", S, causalb[:, :], lambda h, b, to: [(to[:, :, 0:HD], V[:, b * TPB:(b + 1) * TPB, bass.ds(h * HD, HD)])])
                project_out(wo, None, None, Z)

        def experts_layer2():
            with ExitStack() as own:
                def tmp(name, shape, dt=F32):
                    return own.enter_context(sbuf(name, shape, dt))
                wr = own.enter_context(sbuf("wr2", [P, KD, E8], F32))
                routers(wr, a["L2_ffn_router_w"])
                weights, tables = load_experts(tmp, E8, 1024, a["L2_ffn_w1"], a["L2_ffn_w2"])
                plan = Plan(tmp, E8, 2, SLOT_TILES, KD * 1024, tables)
                normalise(X, XN, True, 1e-5)
                route("top2", E8, wr, tg[:, 6:7], plan)
                experts(1024, weights, ACT.Gelu, plan, XN)

        def experts_layer3():
            E4, FF = 4, 1024
            with ExitStack() as own:
                def tmp(name, shape, dt=F32):
                    return own.enter_context(sbuf(name, shape, dt))
                wr = tmp("wr3", [P, KD, E4])
                bg = tmp("bg3", [1, E4])
                def prepare_experts():
                    nonlocal weights, tables
                    weights, tables = load_experts(tmp, E4, FF, a["L3_ffn_W1"], a["L3_ffn_W2"], a["L3_ffn_b1"], a["L3_ffn_b2"])
                    normalise(X, XN, True, 1e-5)

                weights = tables = None
                load_weights([(wr[:, :, :], a["L3_ffn_Wg"].rearrange("(k p) e -> p k e", p=P)), (bg[:, :], a["L3_ffn_bg"])], prepare_experts)
                plan = Plan(tmp, E4, 1, T // P + E4, KD * FF, tables)
                route("top1", E4, wr, tg[:, 7:8], plan, bias=bg)
                experts(FF, weights, ACT.Gelu, plan, XN)

        def alignment():
            NC = 16
            W = S // NC
            NSTEP = L + NC - 1
            NF = -(-NSTEP // 8) * 8
            LN = 32 * B
            down = [max(l - 1, 0) for l in range(32)]
            up = [min(l + 1, 31) for l in range(32)]
            cost_d, path_d = a["dtw_cost"], a["dtw_path"]
            with ExitStack() as own:
                def tmp(name, shape, dt=F32):
                    return own.enter_context(sbuf("t_" + name, shape, dt))
                CD = tmp("CD", [LN, NF, W])
                NL = tmp("NL", [LN, NF, W + 1])
                CC = tmp("CC", [LN, NF, W])
                R = tmp("R", [LN, 4, W + 1])
                M = tmp("M", [LN, 4, W])
                seed = tmp("seed", [LN, W])
                normalise(X, XN, True, 1e-5)
                SQ = XN[:, :, :].rearrange("p c d -> p (c d)").rearrange("p (k t) -> p k t", k=KD)
                with ExitStack() as own2:
                    def tmp2(name, shape, dt=F32):
                        return own2.enter_context(sbuf("t_" + name, shape, dt))
                    C2 = tmp2("C2", [P, KD, B, L])
                    DD = tmp2("DD", [P, 4, 512])
                    aa = tmp2("aa", [P, 2 * B])
                    with nc.Block() as block:
                        outs = [(b, r, n) for b in range(B) for r in range(2) for n in range(2)]

                        @block.scalar
                        def _(act):
                            for k in range(KD):
                                ins = nc.scalar.activation(SQ[:, k, :], XT[:, k, :], ACT.Square)
                            ins.then_inc(squares, 1)
                            for b in range(B):
                                nc.scalar.activation(DD[:, b, 0:D], CR[:, b, :], ACT.Square, accum_out=aa[:, b:b + 1])
                                ins = nc.scalar.activation(DD[0:TAIL, B + b, 0:D], CRT[:, b, :], ACT.Square, accum_out=aa[0:TAIL, B + b:B + b + 1])
                            ins.then_inc(norms, 1)
                            for m, (b, r, n) in enumerate(outs):
                                rows = TAIL if r else P
                                act.wait_ge(dist2, at(dist2, m + 1))
                                nc.scalar.activation(DD[0:rows, m % 4, :], DD[0:rows, m % 4, :], ACT.Sqrt).then_inc(dist, 1)

                        @block.tensor
                        def _(pe):
                            pe.wait_ge(squares, at(squares, 1))
                            pe.wait_ge(cst, at(cst, 1))
                            for m, (b, r, n) in enumerate(outs):
                                rows, lo, hi = (TAIL, P, L) if r else (P, 0, P)
                                for k in range(KD):
                                    cols = slice(b * S + n * 512, b * S + (n + 1) * 512)
                                    nc.tensor.matmul(ps[0:rows, m, :], C2[:, k, b, lo:hi], XT[:, k, cols], start=(k == 0), stop=False)
                                    ins = nc.tensor.matmul(ps[0:rows, m, :], ones[:, 0:rows], SQ[:, k, cols], start=False, stop=(k == KD - 1))
                                ins.then_inc(pe_out, 1)

                        @block.vector
                        def _(dve):
                            nc.vector.tensor_scalar(C2[:, :, :, :], CT[:, :, :, :], -2.0, None, ALU.mult).then_inc(cst, 1)
                            nc.vector.memset(CD[:, :, :], 0.0).then_inc(cleared, 1)
                            nc.vector.memset(NL[:, :, 0:1], 0.0)
                            dve.wait_ge(norms, at(norms, 1))
                            for m, (b, r, n) in enumerate(outs):
                                rows = TAIL if r else P
                                dve.wait_ge(pe_out, at(pe_out, m + 1))
                                if m >= 4:
                                    dve.wait_ge(dist_stored, at(dist_stored, 16 * (m - 3)))
                                nc.vector.tensor_scalar(DD[0:rows, m % 4, :], ps[0:rows, m, :], aa[0:rows, r * B + b:r * B + b + 1], 0.0,
                                                            ALU.add, ALU.max).then_inc(dist2, 1)

                        @block.sync
                        def _(sp):
                            for m, (b, r, n) in enumerate(outs):
                                rows, lo, hi = (TAIL, P, L) if r else (P, 0, P)
                                sp.wait_ge(dist, at(dist, m + 1))
                                sp.dma_start(cost_d[b * L + lo:b * L + hi, n * 512:(n + 1) * 512], DD[0:rows, m % 4, :]).then_inc(dist_stored, 16)
                                sp.wait_ge(dist_stored, at(dist_stored, 16 * (m + 1)))
                            sp.wait_ge(cleared, at(cleared, 1))
                            for b in range(B):
                                for k in range(NC):
                                    lane = 32 * b + 1 + k
                                    sp.dma_start(CD[lane:lane + 1, k:k + L, :],
                                                     cost_d[b * L:(b + 1) * L, k * W:(k + 1) * W].rearrange("(o i) w -> o i w", o=1)).then_inc(skewed, 16)
                            sp.dma_start(R[:, 3, :], a["dtw_start"]).then_inc(skewed, 16)
                            sp.dma_start(seed[:, :], a["dtw_end"]).then_inc(skewed, 16)
                            sp.wait_ge(skewed, at(skewed, 16 * (B * NC + 2)))
                    advance((squares, 1), (norms, 1), (dist2, 8), (dist, 8), (pe_out, 8), (cst, 1), (cleared, 1), (dist_stored, 16 * 8), (skewed, 16 * (B * NC + 2)))

                Z = tmp("Z", [LN, 4, 2, W + 1])
                with nc.Block() as block:
                    @block.vector
                    def _(dve):
                        dve.sem_inc(row_free, 3)
                        step = Steps()
                        with dve.Fori(0, NF // 8) as t:
                            step.turn(t, 8)
                            for q8 in range(8):
                                q, prev = q8 % 4, (q8 + 3) % 4
                                dve.wait_ge(row_free, at(row_free, t * 8 + q8 + 1))
                                nc.vector.tensor_tensor(M[:, q, :], R[:, prev, 0:W], R[:, prev, 1:W + 1], ALU.min)
                                nc.vector.stream_shuffle(R[:, q, 0:1], R[:, prev, W:W + 1], down).then_inc(dve_step, 1)
                                dve.wait_ge(dve_step, at(dve_step, step.next()))
                                nc.vector.tensor_tensor_scan(R[:, q, 1:W + 1], M[:, q, :],
                                                                 CD[:, bass.ds(t * 8 + q8, 1), :].rearrange("p s w -> p (s w)"),
                                                                 R[:, q, 0:1], ALU.min, ALU.add).then_inc(row_made, 1)
                                dve.wait_ge(row_made, at(row_made, t * 8 + q8 + 1))
                        step.end(NF // 8)
                        dve.wait_ge(row_free, at(row_free, 3 + NF))
                        nc.vector.tensor_scalar(NL[:, :, 1:W + 1], NL[:, :, 1:W + 1], 0.0, None, ALU.is_ge)
                        nc.vector.tensor_scalar(CC[:, :, :], CC[:, :, :], 0.0, 2.0, ALU.is_gt, ALU.mult).then_inc(dve_step, 1)
                        dve.wait_ge(dve_step, at(dve_step, step.next()))
                        nc.vector.scalar_tensor_tensor(CC[:, :, :], CC[:, :, :], -1.0, NL[:, :, 1:W + 1], ALU.add, ALU.mult).then_inc(dve_step, 1)
                        dve.wait_ge(dve_step, at(dve_step, step.next()))
                        nc.vector.stream_shuffle(NL[:, 0:NF - 1, 0], NL[:, 1:NF, W], up)
                        nc.vector.memset(Z[:, :, :, :], 0.0).then_inc(dve_step, 1)
                        dve.wait_ge(dve_step, at(dve_step, step.next()))
                        dve.sem_inc(membership_kept, 4)

                        def back(m, s, slot):
                            nl = NL[:, bass.ds(s, 1), :].rearrange("p s w -> p (s w)")
                            c = CC[:, bass.ds(s, 1), :].rearrange("p s w -> p (s w)")
                            dve.wait_ge(membership_kept, at(membership_kept, m + 1))
                            nc.vector.tensor_tensor_scan(Z[:, slot, 0, 1:W + 1], nl[:, 0:W], seed[:, :], Z[:, slot, 0, 0:1],
                                                         ALU.is_lt, ALU.max).then_inc(member, 1)
                            dve.wait_ge(member, at(member, m + 1))
                            nc.vector.tensor_tensor(Z[:, slot, 1, 1:W + 1], Z[:, slot, 0, 1:W + 1], c, ALU.mult).then_inc(dve_step, 1)
                            dve.wait_ge(dve_step, at(dve_step, step.next()))
                            nc.vector.scalar_tensor_tensor(seed[:, :], Z[:, slot, 1, 0:W], -1.0, Z[:, slot, 1, 1:W + 1], ALU.mult, ALU.max)
                            nc.vector.stream_shuffle(Z[:, (slot + 1) % 4, :, 0], Z[:, slot, :, W], up).then_inc(dve_step, 1)
                            dve.wait_ge(dve_step, at(dve_step, step.next()))

                        back(0, NSTEP - 1, 0)
                        n = (NSTEP - 1) // 8
                        assert n * 8 == NSTEP - 1
                        with dve.Fori(0, n) as t:
                            step.turn(t, 16)
                            for q in range(8):
                                back(8 * t + q + 1, t * -8 + (8 * n - 1 - q), (q + 1) % 4)
                        step.end(n)
                        advance((dve_step, step.total))

                    @block.gpsimd
                    def _(pool):
                        with pool.Fori(0, NF // 8) as t:
                            for q8 in range(8):
                                q, prev = q8 % 4, (q8 + 3) % 4
                                pool.wait_ge(row_made, at(row_made, t * 8 + q8 + 1))
                                nc.gpsimd.tensor_tensor(NL[:, bass.ds(t * 8 + q8, 1), 1:W + 1].rearrange("p s w -> p (s w)"),
                                                        R[:, q, 0:W][:, ::-1], M[:, q, :][:, ::-1], ALU.subtract)
                                nc.gpsimd.tensor_tensor(CC[:, bass.ds(t * 8 + q8, 1), :].rearrange("p s w -> p (s w)"),
                                                            R[:, prev, 0:W][:, ::-1], R[:, prev, 1:W + 1][:, ::-1], ALU.subtract).then_inc(row_free, 1)

                        def keep(m, s, slot):
                            pool.wait_ge(member, at(member, m + 1))
                            nc.gpsimd.tensor_copy(CD[:, bass.ds(s, 1), :].rearrange("p s w -> p (s w)"), Z[:, slot, 0, 1:W + 1]).then_inc(membership_kept, 1)

                        keep(0, NSTEP - 1, 0)
                        n = (NSTEP - 1) // 8
                        with pool.Fori(0, n) as t:
                            for q in range(8):
                                keep(8 * t + q + 1, t * -8 + (8 * n - 1 - q), (q + 1) % 4)
                advance((member, NSTEP), (membership_kept, NSTEP + 4))
                advance((row_free, 3 + NF), (row_made, NF))

                RAWT = XN[0:TAIL, 0:8, :].rearrange("p c d -> p (c d)")
                TAILP = XN[0:TAIL, 8:16, :].rearrange("p c d -> p (c d)")
                with nc.Block() as block:
                    @block.sync
                    def _(sp):
                        for b in range(B):
                            for k in range(NC):
                                lane = 32 * b + 1 + k
                                sp.dma_start(path_d[b * L:(b + 1) * L, k * W:(k + 1) * W].rearrange("(o i) w -> o i w", o=1),
                                                 CD[lane:lane + 1, k:k + L, :]).then_inc(path_stored, 16)
                        sp.wait_ge(path_stored, at(path_stored, 16 * B * NC))
                        src = path_d.rearrange("(b i) t -> i b t", b=B)
                        sp.dma_start(XT[:, 0, :].rearrange("p (b t) -> p b t", b=B), src[0:P]).then_inc(loaded, 16)
                        sp.dma_start(RAWT.rearrange("p (b t) -> p b t", b=B), src[P:L]).then_inc(loaded, 16)

                    @block.tensor
                    def _(pe):
                        pe.wait_ge(turned, at(turned, 2))
                        for c in range(NT):
                            b = c // TPB
                            if c >= 8:
                                pe.wait_ge(x_used, at(x_used, c - 7))
                            nc.tensor.matmul(ps[:, c % 8, 0:D], XT[:, 1, c * P:(c + 1) * P], CR[:, b, :], start=True, stop=False)
                            nc.tensor.matmul(ps[:, c % 8, 0:D], TAILP[:, c * P:(c + 1) * P], CRT[:, b, :], start=False, stop=True).then_inc(pe_out, 1)

                    @block.vector
                    def _(dve):
                        dve.wait_ge(loaded, at(loaded, 32))
                        for to, raw in ((XT[:, 1, :], XT[:, 0, :]), (TAILP, RAWT)):
                            nc.vector.tensor_copy(to.rearrange("p (k w) -> p k w", w=W),
                                                      raw.rearrange("p (k w) -> p k w", w=W)[:, :, ::-1]).then_inc(turned, 1)
                        for c in range(NT):
                            dve.wait_ge(pe_out, at(pe_out, c + 1))
                            nc.vector.scalar_tensor_tensor(X[:, c, :], ps[:, c % 8, 0:D], tg[:, 2:3], X[:, c, :], ALU.mult, ALU.add).then_inc(x_used, 1)
                advance((path_stored, 16 * B * NC), (loaded, 32), (pe_out, NT), (x_used, NT), (turned, 2))

        def store():
            with nc.Block() as block:
                @block.sync
                def _(sp):
                    sp.dma_start(out.rearrange("(t p) d -> p t d", p=P), X[:, :, :]).then_inc(stored, 16)
                    sp.wait_ge(stored, at(stored, 16))

        prepare()
        for layer in (attention0, experts_layer0, attention1, block1, alignment, experts_layer2, attention3, experts_layer3):
            layer()
        store()


_INPUTS = ['g_xattn', 'g_ffn', 'L0_xattn_Wq', 'L0_xattn_Wk', 'L0_xattn_Wv', 'L0_xattn_Wo', 'L0_ffn_router_w', 'L0_ffn_w1', 'L0_ffn_w2', 'L1_xattn_Wq', 'L1_xattn_bq', 'L1_xattn_Wkv', 'L1_xattn_bkv', 'L1_xattn_Wo', 'L1_xattn_bo',
           'L3_xattn_Wq', 'L3_xattn_bq', 'L3_xattn_Wk', 'L3_xattn_bk', 'L3_xattn_Wv', 'L3_xattn_bv', 'L3_xattn_Wo', 'L3_xattn_bo',
           'L1_ffn_g1', 'L1_ffn_w_qkv', 'L1_ffn_w_o', 'L1_ffn_g2', 'L1_ffn_w_router', 'L1_ffn_w1', 'L1_ffn_w2', 'L2_ffn_router_w', 'L2_ffn_w1', 'L2_ffn_w2',
           'L3_ffn_W1', 'L3_ffn_b1', 'L3_ffn_W2', 'L3_ffn_b2', 'L3_ffn_Wg', 'L3_ffn_bg']


def kernel(**inputs):
    import concourse.bacc as _bacc
    from concourse.bass_utils import run_bass_kernel_spmd as _run

    nc = _bacc.Bacc("TRN2", target_bir_lowering=False, num_devices=1)
    arrays = {}
    arrays["x"] = np.ascontiguousarray(inputs["x"]).reshape(T, D)
    arrays["ctx"] = np.ascontiguousarray(inputs["ctx_1024"]).reshape(B * L, D)
    arrays["ctx_mask"] = np.ascontiguousarray(inputs["mask_BxS2_bf1"]).reshape(1, B * L)
    arrays["q_mask"] = np.ascontiguousarray(inputs["mask_Bx1xSxS2_bk1"]).reshape(T, L)
    for name in _INPUTS:
        v = np.ascontiguousarray(inputs[name])
        arrays[name] = v.reshape(1, -1) if v.ndim == 1 else v
    arrays.update(shape_constants())
    aps = {k: nc.dram_tensor(f"in_{k}_dram", v.shape, mybir.dt.uint8 if v.dtype == np.bool_ else mybir.dt.from_np(v.dtype), kind="ExternalInput").ap() for k, v in arrays.items()}
    aps["expert_rows"] = nc.dram_tensor("expert_rows", (SLOT_TILES * P + 2 * T, D), F32).ap()
    aps["expert_results"] = nc.dram_tensor("expert_results", (SLOT_TILES * P, D), F32).ap()
    aps["reciprocals"] = nc.dram_tensor("reciprocals", (3 * H, T), BF16).ap()
    aps["attended"] = nc.dram_tensor("attended", (H * B * P, QW), F32).ap()
    for name, n in (("q_parts", T), ("k_parts", T), ("ck_parts", B * L)):
        aps[name] = nc.dram_tensor(name, (3 * D, n), BF16).ap()
    for name in ("dtw_cost", "dtw_path"):
        aps[name] = nc.dram_tensor(name, (B * L, S), F32).ap()
    out = nc.dram_tensor("out_0_dram", (T, D), F32, kind="ExternalOutput").ap()
    build(nc, aps, out)
    r = _run(nc, [{f"in_{k}_dram": v for k, v in arrays.items()}], core_ids=[0])
    return np.asarray(r.results[0]["out_0_dram"]).reshape(B, S, D)
```
